# Optimizing a Trainium2 kernel written in Bass

```python
import numpy as np
import jax
import jax.numpy as jnp

def _softmax(x, axis=-1):
    return jax.nn.softmax(x, axis=axis)

def _gelu(x):
    return jax.nn.gelu(x, approximate=True)

def _silu(x):
    return jax.nn.silu(x)

def _sigmoid(x):
    return jax.nn.sigmoid(x)

def _layernorm(x, axis=-1, eps=1e-05):
    m = jnp.mean(x, axis=axis, keepdims=True)
    v = jnp.var(x, axis=axis, keepdims=True)
    return (x - m) / jnp.sqrt(v + eps)

def _scatter_add(tgt, idx, src, axis=0):
    return tgt.at[idx].add(src)

def _segment_sum(src, seg, n):
    return jax.ops.segment_sum(src, seg, n)
kernel_name = 'mk_decoder_preln_d1_seqx_r4_067e12'

def setup_inputs(seed: int=0):
    np.random.seed(seed)
    _w = jnp.asarray

    def _rec_inputs():
        import jax
        import jax.numpy as jnp
        _rk = jax.random.key(seed)
        x = 7.22e-05 + 1 * jax.random.normal(jax.random.fold_in(_rk, 1), (1, 2048, 256), jnp.float32)
        _lenS = 2048 - jax.random.randint(jax.random.fold_in(_rk, 7), (1,), 0, max(1, 2048 // 4) + 1, jnp.int32)
        _lenS2 = 1601 - jax.random.randint(jax.random.fold_in(_rk, 8), (1,), 0, max(1, 1601 // 4) + 1, jnp.int32)
        _ctx_768P = jax.random.normal(jax.random.fold_in(_rk, 11), (1, 16, 192), jnp.float32)
        _ctx_768c = jax.random.dirichlet(jax.random.fold_in(_rk, 511), 0.3 * jnp.ones((16,), jnp.float32), (1, 1601))
        _ctx_768t = jnp.einsum('bsk,bkd->bsd', _ctx_768c, _ctx_768P)
        _ctx_768t = _ctx_768t * jax.lax.rsqrt(jnp.mean(jnp.square(_ctx_768t)) + 1e-12) * 0.953939
        ctx_768 = -0.000191848 + 0.999787 * (_ctx_768t + 0.3 * jax.random.normal(jax.random.fold_in(_rk, 611), (1, 1601, 192), jnp.float32))
        return (x, ctx_768)
    x, ctx_768 = _rec_inputs()

    def _L0_attn_setup():
        import jax, jax.numpy as jnp
        import numpy as np
        D_MODEL = 256
        D_STATE = 16
        D_CONV = 4
        EXPAND = 2
        D_INNER = EXPAND * D_MODEL
        DT_RANK = (D_MODEL + 15) // 16
        B_SZ = 4
        SEQ = 512
        EPS = 1e-12

        def rmsnorm(x, w, eps=EPS):
            return x * jax.lax.rsqrt(jnp.mean(x * x, axis=-1, keepdims=True) + eps) * w

        def causal_dwconv(x, w, b):
            xc = jnp.swapaxes(x, 1, 2)
            out = jax.lax.conv_general_dilated(xc, w[:, None, :], window_strides=(1,), padding=[(w.shape[1] - 1, 0)], dimension_numbers=('NCH', 'OIH', 'NCH'), feature_group_count=w.shape[0])
            return jnp.swapaxes(out, 1, 2) + b

        def selective_scan(u, delta, A, Bm, Cm):

            def step(h, inp):
                d_t, u_t, b_t, c_t = inp
                dA = jnp.exp(d_t[..., None] * A)
                h = dA * h + (d_t * u_t)[..., None] * b_t[:, None, :]
                y = jnp.einsum('bdn,bn->bd', h, c_t)
                return (h, y)
            h0 = jnp.zeros((u.shape[0], u.shape[2], A.shape[1]), u.dtype)
            xs = (jnp.swapaxes(delta, 0, 1), jnp.swapaxes(u, 0, 1), jnp.swapaxes(Bm, 0, 1), jnp.swapaxes(Cm, 0, 1))
            _, ys = jax.lax.scan(step, h0, xs)
            return jnp.swapaxes(ys, 0, 1)

        def mamba_block(x, in_proj_w, conv_w, conv_b, x_proj_w, dt_proj_w, dt_proj_b, A_log, D, out_proj_w):
            xz = x @ in_proj_w.T
            u, z = jnp.split(xz, 2, axis=-1)
            u = jax.nn.silu(causal_dwconv(u, conv_w, conv_b))
            x_dbl = u @ x_proj_w.T
            dt = x_dbl[..., :DT_RANK]
            Bm = x_dbl[..., DT_RANK:DT_RANK + D_STATE]
            Cm = x_dbl[..., DT_RANK + D_STATE:]
            delta = jax.nn.softplus(dt @ dt_proj_w.T + dt_proj_b)
            A = -jnp.exp(A_log)
            y = selective_scan(u, delta, A, Bm, Cm) + u * D
            y = y * jax.nn.silu(z)
            return y @ out_proj_w.T
        key = jax.random.key(seed)
        ks = jax.random.split(key, 12)
        s = 0.02
        n = lambda k, sh: jax.random.normal(k, sh, jnp.float32) * s
        A_log = jnp.log(jnp.broadcast_to(jnp.arange(1, D_STATE + 1, dtype=jnp.float32), (D_INNER, D_STATE)))
        return {'input_tensor': jax.random.normal(ks[0], (B_SZ, SEQ, D_MODEL), jnp.float32), 'in_proj_w': n(ks[1], (2 * D_INNER, D_MODEL)), 'conv_w': n(ks[2], (D_INNER, D_CONV)), 'conv_b': n(ks[3], (D_INNER,)), 'x_proj_w': n(ks[4], (DT_RANK + 2 * D_STATE, D_INNER)), 'dt_proj_w': n(ks[5], (D_INNER, DT_RANK)), 'dt_proj_b': jax.random.uniform(ks[6], (D_INNER,), jnp.float32, -4.0, -2.0), 'A_log': A_log, 'D': jnp.ones((D_INNER,), jnp.float32), 'out_proj_w': n(ks[7], (D_MODEL, D_INNER)), 'norm_w': jnp.ones((D_MODEL,), jnp.float32), 'ffn_w1': n(ks[8], (4 * D_MODEL, D_MODEL)), 'ffn_b1': jnp.zeros((4 * D_MODEL,), jnp.float32), 'ffn_w2': n(ks[9], (D_MODEL, 4 * D_MODEL)), 'ffn_b2': jnp.zeros((D_MODEL,), jnp.float32), 'ffn_norm_w': jnp.ones((D_MODEL,), jnp.float32)}
    _L0_attn_all = _L0_attn_setup()
    _L0_attn_in = {k: v for k, v in _L0_attn_all.items() if k in ('in_proj_w', 'conv_w', 'conv_b', 'x_proj_w', 'dt_proj_w', 'dt_proj_b', 'A_log', 'D', 'out_proj_w', 'norm_w', 'ffn_w1', 'ffn_b1', 'ffn_w2', 'ffn_b2', 'ffn_norm_w')}
    del _L0_attn_all

    def _L0_xattn_setup():
        import math
        import jax, jax.numpy as jnp
        import numpy as np
        B, SQ, SKV = (4, 512, 512)
        D_EMBED, D_CROSS, D_ATT, N_HEADS = (256, 192, 256, 16)
        D_HEAD = D_ATT // N_HEADS

        def _split_heads(t):
            b, s, _ = t.shape
            return t.reshape(b, s, N_HEADS, D_HEAD).transpose(0, 2, 1, 3)
        key = jax.random.key(seed)
        ks = jax.random.split(key, 10)
        s_e = 1.0 / math.sqrt(D_EMBED)
        s_c = 1.0 / math.sqrt(D_CROSS)
        s_a = 1.0 / math.sqrt(D_ATT)
        return {'x': jax.random.normal(ks[0], (B, SQ, D_EMBED), jnp.float32), 'y': jax.random.normal(ks[1], (B, SKV, D_CROSS), jnp.float32), 'Wq': jax.random.normal(ks[2], (D_EMBED, D_ATT), jnp.float32) * s_e, 'bq': jax.random.normal(ks[3], (D_ATT,), jnp.float32) * 0.01, 'Wk': jax.random.normal(ks[4], (D_CROSS, D_ATT), jnp.float32) * s_c, 'bk': jax.random.normal(ks[5], (D_ATT,), jnp.float32) * 0.01, 'Wv': jax.random.normal(ks[6], (D_CROSS, D_ATT), jnp.float32) * s_c, 'bv': jax.random.normal(ks[7], (D_ATT,), jnp.float32) * 0.01, 'Wo': jax.random.normal(ks[8], (D_ATT, D_EMBED), jnp.float32) * s_a, 'bo': jax.random.normal(ks[9], (D_EMBED,), jnp.float32) * 0.01}
    _L0_xattn_all = _L0_xattn_setup()
    _L0_xattn_in = {k: v for k, v in _L0_xattn_all.items() if k in ('Wq', 'bq', 'Wk', 'bk', 'Wv', 'bv', 'Wo', 'bo')}
    del _L0_xattn_all

    def _L0_ffn_setup():
        import jax, jax.numpy as jnp
        import numpy as np
        B, SEQ, DIM = (2, 1024, 256)
        E, S = (8, 128)
        HID = 4 * DIM
        SCALE = DIM ** 0.5

        def rmsnorm(x, gamma):
            n = jnp.linalg.norm(x, axis=-1, keepdims=True)
            return x / jnp.maximum(n, 1e-12) * SCALE * gamma
        key = jax.random.key(seed)
        ks = jax.random.split(key, 4)
        w_init = lambda k, shape: jax.random.normal(k, shape, dtype=jnp.float32) * 0.02
        return {'x': jax.random.normal(ks[0], (B, SEQ, DIM), dtype=jnp.float32), 'norm_gamma': jnp.ones((DIM,), jnp.float32), 'slot_norm_gamma': jnp.ones((DIM,), jnp.float32), 'slot_embeds': jax.random.normal(ks[1], (E, S, DIM), dtype=jnp.float32), 'w1': w_init(ks[2], (E, DIM, HID)), 'b1': jnp.zeros((E, HID), jnp.float32), 'w2': w_init(ks[3], (E, HID, DIM)), 'b2': jnp.zeros((E, DIM), jnp.float32)}
    _L0_ffn_all = _L0_ffn_setup()
    _L0_ffn_in = {k: v for k, v in _L0_ffn_all.items() if k in ('norm_gamma', 'slot_norm_gamma', 'slot_embeds', 'w1', 'b1', 'w2', 'b2')}
    del _L0_ffn_all
    return {'x': x, 'ctx_768': ctx_768, 'L0_attn_in_proj_w': _L0_attn_in['in_proj_w'], 'L0_attn_conv_w': _L0_attn_in['conv_w'], 'L0_attn_conv_b': _L0_attn_in['conv_b'], 'L0_attn_x_proj_w': _L0_attn_in['x_proj_w'], 'L0_attn_dt_proj_w': _L0_attn_in['dt_proj_w'], 'L0_attn_dt_proj_b': _L0_attn_in['dt_proj_b'], 'L0_attn_A_log': _L0_attn_in['A_log'], 'L0_attn_D': _L0_attn_in['D'], 'L0_attn_out_proj_w': _L0_attn_in['out_proj_w'], 'L0_attn_norm_w': _L0_attn_in['norm_w'], 'L0_attn_ffn_w1': _L0_attn_in['ffn_w1'], 'L0_attn_ffn_b1': _L0_attn_in['ffn_b1'], 'L0_attn_ffn_w2': _L0_attn_in['ffn_w2'], 'L0_attn_ffn_b2': _L0_attn_in['ffn_b2'], 'L0_attn_ffn_norm_w': _L0_attn_in['ffn_norm_w'], 'L0_xattn_Wq': _L0_xattn_in['Wq'], 'L0_xattn_bq': _L0_xattn_in['bq'], 'L0_xattn_Wk': _L0_xattn_in['Wk'], 'L0_xattn_bk': _L0_xattn_in['bk'], 'L0_xattn_Wv': _L0_xattn_in['Wv'], 'L0_xattn_bv': _L0_xattn_in['bv'], 'L0_xattn_Wo': _L0_xattn_in['Wo'], 'L0_xattn_bo': _L0_xattn_in['bo'], 'L0_ffn_norm_gamma': _L0_ffn_in['norm_gamma'], 'L0_ffn_slot_norm_gamma': _L0_ffn_in['slot_norm_gamma'], 'L0_ffn_slot_embeds': _L0_ffn_in['slot_embeds'], 'L0_ffn_w1': _L0_ffn_in['w1'], 'L0_ffn_b1': _L0_ffn_in['b1'], 'L0_ffn_w2': _L0_ffn_in['w2'], 'L0_ffn_b2': _L0_ffn_in['b2']}

def reference(x, ctx_768, L0_attn_in_proj_w, L0_attn_conv_w, L0_attn_conv_b, L0_attn_x_proj_w, L0_attn_dt_proj_w, L0_attn_dt_proj_b, L0_attn_A_log, L0_attn_D, L0_attn_out_proj_w, L0_attn_norm_w, L0_attn_ffn_w1, L0_attn_ffn_b1, L0_attn_ffn_w2, L0_attn_ffn_b2, L0_attn_ffn_norm_w, L0_xattn_Wq, L0_xattn_bq, L0_xattn_Wk, L0_xattn_bk, L0_xattn_Wv, L0_xattn_bv, L0_xattn_Wo, L0_xattn_bo, L0_ffn_norm_gamma, L0_ffn_slot_norm_gamma, L0_ffn_slot_embeds, L0_ffn_w1, L0_ffn_b1, L0_ffn_w2, L0_ffn_b2):
    import jax
    import jax.numpy as jnp

    def _L0_attn_ref(input_tensor, in_proj_w, conv_w, conv_b, x_proj_w, dt_proj_w, dt_proj_b, A_log, D, out_proj_w, norm_w, ffn_w1, ffn_b1, ffn_w2, ffn_b2, ffn_norm_w):
        import jax, jax.numpy as jnp
        import numpy as np
        D_MODEL = 256
        D_STATE = 16
        D_CONV = 4
        EXPAND = 2
        D_INNER = EXPAND * D_MODEL
        DT_RANK = (D_MODEL + 15) // 16
        B_SZ = 4
        SEQ = 512
        EPS = 1e-12

        def rmsnorm(x, w, eps=EPS):
            return x * jax.lax.rsqrt(jnp.mean(x * x, axis=-1, keepdims=True) + eps) * w

        def causal_dwconv(x, w, b):
            xc = jnp.swapaxes(x, 1, 2)
            out = jax.lax.conv_general_dilated(xc, w[:, None, :], window_strides=(1,), padding=[(w.shape[1] - 1, 0)], dimension_numbers=('NCH', 'OIH', 'NCH'), feature_group_count=w.shape[0])
            return jnp.swapaxes(out, 1, 2) + b

        def selective_scan(u, delta, A, Bm, Cm):

            def step(h, inp):
                d_t, u_t, b_t, c_t = inp
                dA = jnp.exp(d_t[..., None] * A)
                h = dA * h + (d_t * u_t)[..., None] * b_t[:, None, :]
                y = jnp.einsum('bdn,bn->bd', h, c_t)
                return (h, y)
            h0 = jnp.zeros((u.shape[0], u.shape[2], A.shape[1]), u.dtype)
            xs = (jnp.swapaxes(delta, 0, 1), jnp.swapaxes(u, 0, 1), jnp.swapaxes(Bm, 0, 1), jnp.swapaxes(Cm, 0, 1))
            _, ys = jax.lax.scan(step, h0, xs)
            return jnp.swapaxes(ys, 0, 1)

        def mamba_block(x, in_proj_w, conv_w, conv_b, x_proj_w, dt_proj_w, dt_proj_b, A_log, D, out_proj_w):
            xz = x @ in_proj_w.T
            u, z = jnp.split(xz, 2, axis=-1)
            u = jax.nn.silu(causal_dwconv(u, conv_w, conv_b))
            x_dbl = u @ x_proj_w.T
            dt = x_dbl[..., :DT_RANK]
            Bm = x_dbl[..., DT_RANK:DT_RANK + D_STATE]
            Cm = x_dbl[..., DT_RANK + D_STATE:]
            delta = jax.nn.softplus(dt @ dt_proj_w.T + dt_proj_b)
            A = -jnp.exp(A_log)
            y = selective_scan(u, delta, A, Bm, Cm) + u * D
            y = y * jax.nn.silu(z)
            return y @ out_proj_w.T
        h = mamba_block(input_tensor, in_proj_w, conv_w, conv_b, x_proj_w, dt_proj_w, dt_proj_b, A_log, D, out_proj_w)
        h = rmsnorm(h + input_tensor, norm_w)
        ff = jax.nn.gelu(h @ ffn_w1.T + ffn_b1, approximate=False) @ ffn_w2.T + ffn_b2
        return rmsnorm(ff + h, ffn_norm_w)

    def _L0_xattn_ref(x, y, Wq, bq, Wk, bk, Wv, bv, Wo, bo):
        import math
        import jax, jax.numpy as jnp
        import numpy as np
        B, SQ, SKV = (4, 512, 512)
        D_EMBED, D_CROSS, D_ATT, N_HEADS = (256, 192, 256, 16)
        D_HEAD = D_ATT // N_HEADS

        def _split_heads(t):
            b, s, _ = t.shape
            return t.reshape(b, s, N_HEADS, D_HEAD).transpose(0, 2, 1, 3)
        q = _split_heads(x @ Wq + bq)
        k = _split_heads(y @ Wk + bk)
        v = _split_heads(y @ Wv + bv)
        scale = 1.0 / math.sqrt(D_HEAD)
        scores = jnp.einsum('bhqd,bhkd->bhqk', q, k) * scale
        weights = jax.nn.softmax(scores, axis=-1)
        out = jnp.einsum('bhqk,bhkd->bhqd', weights, v)
        out = out.transpose(0, 2, 1, 3).reshape(x.shape[0], x.shape[1], D_ATT)
        return out @ Wo + bo

    def _L0_ffn_ref(x, norm_gamma, slot_norm_gamma, slot_embeds, w1, b1, w2, b2):
        import jax, jax.numpy as jnp
        import numpy as np
        B, SEQ, DIM = (2, 1024, 256)
        E, S = (8, 128)
        HID = 4 * DIM
        SCALE = DIM ** 0.5

        def rmsnorm(x, gamma):
            n = jnp.linalg.norm(x, axis=-1, keepdims=True)
            return x / jnp.maximum(n, 1e-12) * SCALE * gamma
        xn = rmsnorm(x, norm_gamma)
        sn = rmsnorm(slot_embeds, slot_norm_gamma)
        logits = jnp.einsum('bnd,esd->bnes', xn, sn)
        dispatch = jax.nn.softmax(logits, axis=1)
        b, n, e, s = logits.shape
        combine = jax.nn.softmax(logits.reshape(b, n, e * s), axis=-1)
        slots = jnp.einsum('bnd,bnes->besd', xn, dispatch)
        h = jnp.einsum('besd,edh->besh', slots, w1) + b1[None, :, None, :]
        h = jax.nn.gelu(h, approximate=False)
        eo = jnp.einsum('besh,ehd->besd', h, w2) + b2[None, :, None, :]
        eo = eo.reshape(b, e * s, DIM)
        out = jnp.einsum('bmd,bnm->bnd', eo, combine)
        return out
    x = x + _L0_attn_ref(_layernorm(x, axis=-1), L0_attn_in_proj_w, L0_attn_conv_w, L0_attn_conv_b, L0_attn_x_proj_w, L0_attn_dt_proj_w, L0_attn_dt_proj_b, L0_attn_A_log, L0_attn_D, L0_attn_out_proj_w, L0_attn_norm_w, L0_attn_ffn_w1, L0_attn_ffn_b1, L0_attn_ffn_w2, L0_attn_ffn_b2, L0_attn_ffn_norm_w)
    x = x + _L0_xattn_ref(_layernorm(x, axis=-1), ctx_768, L0_xattn_Wq, L0_xattn_bq, L0_xattn_Wk, L0_xattn_bk, L0_xattn_Wv, L0_xattn_bv, L0_xattn_Wo, L0_xattn_bo)
    x = x + _L0_ffn_ref(_layernorm(x, axis=-1), L0_ffn_norm_gamma, L0_ffn_slot_norm_gamma, L0_ffn_slot_embeds, L0_ffn_w1, L0_ffn_b1, L0_ffn_w2, L0_ffn_b2)
    return x

_drawn_inputs = setup_inputs


def setup_inputs(seed=0):
    import zlib

    import numpy as np

    out = dict(_drawn_inputs(seed))
    spreads = {'L0_attn_D': (1.0, 0.6),
     'L0_attn_norm_w': (1.0, 0.2),
     'L0_attn_ffn_b1': (0.0, 0.468),
     'L0_attn_ffn_b2': (0.0, 0.1),
     'L0_attn_ffn_norm_w': (1.0, 0.2),
     'L0_ffn_norm_gamma': (1.0, 0.2),
     'L0_ffn_slot_norm_gamma': (1.0, 0.556),
     'L0_ffn_b1': (0.0, 0.471),
     'L0_ffn_b2': (0.0, 0.1)}
    factors = {'L0_attn_in_proj_w': 8.0,
     'L0_attn_conv_w': 8.0,
     'L0_attn_conv_b': 8.0,
     'L0_attn_x_proj_w': 8.0,
     'L0_attn_dt_proj_w': 8.0,
     'L0_attn_dt_proj_b': 8.0,
     'L0_attn_A_log': 8.0,
     'L0_attn_out_proj_w': 8.0,
     'L0_xattn_bq': 8.0,
     'L0_xattn_bk': 8.0,
     'L0_xattn_bv': 8.0,
     'L0_xattn_bo': 8.0}
    for name, (base, spread) in spreads.items():
        noise = np.random.default_rng([zlib.crc32(name.encode()), seed]).standard_normal(out[name].shape)
        drawn = base * np.exp(spread * noise) if base else spread * noise
        out[name] = jnp.asarray(drawn.astype(out[name].dtype))
    for name, factor in factors.items():
        out[name] = (out[name] * factor).astype(out[name].dtype)
    return out
```

```python
from contextlib import ExitStack

import concourse.bass as bass
from concourse import mybir

F32 = mybir.dt.float32
BF16 = mybir.dt.bfloat16
ALU = mybir.AluOpType
ACT = mybir.ActivationFunctionType
AX = mybir.AxisListType.X

P = 128
T = 2048
DM = 256
DK = DM // P
DI = 512
DB = DI // P
NS = 16
RANK = 16
TAPS = 4
FH = 1024
FB = FH // P
NH, HD = 16, 16
KV = 1601
KB = -(-KV // P)
CW = 192
CP = CW // 2
NE, SL = 8, 128
MS = NE * SL
C = 512
NC = T // C
CT = C // P
TT = T // P
G = 4
NG = NH // G
HALF = NH // DK
BG = 4
NBG = NS // BG
NW = 4
ARENA = 46400
ENGINES = 5

TERMS = [(0, 0), (0, 1), (1, 0), (1, 1), (0, 2), (2, 0)]
XR = len(TERMS) * HD
KCOLS = [(o, min(512, KV - o)) for o in range(0, KV, 512)]

CH = {}
_at = 0
for _n, _w in (("conv_w", DB * TAPS), ("conv_b", DB), ("dt_b", DB), ("a_log", DB * NS), ("skip", DB),
               ("ffn_b1", FB), ("bq", DK), ("bk", DK), ("moe_b1", NE * FB)):
    CH[_n] = (_at, _at + _w)
    _at += _w
CHW = _at


def decoder_layer(nc, x_d, ctx_d, win_d, xproj_d, dtw_d, wout_d, w1_d, w2_d, wq_d, wk_d, wv_d, wo_d,
                  chan_d, scales_d, rows_d, slots_d, mw1_d, mw2_d, mb2_d, out_d, bc_scratch):
    with ExitStack() as ctx:
        def sb(name, shape, dt=F32):
            return ctx.enter_context(nc.sbuf_tensor(name, shape, dt))

        def sem(name):
            return ctx.enter_context(nc.semaphore(name))

        ps = ctx.enter_context(nc.psum_tensor("ps", [P, 8, 512], F32))
        xt = sb("xt", [P, TT, DM])
        ident = sb("ident", [P, P])
        ones = sb("ones", [P, P])
        mhalf = sb("mhalf", [P, TT])
        chan = sb("chan", [P, CHW])
        scales = sb("scales", [P, 4, DM])
        rows = sb("rows", [1, 3, DM])
        stat = sb("stat", [P, TT, 6])
        mv = sb("mv", [P, TT, 2])
        sq = sb("sq", [P, TT])
        ve = sb("ve", [P, TT])
        rstd = sb("rstd", [P, TT])
        ve2 = sb("ve2", [P, TT])
        rstd2 = sb("rstd2", [P, TT])
        mark = sb("mark", [P, 1])
        arena = sb("arena", [P, ARENA])

        def ch(name, *dims):
            a, b = CH[name]
            v = chan[:, a:b]
            return v.rearrange("p (a b) -> p a b", b=dims[0]) if dims else v

        class Stack:
            def __init__(self, at=0):
                self.at = at

            def take(self, *shape, dt=F32):
                n = 1
                for s in shape:
                    n *= s
                words = n if dt == F32 else (n + 1) // 2
                v = arena[:, self.at:self.at + words]
                self.at += words
                assert self.at <= ARENA, self.at
                if dt != F32:
                    v = v.bitcast(dt)[:, 0:n]
                if len(shape) == 2:
                    v = v.rearrange("p (a b) -> p a b", b=shape[1])
                if len(shape) == 3:
                    v = v.rearrange("p (a b c) -> p a b c", b=shape[1], c=shape[2])
                if len(shape) == 4:
                    v = v.rearrange("p (a b c d) -> p a b c d", b=shape[1], c=shape[2], d=shape[3])
                return v

        m = Stack()
        win = m.take(DK, 2 * DI)
        xproj = m.take(DB, RANK + 2 * NS)
        dtw = m.take(DI)
        wout = m.take(DB, DM)
        w1 = m.take(DK, FH)
        w2 = m.take(FB, DM)
        neg_a = m.take(DB, NS)
        diag_skip = m.take(DB, P)
        carry = m.take(DB, NS)
        hist = m.take(DB, TAPS - 1)
        a0 = m.take(CT, DM)
        u = m.take(DB, C)
        zs = m.take(DB, C)
        xdbl = m.take(C)
        delta = m.take(DB, C)
        du = m.take(DB, C)
        bg = m.take(2, BG, C)
        cg = m.take(2, BG, C)
        region = m.at
        da = m.take(2, DB, C)
        dbu = m.take(2, DB, C)
        hs = m.take(2, DB, C)
        hc = m.take(2, DB, C)
        m2 = Stack(region)
        a0t = m2.take(DK, C)
        conv = m2.take(DB, C)
        upad = m2.take(DB, TAPS - 1 + C)
        sp_abs = m2.take(DB, C)
        sp_exp = m2.take(DB, C)
        sp_ln = m2.take(DB, C)
        sp_cor = m2.take(DB, C)
        m3 = Stack(region)
        yz = m3.take(DB, C)
        gate = m3.take(FB, C)
        hsum = m3.take(CT, DM)
        h1 = m3.take(CT, DM)
        h1t = m3.take(DK, C)
        rsum = m3.take(CT, DM)
        rnorm = m3.take(CT, DM)
        junk = m3.take(CT, DM)
        junk2 = m3.take(CT, DM)
        assert max(m2.at, m3.at) <= m.at

        a = Stack()
        kx = a.take(NH, KV, dt=BF16)
        qx = a.take(NH, C, dt=BF16)
        vx = a.take(KB, NH, 2 * HD)
        wq = a.take(DK, DM)
        wk = a.take(2, DM)
        wv = a.take(2, DM)
        wo = a.take(DK, DM)
        region = a.at
        ctxt = a.take(2, KV)
        kf = a.take(DK, KV)
        kp = [a.take(DK, KV, dt=BF16) for _ in range(3)]
        kr = [a.take(DK, KV) for _ in range(2)]
        a2 = Stack(region)
        xa = a2.take(CT, DM)
        xat = a2.take(DK, C)
        qf = a2.take(DK, C)
        qp = [a2.take(DK, C, dt=BF16) for _ in range(3)]
        qr = [a2.take(DK, C) for _ in range(2)]
        nmax = a2.take(CT, NH)
        nrow = a2.take(C, dt=BF16)
        prob = a2.take(2, G, C)
        ot = a2.take(NG, C)
        orec = a2.take(CT, NH)
        at = a2.take(CT, DM)
        att = a2.take(DK, C)

        e1 = Stack()
        lg = e1.take(TT, MS)
        cwt = e1.take(NE, T)
        xn = e1.take(TT, DM + 1)
        region = e1.at
        snt = e1.take(DK, MS)
        ex = e1.take(2, MS)
        xnt = e1.take(2, DK, P)
        mrun = e1.take(MS)
        mdiag = e1.take(NE, P)
        junk3 = e1.take(DM)
        e2 = Stack(region)
        slot = e2.take(2, DM)
        slt = e2.take(NE, DK, P)
        hid = e2.take(2, FB, P)
        eo = e2.take(NE, DM)
        b2 = e2.take(NE, DM)
        mcol = sb("mcol", [P, NE])
        srec = sb("srec", [P, NE])
        sqs = sb("sqs", [P, NE])
        nmx = sb("nmx", [P, TT])
        csum = sb("csum", [P, TT])
        crec = sb("crec", [P, TT])
        e3 = Stack()
        se = e3.take(NE, DM)
        sn = e3.take(NE, DM)
        junk4 = e3.take(NE, DM)
        e4 = Stack()
        mw1 = e4.take(NW, DK, FH)
        mw2 = e4.take(NW, FB, DM)
        assert e4.at <= TT * MS

        S = {name: sem(name) for name in """
            w_mamba x_in consts prep_act prep_dve chunk_done1 chunk_done2
            mark1 st1 mv1 ve1 rs1 a0_ready a0t_ps a0t_ready proj_ps u_raw z_ready hist_in conv_step hist_out u_ready
            xdbl_ps xdbl_ready bc_stored bc_even bc_odd dt_ps sp_in sp_act relu_ready sp_step delta_ready
            du_ready da_ready dbu_ready scan_done carry_done hc_ready y_acc y_ready
            yz_ready op_ps hsum_ready ss1 ms1 rms1 h1_ready h1t_ps h1t_ready ff1_ps g_ready ff2_ps
            r_ready ss2 ms2 rms2 rn_ready x1_ready
            w_attn w_ctx k_ps kf_ready kp_ready kr_ready kx_in v_ps vx_ready vx_init
            mark2 st2 mv2 ve3 rs3 xa_ready xat_ps xat_ready q_ps qf_ready qp_ready qr_ready qx_in
            ms_ps nm_ready nt_ps nrow_ready shift_in s_ps p_ready pv_done o_evac oq_ps orec_ready at_ready
            att_ps att_ready o_ps x2_ready
            w_slots ss4 ms4 rms4 sn_ready snt_ps snt_ready
            st5 mv5 ve5 rs5 y_normed ss5 ms5 rms5 xn_ready xn_one xnt_ps xnt_ready l_ps l_copy l_max l_run
            l_exp et_ps et_ready mt_ps mcol_ready mdiag_ready mb_ps l_sub d_ready
            slot_ps srec_ready slot_ready slt_ps slt_ready w_exp0 w_exp1 w_exp2 w_exp3 w_b2
            h_ps hid_ready eo_ps eo_ready c_ps crec_ready res_ready out_done""".split()}
        w_exp = [S["w_exp0"], S["w_exp1"], S["w_exp2"], S["w_exp3"]]
        bc_in = [S["bc_even"], S["bc_odd"]]

        def flat(v):
            return v.rearrange("p a b -> p (a b)")

        def over(v, n):
            return v.unsqueeze(1).to_broadcast([v.shape[0], n, v.shape[1]])

        def bank(n):
            return ps[:, n, :]

        def banks(n, k):
            return ps[:, n:n + k, :].rearrange("p a b -> p (a b)")

        def tok(n):
            return slice(n * P, n * P + P)

        def part(n):
            return slice(n * DM, n * DM + DM)

        block = ctx.enter_context(nc.Block())

        @block.sync
        def _(sp):
            sp.dma_start(xt[:, :, :], x_d.rearrange("(t p) d -> p t d", p=P)).then_inc(S["x_in"], 16)
            for dst, src in ((chan[:, :], chan_d), (win, win_d), (xproj, xproj_d), (dtw[0:RANK, :], dtw_d),
                             (wout, wout_d), (w1, w1_d), (w2, w2_d),
                             (flat(scales[:, :, :]), scales_d.to_broadcast([P, 4 * DM])),
                             (flat(rows[:, :, :]), rows_d)):
                sp.dma_start(dst, src).then_inc(S["w_mamba"], 16)

            with sp.Fori(0, NC) as c:
                sp.wait_ge(S["xdbl_ready"], c + 1)
                sp.dma_start(bc_scratch[bass.ds(c, 1), :, :].rearrange("o n t -> (o n) t"),
                             xdbl[RANK:RANK + 2 * NS, :]).then_inc(S["bc_stored"], 16)
                sp.wait_ge(S["bc_stored"], c * 16 + 16)
                for q in range(NBG):
                    if q >= 2:
                        sp.wait_ge(S["dbu_ready"], c * NS + BG * (q - 1))
                        sp.wait_ge(S["hc_ready"], c * NS + BG * (q - 1))
                    for dst, n in ((bg, q * BG), (cg, NS + q * BG)):
                        row = bc_scratch[bass.ds(c, 1), n:n + BG, :].rearrange("o n t -> o (n t)")
                        sp.dma_start(flat(dst[:, q % 2]), row.to_broadcast([P, BG * C])).then_inc(bc_in[q % 2], 16)
                sp.sem_inc(S["chunk_done1"], 1)

            sp.wait_ge(S["chunk_done1"], ENGINES * NC + 1)
            sp.dma_start(ctxt[0:CP], ctx_d).then_inc(S["w_ctx"], 16)
            for dst, src in ((wk[0:CP], wk_d), (wv[0:CP], wv_d), (wq, wq_d), (wo, wo_d)):
                sp.dma_start(dst, src).then_inc(S["w_attn"], 16)
            for n in range(3):
                sp.wait_ge(S["kp_ready"], n + 1)
                for j, (_, b) in enumerate(TERMS):
                    if b == n:
                        for k in range(DK):
                            sp.dma_start(kx[HD * j:HD * j + HD, HALF * k:HALF * k + HALF, :],
                                         kp[n][:, k, :]).then_inc(S["kx_in"], 16)

            with sp.Fori(0, NC) as c:
                for n in range(3):
                    sp.wait_ge(S["qp_ready"], c * 3 + n + 1)
                    for j, (b, _) in enumerate(TERMS):
                        if b == n:
                            for k in range(DK):
                                sp.dma_start(qx[HD * j:HD * j + HD, HALF * k:HALF * k + HALF, :],
                                             qp[n][:, k, :]).then_inc(S["qx_in"], 16)
                sp.wait_ge(S["nrow_ready"], c + 1)
                sp.dma_start(qx[XR:XR + 1, :, :], nrow[0:NH, :]).then_inc(S["shift_in"], 16)
                sp.wait_ge(S["shift_in"], c * 16 + 16)
                sp.sem_inc(S["chunk_done2"], 1)

            sp.wait_ge(S["chunk_done2"], ENGINES * NC + 1)
            sp.dma_start(se, slots_d).then_inc(S["w_slots"], 16)
            sp.wait_ge(S["mb_ps"], 2)
            sp.wait_ge(S["et_ready"], TT)
            sp.dma_start(flat(b2[0:1]), mb2_d).then_inc(S["w_b2"], 16)
            for x in range(NE):
                if x < NW:
                    sp.wait_ge(S["slot_ps"], NE)
                else:
                    sp.wait_ge(S["eo_ps"], x - NW + 1)
                sp.dma_start(mw1[:, x % NW], mw1_d[x]).then_inc(w_exp[x % NW], 16)
                sp.dma_start(mw2[:, x % NW], mw2_d[x]).then_inc(w_exp[x % NW], 16)
            for t in range(0, TT, CT):
                sp.wait_ge(S["res_ready"], t + CT)
                sp.dma_start(out_d[t * P:(t + CT) * P, :].rearrange("(t p) d -> p t d", p=P),
                             xt[:, t:t + CT, :]).then_inc(S["out_done"], 16)
            sp.wait_ge(S["out_done"], 16 * (TT // CT))

        @block.gpsimd
        def _(pool):
            pool.memset(ident[:, :], 0.0).then_inc(S["consts"], 1)
            pool.memset(ones[:, :], 1.0).then_inc(S["consts"], 1)
            pool.memset(mhalf[:, :], -0.5).then_inc(S["consts"], 1)
            pool.memset(flat(carry), 0.0).then_inc(S["consts"], 1)
            pool.memset(flat(hist), 0.0).then_inc(S["consts"], 1)
            pool.wait_ge(S["consts"], 1)
            pool.affine_select(out=ident[:, :], in_=ident[:, :], compare_op=ALU.not_equal, fill=1.0, base=0,
                               pattern=[[-1, P]], channel_multiplier=1).then_inc(S["consts"], 1)

            def rsqrt(dst, src, n):
                return pool.tensor_tensor(dst[:, 0:n], src[:, 0:n], mhalf[:, 0:n], ALU.pow)

            pool.wait_ge(S["consts"], 6)
            with pool.Fori(0, NC) as c:
                pool.wait_ge(S["ve1"], c + 1)
                rsqrt(rstd, ve, CT).then_inc(S["rs1"], 1)
                for n in range(NS):
                    q = n // BG
                    if n == 0:
                        pool.wait_ge(S["du_ready"], c + 1)
                    if n % BG == 0:
                        pool.wait_ge(bc_in[q % 2], c * 64 + 32 * (q // 2 + 1))
                    if n >= 2:
                        pool.wait_ge(S["scan_done"], c * NS * DB + DB * (n - 1))
                    pool.tensor_tensor(dbu[:, n % 2], du, over(bg[:, q % 2, n % BG], DB),
                                       ALU.mult).then_inc(S["dbu_ready"], 1)
                pool.wait_ge(S["ms1"], c + 1)
                rsqrt(rstd2, ve2, CT).then_inc(S["rms1"], 1)
                pool.wait_ge(S["ms2"], c + 1)
                rsqrt(rstd, ve, CT).then_inc(S["rms2"], 1)
                pool.wait_ge(S["rms2"], c + 1)
                pool.sem_inc(S["chunk_done1"], 1)

            pool.wait_ge(S["chunk_done1"], ENGINES * NC + 1)
            pool.memset(vx, 0.0).then_inc(S["vx_init"], 1)
            pool.wait_ge(S["vx_init"], 1)
            pool.memset(kx[XR:XR + 1, :, :], 1.0).then_inc(S["vx_init"], 1)
            pool.wait_ge(S["vx_init"], 2)
            pool.memset(vx[:, :, :, HD:HD + 1], 1.0).then_inc(S["vx_init"], 1)

            with pool.Fori(0, NC) as c:
                pool.wait_ge(S["ve3"], c + 1)
                rsqrt(rstd, ve, CT).then_inc(S["rs3"], 1)
                pool.wait_ge(S["rs3"], c + 1)
                pool.sem_inc(S["chunk_done2"], 1)

            pool.wait_ge(S["ms4"], 1)
            rsqrt(rstd2, ve2, NE).then_inc(S["rms4"], 1)
            pool.wait_ge(S["ve5"], 1)
            rsqrt(rstd, ve, TT).then_inc(S["rs5"], 1)
            pool.wait_ge(S["ms5"], 1)
            rsqrt(rstd2, ve2, TT).then_inc(S["rms5"], 1)

        @block.scalar
        def _(act):
            act.wait_ge(S["w_mamba"], 16 * 9)
            act.activation(flat(neg_a), ch("a_log"), ACT.Exp).then_inc(S["prep_act"], 1)

            with act.Fori(0, NC) as c:
                for k in range(DK):
                    act.wait_ge(S["a0t_ps"], c * DK + k + 1)
                    act.activation(a0t[:, k], bank(k), ACT.Copy).then_inc(S["a0t_ready"], 1)
                for d in range(DB):
                    act.wait_ge(S["proj_ps"], c * 2 * DB + DB + d + 1)
                    act.activation(zs[:, d], bank(2 + (DB + d) % 6), ACT.Silu).then_inc(S["z_ready"], 1)
                for d in range(DB):
                    act.wait_ge(S["conv_step"], c * TAPS * DB + (TAPS - 1) * DB + d + 1)
                    act.activation(u[:, d], conv[:, d], ACT.Silu).then_inc(S["u_ready"], 1)
                act.wait_ge(S["sp_in"], c * DB + DB)
                act.activation(flat(sp_abs), flat(delta), ACT.Abs).then_inc(S["sp_act"], 1)
                act.wait_ge(S["sp_act"], c * 3 + 1)
                act.activation(flat(sp_exp), flat(sp_abs), ACT.Exp, scale=-1.0).then_inc(S["sp_act"], 1)
                act.wait_ge(S["sp_act"], c * 3 + 2)
                act.activation(flat(sp_ln), flat(sp_exp), ACT.Ln, bias=1.0).then_inc(S["sp_act"], 1)

                def carry_over(n):
                    act.wait_ge(S["scan_done"], c * NS * DB + DB * (n + 1))
                    act.activation(carry[:, :, n:n + 1], hs[:, n % 2, :, C - 1:C], ACT.Copy).then_inc(S["carry_done"], 1)

                act.wait_ge(S["prep_dve"], 1 + DB)
                for n in range(NS):
                    if n == 0:
                        act.wait_ge(S["delta_ready"], c + 1)
                    if n >= 2:
                        act.wait_ge(S["scan_done"], c * NS * DB + DB * (n - 1))
                    for d in range(DB):
                        act.activation(da[:, n % 2, d], delta[:, d], ACT.Exp,
                                       scale=neg_a[:, d, n:n + 1]).then_inc(S["da_ready"], 1)
                    if n >= 1:
                        carry_over(n - 1)
                carry_over(NS - 1)
                act.wait_ge(S["carry_done"], c * NS + NS)

                for i in range(CT):
                    act.wait_ge(S["hsum_ready"], c * 2 + i // 2 + 1)
                    act.activation(junk[:, i], hsum[:, i], ACT.Square, accum_out=sq[:, i:i + 1]).then_inc(S["ss1"], 1)
                for k in range(DK):
                    act.wait_ge(S["h1t_ps"], c * DK + k + 1)
                    act.activation(h1t[:, k], bank(6 + k), ACT.Copy).then_inc(S["h1t_ready"], 1)
                for f in range(FB):
                    act.wait_ge(S["ff1_ps"], c * FB + f + 1)
                    act.activation(gate[:, f], bank(f % 4), ACT.Gelu,
                                   bias=ch("ffn_b1")[:, f:f + 1]).then_inc(S["g_ready"], 1)
                act.wait_ge(S["ms1"], c + 1)
                for i in range(CT):
                    act.wait_ge(S["r_ready"], c * 2 + i // 2 + 1)
                    act.activation(junk2[:, i], rsum[:, i], ACT.Square, accum_out=sq[:, i:i + 1]).then_inc(S["ss2"], 1)
                act.wait_ge(S["ss2"], c * CT + CT)
                act.sem_inc(S["chunk_done1"], 1)

            act.wait_ge(S["kf_ready"], DK * len(KCOLS))
            act.activation(flat(kp[0]), flat(kf), ACT.Copy).then_inc(S["kp_ready"], 1)
            for n in range(1, 3):
                act.wait_ge(S["kr_ready"], n)
                act.activation(flat(kp[n]), flat(kr[n - 1]), ACT.Copy).then_inc(S["kp_ready"], 1)
            act.wait_ge(S["vx_init"], 3)
            for b in range(0, KB, 2):
                nb, n = min(2, KB - b), min(P, KV - b * P)
                act.wait_ge(S["v_ps"], b // 2 + 1)
                act.activation(vx[0:n, b:b + nb, :, 0:HD],
                               ps[0:n, b // 2, 0:nb * DM].rearrange("p (b h d) -> p b h d", b=nb, d=HD),
                               ACT.Copy).then_inc(S["vx_ready"], 1)

            with act.Fori(0, NC) as c:
                for k in range(DK):
                    act.wait_ge(S["xat_ps"], c * DK + k + 1)
                    act.activation(xat[:, k], bank(k), ACT.Copy).then_inc(S["xat_ready"], 1)
                act.wait_ge(S["qf_ready"], c * DK + DK)
                act.activation(flat(qp[0]), flat(qf), ACT.Copy).then_inc(S["qp_ready"], 1)
                for n in range(1, 3):
                    act.wait_ge(S["qr_ready"], c * 2 + n)
                    act.activation(flat(qp[n]), flat(qr[n - 1]), ACT.Copy).then_inc(S["qp_ready"], 1)
                act.wait_ge(S["nt_ps"], c + 1)
                act.activation(nrow[0:NH, :], ps[0:NH, 0, :], ACT.Copy).then_inc(S["nrow_ready"], 1)
                for v in range(NG * KB):
                    n = min(P, KV - v % KB * P)
                    if v >= 2:
                        act.wait_ge(S["pv_done"], c * NG * KB + v - 1)
                    for h in range(2):
                        r = 2 * v + h
                        act.wait_ge(S["s_ps"], c * 2 * NG * KB + r + 1)
                        act.activation(flat(prob[0:n, v % 2, 2 * h:2 * h + 2]),
                                       ps[0:n, 2 * (r % 3):2 * (r % 3) + 2, :].rearrange("p a b -> p (a b)"),
                                       ACT.Exp, scale=HD ** -0.5).then_inc(S["p_ready"], 1)
                for k in range(DK):
                    act.wait_ge(S["att_ps"], c * DK + k + 1)
                    act.activation(att[:, k], bank(4 + k), ACT.Copy).then_inc(S["att_ready"], 1)
                act.wait_ge(S["att_ready"], c * DK + DK)
                act.sem_inc(S["chunk_done2"], 1)

            act.wait_ge(S["w_slots"], 16)
            for x in range(NE):
                act.activation(junk4[:, x], se[:, x], ACT.Square, accum_out=sqs[:, x:x + 1]).then_inc(S["ss4"], 1)
            for r in range(4):
                act.wait_ge(S["snt_ps"], r + 1)
                act.activation(snt[:, r // 2, r % 2 * 512:r % 2 * 512 + 512], bank(r), ACT.Copy).then_inc(S["snt_ready"], 1)
            for t in range(TT):
                act.wait_ge(S["y_normed"], t + 1)
                if t >= 1:
                    act.wait_ge(S["ss5"], t)
                act.activation(junk3, xn[:, t, 0:DM], ACT.Square, accum_out=sq[:, t:t + 1]).then_inc(S["ss5"], 1)

            def turned(t):
                act.wait_ge(S["et_ps"], t + 1)
                act.activation(cwt[:, :, tok(t)], banks(4, 2).rearrange("p (e n) -> p e n", n=P),
                               ACT.Copy).then_inc(S["et_ready"], 1)

            def combine_weights(t):
                act.wait_ge(S["l_max"], t + 1)
                if t >= 2:
                    act.wait_ge(S["et_ps"], t - 1)
                act.activation(ex[:, t % 2], lg[:, t], ACT.Exp, bias=nmx[:, t:t + 1],
                               accum_out=csum[:, t:t + 1]).then_inc(S["l_exp"], 1)

            for t in range(TT + 2):
                if t < TT:
                    act.wait_ge(S["xnt_ps"], t + 1)
                    if t >= 2:
                        act.wait_ge(S["l_ps"], t - 1)
                    act.activation(flat(xnt[:, t % 2]), ps[:, 6 + t % 2, 0:DK * P], ACT.Copy).then_inc(S["xnt_ready"], 1)
                    act.wait_ge(S["l_ps"], t + 1)
                    act.activation(lg[:, t], banks(2 * (t % 2), 2), ACT.Copy).then_inc(S["l_copy"], 1)
                if 1 <= t <= TT:
                    combine_weights(t - 1)
                if t >= 2:
                    turned(t - 2)
            for t in range(TT):
                act.wait_ge(S["l_sub"], t + 1)
                act.activation(lg[:, t], lg[:, t], ACT.Exp).then_inc(S["d_ready"], 1)
            for x in range(NE):
                act.wait_ge(S["slt_ps"], x + 1)
                act.activation(flat(slt[:, x]), ps[:, 6 + x % 2, 0:DK * P], ACT.Copy).then_inc(S["slt_ready"], 1)
            for x in range(NE):
                if x >= 2:
                    act.wait_ge(S["eo_ps"], x - 1)
                for f in range(FB):
                    if f % 4 == 0:
                        act.wait_ge(S["h_ps"], 2 * x + f // 4 + 1)
                    act.activation(hid[:, x % 2, f], ps[:, 2 * (x % 2) + f // 4, tok(f % 4)], ACT.Gelu,
                                   bias=ch("moe_b1")[:, x * FB + f:x * FB + f + 1]).then_inc(S["hid_ready"], 1)

        @block.vector
        def _(dve):
            dve.wait_ge(S["prep_act"], 1)
            dve.tensor_scalar(flat(neg_a), flat(neg_a), -1.0, None, ALU.mult).then_inc(S["prep_dve"], 1)
            dve.wait_ge(S["consts"], 6)
            for d in range(DB):
                dve.tensor_scalar(diag_skip[:, d], ident[:, :], ch("skip")[:, d:d + 1], None,
                                  ALU.mult).then_inc(S["prep_dve"], 1)
            dve.wait_ge(S["x_in"], 16)
            dve.sem_inc(S["chunk_done1"], 1)
            dve.sem_inc(S["chunk_done2"], 1)

            def xtile(t, n=1):
                v = xt[:, bass.ds(t, n), :]
                return flat(v) if n == 1 else v

            conv_w = ch("conv_w", TAPS)
            with dve.Fori(0, NC) as c:
                dve.wait_ge(S["chunk_done1"], c * ENGINES + 1)
                dve.tensor_copy(upad[:, :, 0:TAPS - 1], hist).then_inc(S["hist_in"], 1)
                for i in range(CT):
                    dve.bn_stats(stat[:, i, :], xtile(c * CT + i)).then_inc(S["st1"], 1)
                dve.wait_ge(S["st1"], c * CT + CT)
                dve.memset(mark[:, :], 0.0).then_inc(S["mark1"], 1)
                for i in range(CT):
                    dve.bn_aggr(mv[:, i, :], stat[:, i, :]).then_inc(S["mv1"], 1)
                dve.wait_ge(S["mv1"], c * CT + CT)
                dve.tensor_scalar(ve[:, 0:CT], mv[:, 0:CT, 1], 1e-5, None, ALU.add).then_inc(S["ve1"], 1)
                dve.wait_ge(S["rs1"], c + 1)
                for i in range(CT):
                    dve.tensor_scalar(a0[:, i], xtile(c * CT + i), mv[:, i, 0:1], rstd[:, i:i + 1],
                                      ALU.subtract, ALU.mult).then_inc(S["a0_ready"], 1)
                for d in range(DB):
                    dve.wait_ge(S["proj_ps"], c * 2 * DB + d + 1)
                    dve.tensor_copy(upad[:, d, TAPS - 1:TAPS - 1 + C], bank(2 + d)).then_inc(S["u_raw"], 1)
                dve.wait_ge(S["hist_in"], c + 1)
                for step, j in enumerate(reversed(range(TAPS))):
                    for d in range(DB):
                        if step == 0:
                            dve.wait_ge(S["u_raw"], c * DB + d + 1)
                            dve.tensor_scalar(conv[:, d], upad[:, d, j:j + C], conv_w[:, d, j:j + 1],
                                              ch("conv_b")[:, d:d + 1], ALU.mult, ALU.add).then_inc(S["conv_step"], 1)
                        else:
                            dve.wait_ge(S["conv_step"], c * TAPS * DB + (step - 1) * DB + d + 1)
                            dve.scalar_tensor_tensor(conv[:, d], upad[:, d, j:j + C], conv_w[:, d, j:j + 1],
                                                     conv[:, d], ALU.mult, ALU.add).then_inc(S["conv_step"], 1)
                dve.tensor_copy(hist, upad[:, :, C:C + TAPS - 1]).then_inc(S["hist_out"], 1)
                dve.wait_ge(S["xdbl_ps"], c + 1)
                dve.tensor_copy(xdbl[0:RANK + 2 * NS, :], ps[0:RANK + 2 * NS, 0, :]).then_inc(S["xdbl_ready"], 1)
                for d in range(DB):
                    dve.wait_ge(S["dt_ps"], c * DB + d + 1)
                    dve.tensor_scalar(delta[:, d], bank(4 + d), ch("dt_b")[:, d:d + 1], None,
                                      ALU.add).then_inc(S["sp_in"], 1)
                dve.wait_ge(S["sp_in"], c * DB + DB)
                dve.wait_ge(S["sp_act"], c * 3 + 1)
                dve.tensor_scalar(flat(delta), flat(delta), 0.0, None, ALU.max).then_inc(S["relu_ready"], 1)
                dve.wait_ge(S["sp_act"], c * 3 + 2)
                dve.tensor_scalar(flat(sp_cor), flat(sp_exp), 1.0, 1.0, ALU.add, ALU.subtract).then_inc(S["sp_step"], 1)
                dve.wait_ge(S["sp_step"], c * 3 + 1)
                dve.tensor_tensor(flat(sp_cor), flat(sp_exp), flat(sp_cor), ALU.subtract).then_inc(S["sp_step"], 1)
                dve.wait_ge(S["sp_act"], c * 3 + 3)
                dve.wait_ge(S["sp_step"], c * 3 + 2)
                dve.tensor_tensor(flat(sp_cor), flat(sp_cor), flat(sp_ln), ALU.add).then_inc(S["sp_step"], 1)
                dve.wait_ge(S["relu_ready"], c + 1)
                dve.wait_ge(S["sp_step"], c * 3 + 3)
                dve.tensor_tensor(flat(delta), flat(delta), flat(sp_cor), ALU.add).then_inc(S["delta_ready"], 1)
                dve.wait_ge(S["delta_ready"], c + 1)
                dve.wait_ge(S["u_ready"], c * DB + DB)
                dve.tensor_tensor(flat(du), flat(delta), flat(u), ALU.mult).then_inc(S["du_ready"], 1)

                for n in range(NS + 1):
                    if n < NS:
                        dve.wait_ge(S["dbu_ready"], c * NS + n + 1)
                        if n >= 2:
                            dve.wait_ge(S["hc_ready"], c * NS + n - 1)
                            dve.wait_ge(S["carry_done"], c * NS + n - 1)
                        for d in range(DB):
                            dve.wait_ge(S["da_ready"], c * NS * DB + n * DB + d + 1)
                            dve.tensor_tensor_scan(hs[:, n % 2, d], da[:, n % 2, d], dbu[:, n % 2, d],
                                                   carry[:, d, n:n + 1], ALU.mult, ALU.add).then_inc(S["scan_done"], 1)
                    if n >= 1:
                        k, q = n - 1, (n - 1) // BG
                        if k % BG == 0:
                            dve.wait_ge(bc_in[q % 2], c * 64 + 32 * (q // 2 + 1))
                        if k >= 2:
                            dve.wait_ge(S["y_acc"], c * NS + k - 1)
                        dve.wait_ge(S["scan_done"], c * NS * DB + n * DB)
                        dve.tensor_tensor(hc[:, k % 2], hs[:, k % 2], over(cg[:, q % 2, k % BG], DB),
                                          ALU.mult).then_inc(S["hc_ready"], 1)

                dve.wait_ge(S["y_ready"], c + 1)
                dve.wait_ge(S["z_ready"], c * DB + DB)
                dve.tensor_tensor(flat(yz), banks(0, DB), flat(zs), ALU.mult).then_inc(S["yz_ready"], 1)
                for b in range(2):
                    dve.wait_ge(S["op_ps"], c * 2 + b + 1)
                    dve.tensor_tensor(flat(hsum[:, 2 * b:2 * b + 2]), bank(4 + b), flat(a0[:, 2 * b:2 * b + 2]),
                                      ALU.add).then_inc(S["hsum_ready"], 1)
                dve.wait_ge(S["ss1"], c * CT + CT)
                dve.tensor_scalar(ve2[:, 0:CT], sq[:, 0:CT], 1.0 / DM, 1e-12, ALU.mult, ALU.add).then_inc(S["ms1"], 1)
                dve.wait_ge(S["hsum_ready"], c * 2 + 2)
                dve.wait_ge(S["rms1"], c + 1)
                for i in range(CT):
                    dve.scalar_tensor_tensor(h1[:, i], hsum[:, i], rstd2[:, i:i + 1], scales[:, 0, :],
                                             ALU.mult, ALU.mult).then_inc(S["h1_ready"], 1)
                dve.wait_ge(S["h1_ready"], c * CT + CT)
                for b in range(2):
                    dve.wait_ge(S["ff2_ps"], c * 2 + b + 1)
                    dve.tensor_tensor(flat(rsum[:, 2 * b:2 * b + 2]), bank(4 + b), flat(h1[:, 2 * b:2 * b + 2]),
                                      ALU.add).then_inc(S["r_ready"], 1)
                dve.wait_ge(S["ss2"], c * CT + CT)
                dve.tensor_scalar(ve[:, 0:CT], sq[:, 0:CT], 1.0 / DM, 1e-12, ALU.mult, ALU.add).then_inc(S["ms2"], 1)
                dve.wait_ge(S["r_ready"], c * 2 + 2)
                dve.wait_ge(S["rms2"], c + 1)
                for i in range(CT):
                    dve.scalar_tensor_tensor(rnorm[:, i], rsum[:, i], rstd[:, i:i + 1], scales[:, 1, :],
                                             ALU.mult, ALU.mult).then_inc(S["rn_ready"], 1)
                dve.wait_ge(S["rn_ready"], c * CT + CT)
                dve.tensor_tensor(xtile(c * CT, CT), xtile(c * CT, CT), rnorm, ALU.add).then_inc(S["x1_ready"], 1)
                dve.wait_ge(S["x1_ready"], c + 1)
                dve.sem_inc(S["chunk_done1"], 1)

            for k in range(DK):
                for j, (o, w) in enumerate(KCOLS):
                    dve.wait_ge(S["k_ps"], k * len(KCOLS) + j + 1)
                    dve.tensor_scalar(kf[:, k, o:o + w], ps[:, 4 * k + j, 0:w], ch("bk")[:, k:k + 1], None,
                                      ALU.add).then_inc(S["kf_ready"], 1)
            dve.wait_ge(S["kf_ready"], DK * len(KCOLS))
            for n in range(2):
                dve.wait_ge(S["kp_ready"], n + 1)
                if n:
                    dve.wait_ge(S["kr_ready"], n)
                dve.tensor_tensor(flat(kr[n]), flat(kr[n - 1] if n else kf), flat(kp[n]),
                                  ALU.subtract).then_inc(S["kr_ready"], 1)

            dve.wait_ge(S["v_ps"], -(-KB // 2))
            dve.wait_ge(S["kx_in"], 16 * DK * len(TERMS))
            with dve.Fori(0, NC) as c:
                dve.wait_ge(S["chunk_done2"], c * ENGINES + 1)
                dve.memset(mark[:, :], 0.0).then_inc(S["mark2"], 1)
                for i in range(CT):
                    dve.bn_stats(stat[:, i, :], xtile(c * CT + i)).then_inc(S["st2"], 1)
                dve.wait_ge(S["mark2"], c * 2 + 1)
                dve.wait_ge(S["st2"], c * CT + CT)
                dve.memset(mark[:, :], 0.0).then_inc(S["mark2"], 1)
                for i in range(CT):
                    dve.bn_aggr(mv[:, i, :], stat[:, i, :]).then_inc(S["mv2"], 1)
                dve.wait_ge(S["mv2"], c * CT + CT)
                dve.tensor_scalar(ve[:, 0:CT], mv[:, 0:CT, 1], 1e-5, None, ALU.add).then_inc(S["ve3"], 1)
                dve.wait_ge(S["rs3"], c + 1)
                for i in range(CT):
                    dve.tensor_scalar(xa[:, i], xtile(c * CT + i), mv[:, i, 0:1], rstd[:, i:i + 1],
                                      ALU.subtract, ALU.mult).then_inc(S["xa_ready"], 1)
                for k in range(DK):
                    dve.wait_ge(S["q_ps"], c * DK + k + 1)
                    dve.tensor_scalar(qf[:, k], bank(2 + k), ch("bq")[:, k:k + 1], None, ALU.add).then_inc(S["qf_ready"], 1)
                dve.wait_ge(S["qf_ready"], c * DK + DK)
                for n in range(2):
                    dve.wait_ge(S["qp_ready"], c * 3 + n + 1)
                    if n:
                        dve.wait_ge(S["qr_ready"], c * 2 + n)
                    dve.tensor_tensor(flat(qr[n]), flat(qr[n - 1] if n else qf), flat(qp[n]),
                                      ALU.subtract).then_inc(S["qr_ready"], 1)
                for w in range(CT * NH):
                    dve.wait_ge(S["ms_ps"], c * CT * NH + w + 1)
                    dve.tensor_reduce(nmax[:, w // NH, w % NH:w % NH + 1], banks(4 * (w % 2), 4)[:, 0:KV], AX, ALU.max,
                                      negate=True).then_inc(S["nm_ready"], 1)
                for g in range(NG):
                    dve.wait_ge(S["pv_done"], c * NG * KB + KB * (g + 1))
                    dve.tensor_copy(ot[:, g], bank(6 + g % 2)).then_inc(S["o_evac"], 1)
                for i in range(CT):
                    dve.wait_ge(S["oq_ps"], c * CT + i + 1)
                    o = bank(i).rearrange("p (h w) -> p h w", w=2 * HD)
                    dve.reciprocal(orec[:, i, :].unsqueeze(2), o[:, :, HD:HD + 1]).then_inc(S["orec_ready"], 1)
                    dve.wait_ge(S["orec_ready"], c * CT + i + 1)
                    dve.tensor_tensor(at[:, i].rearrange("p (h w) -> p h w", w=HD), o[:, :, 0:HD],
                                      orec[:, i, :].unsqueeze(2).to_broadcast([P, NH, HD]), ALU.mult).then_inc(S["at_ready"], 1)
                for b in range(2):
                    dve.wait_ge(S["o_ps"], c * 2 + b + 1)
                    dve.tensor_tensor(xtile(c * CT + 2 * b, 2), xtile(c * CT + 2 * b, 2),
                                      bank(6 + b).rearrange("p (a d) -> p a d", d=DM), ALU.add).then_inc(S["x2_ready"], 1)
                dve.wait_ge(S["x2_ready"], c * 2 + 2)
                dve.sem_inc(S["chunk_done2"], 1)

            dve.wait_ge(S["ss4"], NE)
            dve.tensor_scalar(ve2[:, 0:NE], sqs[:, :], 1e-24, 1.0 / DM, ALU.max, ALU.mult).then_inc(S["ms4"], 1)
            for t in range(TT):
                dve.bn_stats(stat[:, t, :], xt[:, t, :]).then_inc(S["st5"], 1)
            for t in range(TT):
                dve.wait_ge(S["st5"], t + 1)
                dve.bn_aggr(mv[:, t, :], stat[:, t, :]).then_inc(S["mv5"], 1)
            dve.wait_ge(S["mv5"], TT)
            dve.tensor_scalar(ve[:, :], mv[:, :, 1], 1e-5, None, ALU.add).then_inc(S["ve5"], 1)
            dve.wait_ge(S["rms4"], 1)
            for x in range(NE):
                dve.scalar_tensor_tensor(sn[:, x], se[:, x], rstd2[:, x:x + 1], scales[:, 3, :],
                                         ALU.mult, ALU.mult).then_inc(S["sn_ready"], 1)
            dve.wait_ge(S["rs5"], 1)
            for t in range(TT):
                dve.tensor_scalar(xn[:, t, 0:DM], xt[:, t, :], mv[:, t, 0:1], rstd[:, t:t + 1],
                                  ALU.subtract, ALU.mult).then_inc(S["y_normed"], 1)
            dve.memset(xn[:, :, DM:DM + 1], 1.0).then_inc(S["xn_one"], 1)
            dve.memset(mrun, -3.0e38).then_inc(S["xn_one"], 1)
            dve.wait_ge(S["ss5"], TT)
            dve.wait_ge(S["sn_ready"], NE)
            dve.tensor_scalar(ve2[:, :], sq[:, :], 1e-24, 1.0 / DM, ALU.max, ALU.mult).then_inc(S["ms5"], 1)
            dve.wait_ge(S["rms5"], 1)
            for t in range(TT):
                dve.wait_ge(S["y_normed"], t + 1)
                dve.scalar_tensor_tensor(xn[:, t, 0:DM], xn[:, t, 0:DM], rstd2[:, t:t + 1], scales[:, 2, :],
                                         ALU.mult, ALU.mult).then_inc(S["xn_ready"], 1)
            dve.wait_ge(S["xn_one"], 2)
            for t in range(TT):
                dve.wait_ge(S["l_copy"], t + 1)
                dve.tensor_reduce(nmx[:, t:t + 1], lg[:, t], AX, ALU.max, negate=True).then_inc(S["l_max"], 1)
                if t >= 1:
                    dve.wait_ge(S["l_run"], t)
                dve.tensor_tensor(mrun, mrun, lg[:, t], ALU.max).then_inc(S["l_run"], 1)
            dve.wait_ge(S["mt_ps"], 1)
            dve.tensor_reduce(mcol[:, :], banks(0, 2).rearrange("p (e n) -> p e n", n=P), AX, ALU.max).then_inc(S["mcol_ready"], 1)
            dve.wait_ge(S["mcol_ready"], 1)
            for x in range(NE):
                dve.tensor_scalar(mdiag[:, x], ident[:, :], mcol[:, x:x + 1], None, ALU.mult).then_inc(S["mdiag_ready"], 1)
            dve.wait_ge(S["mb_ps"], 2)
            for t in range(TT):
                dve.wait_ge(S["l_exp"], t + 1)
                dve.tensor_tensor(lg[:, t], lg[:, t], banks(2, 2), ALU.subtract).then_inc(S["l_sub"], 1)
            for x in range(NE):
                dve.wait_ge(S["slot_ps"], x + 1)
                dve.reciprocal(srec[:, x:x + 1], ps[:, 4 + x % 2, DM:DM + 1]).then_inc(S["srec_ready"], 1)
                dve.wait_ge(S["srec_ready"], x + 1)
                if x >= 2:
                    dve.wait_ge(S["slt_ps"], x - 1)
                dve.tensor_scalar(slot[:, x % 2], ps[:, 4 + x % 2, 0:DM], srec[:, x:x + 1], None,
                                  ALU.mult).then_inc(S["slot_ready"], 1)
            for x in range(NE):
                dve.wait_ge(S["eo_ps"], x + 1)
                dve.tensor_copy(eo[:, x], ps[:, 4 + x % 2, 0:DM]).then_inc(S["eo_ready"], 1)
            dve.reciprocal(crec[:, :], csum[:, :]).then_inc(S["crec_ready"], 1)
            dve.wait_ge(S["crec_ready"], 1)
            for t in range(TT):
                dve.wait_ge(S["c_ps"], t + 1)
                dve.scalar_tensor_tensor(xt[:, t, :], ps[:, t % 8, 0:DM], crec[:, t:t + 1], xt[:, t, :],
                                         ALU.mult, ALU.add).then_inc(S["res_ready"], 1)

        @block.tensor
        def _(pe):
            mm = pe.matmul
            pe.wait_ge(S["consts"], 6)
            pe.wait_ge(S["w_mamba"], 16 * 9)
            pe.wait_ge(S["prep_dve"], 1 + DB)

            def turn(dst, src):
                return pe.transpose(dst, src, ident[:, :])

            with pe.Fori(0, NC) as c:
                for k in range(DK):
                    for i in range(CT):
                        if k == 0:
                            pe.wait_ge(S["a0_ready"], c * CT + i + 1)
                        last = turn(bank(k)[:, tok(i)], a0[:, i, tok(k)])
                    last.then_inc(S["a0t_ps"], 1)
                for o in range(2 * DB):
                    if o >= 6:
                        pe.wait_ge(S["u_raw"], c * DB + o - 5)
                    for k in range(DK):
                        if o == 0:
                            pe.wait_ge(S["a0t_ready"], c * DK + k + 1)
                        last = mm(bank(2 + o % 6), win[:, k, tok(o)], a0t[:, k], start=(k == 0), stop=(k == DK - 1))
                    last.then_inc(S["proj_ps"], 1)
                for d in range(DB):
                    pe.wait_ge(S["u_ready"], c * DB + d + 1)
                    last = mm(ps[0:RANK + 2 * NS, 0, :], xproj[:, d], u[:, d], start=(d == 0), stop=(d == DB - 1))
                last.then_inc(S["xdbl_ps"], 1)
                pe.wait_ge(S["xdbl_ready"], c + 1)
                pe.wait_ge(S["z_ready"], c * DB + DB)
                for d in range(DB):
                    mm(bank(4 + d), dtw[0:RANK, tok(d)], xdbl[0:RANK, :], start=True, stop=True).then_inc(S["dt_ps"], 1)
                for n in range(NS):
                    pe.wait_ge(S["hc_ready"], c * NS + n + 1)
                    for d in range(DB):
                        last = mm(bank(d), ident[:, :], hc[:, n % 2, d], start=(n == 0), stop=False)
                    last.then_inc(S["y_acc"], 1)
                for d in range(DB):
                    last = mm(bank(d), diag_skip[:, d], u[:, d], start=False, stop=True)
                last.then_inc(S["y_ready"], 1)
                pe.wait_ge(S["yz_ready"], c + 1)
                for i in range(CT):
                    for d in range(DB):
                        last = mm(bank(4 + i // 2)[:, part(i % 2)], yz[:, d, tok(i)], wout[:, d],
                                  start=(d == 0), stop=(d == DB - 1))
                    if i % 2:
                        last.then_inc(S["op_ps"], 1)
                for k in range(DK):
                    for i in range(CT):
                        if k == 0:
                            pe.wait_ge(S["h1_ready"], c * CT + i + 1)
                        last = turn(bank(6 + k)[:, tok(i)], h1[:, i, tok(k)])
                    last.then_inc(S["h1t_ps"], 1)
                for f in range(FB):
                    if f >= 4:
                        pe.wait_ge(S["g_ready"], c * FB + f - 3)
                    for k in range(DK):
                        if f == 0:
                            pe.wait_ge(S["h1t_ready"], c * DK + k + 1)
                        last = mm(bank(f % 4), w1[:, k, tok(f)], h1t[:, k], start=(k == 0), stop=(k == DK - 1))
                    last.then_inc(S["ff1_ps"], 1)
                for i in range(CT):
                    acc = bank(4 + i // 2)[:, part(i % 2)]
                    for f in range(FB):
                        if i == 0:
                            pe.wait_ge(S["g_ready"], c * FB + f + 1)
                        mm(acc, gate[:, f, tok(i)], w2[:, f], start=(f == 0), stop=False)
                    last = mm(acc, ones[0:1, :], rows[0:1, 0, :], start=False, stop=True)
                    if i % 2:
                        last.then_inc(S["ff2_ps"], 1)
                pe.wait_ge(S["ff2_ps"], c * 2 + 2)
                pe.sem_inc(S["chunk_done1"], 1)

            pe.wait_ge(S["chunk_done1"], ENGINES * NC + 1)
            pe.wait_ge(S["w_ctx"], 16)
            pe.wait_ge(S["w_attn"], 16 * 4)
            for k in range(DK):
                for j, (o, w) in enumerate(KCOLS):
                    for x in range(2):
                        last = mm(ps[:, 4 * k + j, 0:w], wk[0:CP, x, tok(k)], ctxt[0:CP, x, o:o + w],
                                  start=(x == 0), stop=(x == 1))
                    last.then_inc(S["k_ps"], 1)
            for b in range(KB):
                n = min(P, KV - b * P)
                if b % 2 == 0:
                    pe.wait_ge(S["kf_ready"], b // 2 + 1)
                acc = ps[0:n, b // 2, part(b % 2)]
                for x in range(2):
                    mm(acc, ctxt[0:CP, x, b * P:b * P + n], wv[0:CP, x], start=(x == 0), stop=False)
                last = mm(acc, ones[0:1, 0:n], rows[0:1, 1, :], start=False, stop=True)
                if b % 2 or b == KB - 1:
                    last.then_inc(S["v_ps"], 1)
            pe.wait_ge(S["kx_in"], 16 * DK * len(TERMS))
            pe.wait_ge(S["vx_ready"], -(-KB // 2))

            with pe.Fori(0, NC) as c:
                for k in range(DK):
                    for i in range(CT):
                        if k == 0:
                            pe.wait_ge(S["xa_ready"], c * CT + i + 1)
                        last = turn(bank(k)[:, tok(i)], xa[:, i, tok(k)])
                    last.then_inc(S["xat_ps"], 1)
                for k in range(DK):
                    for x in range(DK):
                        if k == 0:
                            pe.wait_ge(S["xat_ready"], c * DK + x + 1)
                        last = mm(bank(2 + k), wq[:, x, tok(k)], xat[:, x], start=(x == 0), stop=(x == DK - 1))
                    last.then_inc(S["q_ps"], 1)
                pe.wait_ge(S["qx_in"], c * 16 * DK * len(TERMS) + 16 * DK * len(TERMS))
                for w in range(CT * NH):
                    i, h = w // NH, w % NH
                    if w >= 2:
                        pe.wait_ge(S["nm_ready"], c * CT * NH + w - 1)
                    for j, (o, n) in enumerate(KCOLS):
                        last = mm(ps[:, 4 * (w % 2) + j, 0:n], qx[0:XR, h, tok(i)], kx[0:XR, h, o:o + n],
                                  start=True, stop=True)
                    last.then_inc(S["ms_ps"], 1)
                pe.wait_ge(S["nm_ready"], c * CT * NH + CT * NH)
                for i in range(CT):
                    last = turn(ps[0:NH, 0, tok(i)], nmax[:, i, :])
                last.then_inc(S["nt_ps"], 1)
                pe.wait_ge(S["shift_in"], c * 16 + 16)
                for v in range(NG * KB + 1):
                    if v < NG * KB:
                        g, b = v // KB, v % KB
                        n = min(P, KV - b * P)
                        for h in range(2):
                            r = 2 * v + h
                            if r >= 3:
                                pe.wait_ge(S["p_ready"], c * 2 * NG * KB + r - 2)
                            for x in range(2):
                                head = G * g + 2 * h + x
                                last = mm(ps[0:n, 2 * (r % 3) + x, :], kx[0:XR + 1, head, b * P:b * P + n],
                                          qx[0:XR + 1, head, :], start=True, stop=True)
                            last.then_inc(S["s_ps"], 1)
                    if v >= 1:
                        g, b = (v - 1) // KB, (v - 1) % KB
                        n = min(P, KV - b * P)
                        if b == 0 and g >= 2:
                            pe.wait_ge(S["o_evac"], c * NG + g - 1)
                        pe.wait_ge(S["p_ready"], c * 2 * NG * KB + 2 * v)
                        for x in range(G):
                            last = mm(ps[2 * HD * x:2 * HD * x + 2 * HD, 6 + g % 2, :], vx[0:n, b, G * g + x, :],
                                      prob[0:n, (v - 1) % 2, x], start=(b == 0), stop=(b == KB - 1))
                        last.then_inc(S["pv_done"], 1)
                pe.wait_ge(S["o_evac"], c * NG + NG)
                for i in range(CT):
                    for g in range(NG):
                        last = turn(bank(i)[:, tok(g)], ot[:, g, tok(i)])
                    last.then_inc(S["oq_ps"], 1)
                for k in range(DK):
                    for i in range(CT):
                        if k == 0:
                            pe.wait_ge(S["at_ready"], c * CT + i + 1)
                        last = turn(bank(4 + k)[:, tok(i)], at[:, i, tok(k)])
                    last.then_inc(S["att_ps"], 1)
                pe.wait_ge(S["att_ready"], c * DK + DK)
                for i in range(CT):
                    acc = bank(6 + i // 2)[:, part(i % 2)]
                    for k in range(DK):
                        mm(acc, att[:, k, tok(i)], wo[:, k], start=(k == 0), stop=False)
                    last = mm(acc, ones[0:1, :], rows[0:1, 2, :], start=False, stop=True)
                    if i % 2:
                        last.then_inc(S["o_ps"], 1)
                pe.wait_ge(S["o_ps"], c * 2 + 2)
                pe.sem_inc(S["chunk_done2"], 1)

            pe.wait_ge(S["chunk_done2"], ENGINES * NC + 1)
            for r in range(4):
                for x in range(4):
                    if r < 2:
                        pe.wait_ge(S["sn_ready"], 4 * r + x + 1)
                    last = turn(bank(r)[:, tok(x)], sn[:, 4 * (r % 2) + x, tok(r // 2)])
                last.then_inc(S["snt_ps"], 1)
            pe.wait_ge(S["snt_ready"], 4)

            def turn_tokens(t):
                pe.wait_ge(S["xn_ready"], t + 1)
                if t >= 2:
                    pe.wait_ge(S["xnt_ready"], t - 1)
                for k in range(DK):
                    last = turn(ps[:, 6 + t % 2, tok(k)], xn[:, t, tok(k)])
                last.then_inc(S["xnt_ps"], 1)

            turn_tokens(0)
            for t in range(TT + 1):
                if t + 1 < TT:
                    turn_tokens(t + 1)
                if t < TT:
                    pe.wait_ge(S["xnt_ready"], t + 1)
                    if t >= 2:
                        pe.wait_ge(S["l_copy"], t - 1)
                    for n in range(2):
                        for k in range(DK):
                            last = mm(bank(2 * (t % 2) + n), xnt[:, t % 2, k], snt[:, k, n * 512:n * 512 + 512],
                                      start=(k == 0), stop=(k == DK - 1))
                    last.then_inc(S["l_ps"], 1)
                if t >= 1:
                    pe.wait_ge(S["l_exp"], t)
                    if t >= 2:
                        pe.wait_ge(S["et_ready"], t - 1)
                    for x in range(NE):
                        last = turn(bank(4 + x // 4)[:, tok(x % 4)], ex[:, (t - 1) % 2, tok(x)])
                    last.then_inc(S["et_ps"], 1)
            pe.wait_ge(S["l_run"], TT)
            pe.wait_ge(S["l_copy"], TT)
            for x in range(NE):
                last = turn(bank(x // 4)[:, tok(x % 4)], mrun[:, tok(x)])
            last.then_inc(S["mt_ps"], 1)
            for n in range(2):
                pe.wait_ge(S["mdiag_ready"], 4 * n + 4)
                mm(bank(2 + n), ones[:, :], mdiag[:, 4 * n:4 * n + 4], start=True, stop=True).then_inc(S["mb_ps"], 1)

            def turn_slots(x):
                pe.wait_ge(S["slot_ready"], x + 1)
                if x >= 2:
                    pe.wait_ge(S["slt_ready"], x - 1)
                for k in range(DK):
                    last = turn(ps[:, 6 + x % 2, tok(k)], slot[:, x % 2, tok(k)])
                last.then_inc(S["slt_ps"], 1)

            pe.wait_ge(S["xnt_ready"], TT)
            pe.wait_ge(S["et_ready"], TT)
            for x in range(NE):
                if x >= 2:
                    pe.wait_ge(S["slot_ready"], x - 1)
                for t in range(TT):
                    if x == 0:
                        pe.wait_ge(S["d_ready"], t + 1)
                    last = mm(ps[:, 4 + x % 2, 0:DM + 1], lg[:, t, tok(x)], xn[:, t, :], start=(t == 0), stop=(t == TT - 1))
                last.then_inc(S["slot_ps"], 1)
                if x >= 1:
                    turn_slots(x - 1)
            turn_slots(NE - 1)
            pe.wait_ge(S["w_b2"], 16)
            for x in range(NE + 1):
                if x < NE:
                    pe.wait_ge(S["slt_ready"], x + 1)
                    pe.wait_ge(w_exp[x % NW], 32 * (x // NW + 1))
                    if x >= 2:
                        pe.wait_ge(S["hid_ready"], FB * (x - 1))
                    for f in range(FB):
                        for k in range(DK):
                            last = mm(ps[:, 2 * (x % 2) + f // 4, tok(f % 4)], mw1[:, x % NW, k, tok(f)], slt[:, x, k],
                                      start=(k == 0), stop=(k == DK - 1))
                        if f % 4 == 3:
                            last.then_inc(S["h_ps"], 1)
                if x >= 1:
                    y = x - 1
                    if y >= 2:
                        pe.wait_ge(S["eo_ready"], y - 1)
                    acc = ps[:, 4 + y % 2, 0:DM]
                    for f in range(FB):
                        pe.wait_ge(S["hid_ready"], FB * y + f + 1)
                        mm(acc, hid[:, y % 2, f], mw2[:, y % NW, f], start=(f == 0), stop=False)
                    mm(acc, ones[0:1, :], b2[0:1, y, :], start=False, stop=True).then_inc(S["eo_ps"], 1)
            for t in range(TT):
                if t >= 8:
                    pe.wait_ge(S["res_ready"], t - 7)
                if t == 0:
                    pe.wait_ge(S["hid_ready"], FB * NE)
                if t == 4:
                    pe.wait_ge(S["eo_ready"], NE)
                for x in range(NE):
                    if t == 0:
                        pe.wait_ge(S["eo_ready"], x + 1)
                    last = mm(ps[:, t % 8, 0:DM], cwt[:, x, tok(t)], eo[:, x], start=(x == 0), stop=(x == NE - 1))
                last.then_inc(S["c_ps"], 1)


def kernel(x, ctx_768, L0_attn_in_proj_w, L0_attn_conv_w, L0_attn_conv_b, L0_attn_x_proj_w, L0_attn_dt_proj_w,
           L0_attn_dt_proj_b, L0_attn_A_log, L0_attn_D, L0_attn_out_proj_w, L0_attn_norm_w, L0_attn_ffn_w1,
           L0_attn_ffn_b1, L0_attn_ffn_w2, L0_attn_ffn_b2, L0_attn_ffn_norm_w, L0_xattn_Wq, L0_xattn_bq,
           L0_xattn_Wk, L0_xattn_bk, L0_xattn_Wv, L0_xattn_bv, L0_xattn_Wo, L0_xattn_bo, L0_ffn_norm_gamma,
           L0_ffn_slot_norm_gamma, L0_ffn_slot_embeds, L0_ffn_w1, L0_ffn_b1, L0_ffn_w2, L0_ffn_b2):
    import numpy as np
    import concourse.bacc as bacc
    from concourse.bass_utils import run_bass_kernel_spmd as run

    def blocks(w, p=P):
        w = np.asarray(w)
        return w.reshape(w.shape[0] // p, p, -1).transpose(1, 0, 2)

    def cols(v):
        return blocks(np.asarray(v).reshape(-1, 1))[:, :, 0]

    def spread(w):
        w = np.asarray(w)
        lead = w.shape[:-1]
        return w.reshape(*lead, DK, HALF, HD).swapaxes(-1, -2).reshape(*lead, DM)

    ins = {
        "x": np.asarray(x)[0],
        "ctx": blocks(np.asarray(ctx_768)[0].T, CP),
        "win": blocks(np.asarray(L0_attn_in_proj_w).T),
        "xproj": blocks(np.asarray(L0_attn_x_proj_w).T),
        "dtw": np.asarray(L0_attn_dt_proj_w).T,
        "wout": blocks(np.asarray(L0_attn_out_proj_w).T),
        "w1": blocks(np.asarray(L0_attn_ffn_w1).T),
        "w2": blocks(np.asarray(L0_attn_ffn_w2).T),
        "wq": blocks(spread(L0_xattn_Wq)),
        "wk": blocks(spread(L0_xattn_Wk), CP),
        "wv": blocks(L0_xattn_Wv, CP),
        "wo": blocks(L0_xattn_Wo),
        "chan": np.concatenate([
            blocks(L0_attn_conv_w).reshape(P, -1), cols(L0_attn_conv_b), cols(L0_attn_dt_proj_b),
            blocks(L0_attn_A_log).reshape(P, -1), cols(L0_attn_D), cols(L0_attn_ffn_b1),
            cols(spread(L0_xattn_bq)), cols(spread(L0_xattn_bk)), cols(np.asarray(L0_ffn_b1).reshape(-1))], axis=1),
        "scales": np.concatenate([np.asarray(v) for v in (L0_attn_norm_w, L0_attn_ffn_norm_w, L0_ffn_norm_gamma,
                                                          L0_ffn_slot_norm_gamma)])[None],
        "rows": np.concatenate([np.asarray(v) for v in (L0_attn_ffn_b2, L0_xattn_bv, L0_xattn_bo)])[None],
        "slots": np.asarray(L0_ffn_slot_embeds).transpose(1, 0, 2),
        "mw1": np.asarray(L0_ffn_w1).reshape(NE, DK, P, FH).transpose(0, 2, 1, 3),
        "mw2": np.asarray(L0_ffn_w2).reshape(NE, FB, P, DM).transpose(0, 2, 1, 3),
        "mb2": np.asarray(L0_ffn_b2).reshape(1, -1),
    }
    nc = bacc.Bacc("TRN2", target_bir_lowering=False, num_devices=1)
    arrays = {"in_" + k: np.ascontiguousarray(v) for k, v in ins.items()}
    args = [nc.dram_tensor(k, v.shape, mybir.dt.from_np(v.dtype), kind="ExternalInput").ap()
            for k, v in arrays.items()]
    out = nc.dram_tensor("out", (T, DM), F32, kind="ExternalOutput").ap()
    scratch = nc.dram_tensor("bc_scratch", (NC, 2 * NS, C), F32, kind="Internal").ap()
    decoder_layer(nc, *args, out, scratch)
    r = run(nc, [arrays], core_ids=[0])
    return r.results[0]["out"].reshape(1, T, DM)
```

```python
from contextlib import ExitStack

import concourse.bass as bass
from concourse import mybir

F32 = mybir.dt.float32
BF16 = mybir.dt.bfloat16
ALU = mybir.AluOpType
ACT = mybir.ActivationFunctionType
AX = mybir.AxisListType.X

P = 128
T = 2048
DM = 256
DK = DM // P
DI = 512
DB = DI // P
NS = 16
RANK = 16
TAPS = 4
FH = 1024
FB = FH // P
NH, HD = 16, 16
KV = 1601
KB = -(-KV // P)
CW = 192
CP = CW // 2
NE, SL = 8, 128
MS = NE * SL
C = 512
NC = T // C
CT = C // P
TT = T // P
G = 4
NG = NH // G
NV = NG * KB
LAST = KV - (KB - 1) * P
PIECES = 2 * CT + DK
HALF = NH // DK
BG = 4
NBG = NS // BG
NW = 4
ARENA = 46250
SMALL = 120.0
ENGINES = 5

TERMS = [(0, 0), (0, 1), (1, 0), (1, 1), (0, 2), (2, 0)]
XR = len(TERMS) * HD
QX_SENT = 16 * DK * len(TERMS)
KCOLS = [(o, min(512, KV - o)) for o in range(0, KV, 512)]

CH = {}
_at = 0
for _n, _w in (("conv_w", DB * TAPS), ("conv_b", DB), ("dt_b", DB), ("a_log", DB * NS), ("skip", DB),
               ("ffn_b1", FB), ("bq", DK), ("bk", DK), ("moe_b1", NE * FB)):
    CH[_n] = (_at, _at + _w)
    _at += _w
CHW = _at


def decoder_layer(nc, x_d, ctx_d, win_d, xproj_d, dtw_d, wout_d, w1_d, w2_d, wq_d, wk_d, wv_d, wo_d,
                  chan_d, scales_d, rows_d, slots_d, mw1_d, mw2_d, mb2_d, out_d, bc_scratch):
    with ExitStack() as ctx:
        def sb(name, shape, dt=F32):
            return ctx.enter_context(nc.sbuf_tensor(name, shape, dt))

        def sem(name):
            return ctx.enter_context(nc.semaphore(name))

        ps = ctx.enter_context(nc.psum_tensor("ps", [P, 8, 512], F32))
        xt = sb("xt", [P, TT, DM])
        ident = sb("ident", [P, P])
        ones = sb("ones", [P, P])
        mhalf = sb("mhalf", [P, TT])
        chan = sb("chan", [P, CHW])
        scales = sb("scales", [P, 4, DM])
        rows = sb("rows", [1, 3, DM])
        stat = sb("stat", [P, TT, 6])
        mv = sb("mv", [P, TT, 2])
        sq = sb("sq", [P, TT])
        ve = sb("ve", [P, TT])
        rstd = sb("rstd", [P, TT])
        ve2 = sb("ve2", [P, TT])
        rstd2 = sb("rstd2", [P, TT])
        mark = sb("mark", [P, 1])
        sel = sb("sel", [P, HALF])
        norm2 = sb("norm2", [P, 2, NH])
        ncol = sb("ncol", [P, 4])
        half = sb("half", [P, 1])
        bound = sb("bound", [P, 4])
        loose = sb("loose", [1, 1], mybir.dt.int32)
        arena = sb("arena", [P, ARENA])

        def ch(name, *dims):
            a, b = CH[name]
            v = chan[:, a:b]
            return v.rearrange("p (a b) -> p a b", b=dims[0]) if dims else v

        class Stack:
            def __init__(self, at=0):
                self.at = at

            def take(self, *shape, dt=F32):
                n = 1
                for s in shape:
                    n *= s
                words = n if dt == F32 else (n + 1) // 2
                v = arena[:, self.at:self.at + words]
                self.at += words
                assert self.at <= ARENA, self.at
                if dt != F32:
                    v = v.bitcast(dt)[:, 0:n]
                if len(shape) == 2:
                    v = v.rearrange("p (a b) -> p a b", b=shape[1])
                if len(shape) == 3:
                    v = v.rearrange("p (a b c) -> p a b c", b=shape[1], c=shape[2])
                if len(shape) == 4:
                    v = v.rearrange("p (a b c d) -> p a b c d", b=shape[1], c=shape[2], d=shape[3])
                return v

        m = Stack()
        win = m.take(DK, 2 * DI)
        xproj = m.take(DB, RANK + 2 * NS)
        dtw = m.take(DI)
        wout = m.take(DB, DM)
        w1 = m.take(DK, FH)
        w2 = m.take(FB, DM)
        neg_a = m.take(DB, NS)
        diag_skip = m.take(DB, P)
        carry = m.take(DB, NS)
        hist = m.take(DB, TAPS - 1)
        a0 = m.take(CT, DM)
        u = m.take(DB, C)
        zs = m.take(DB, C)
        xdbl = m.take(C)
        delta = m.take(DB, C)
        du = m.take(DB, C)
        bg = m.take(2, BG, C)
        cg = m.take(2, BG, C)
        region = m.at
        da = m.take(2, DB, C)
        dbu = m.take(2, DB, C)
        hs = m.take(2, DB, C)
        hc = m.take(2, DB, C)
        m2 = Stack(region)
        a0t = m2.take(DK, C)
        conv = m2.take(DB, C)
        upad = m2.take(DB, TAPS - 1 + C)
        sp_abs = m2.take(DB, C)
        sp_exp = m2.take(DB, C)
        sp_ln = m2.take(DB, C)
        sp_cor = m2.take(DB, C)
        m3 = Stack(region)
        yz = m3.take(DB, C)
        gate = m3.take(FB, C)
        hsum = m3.take(CT, DM)
        h1 = m3.take(CT, DM)
        h1t = m3.take(DK, C)
        rsum = m3.take(CT, DM)
        rnorm = m3.take(CT, DM)
        junk = m3.take(CT, DM)
        junk2 = m3.take(CT, DM)
        assert max(m2.at, m3.at) <= m.at

        a = Stack()
        kx = a.take(NH, KV, dt=BF16)
        qx_at = a.at
        qx = a.take(NH, T, dt=BF16)
        vx = a.take(KB, NH, 2 * HD)
        wq = a.take(DK, DM)
        wo = a.take(DK, DM)
        region = a.at
        a1 = Stack(qx_at)
        ctxt = a1.take(2, KV)
        wk = a1.take(2, DM)
        wv = a1.take(2, DM)
        kf = a1.take(DK, KV)
        kp = [a1.take(DK, KV, dt=BF16) for _ in range(3)]
        ksq = a1.take(DK, KV)
        assert a1.at <= qx_at + NH * T // 2
        a2 = Stack(region)
        xa = a2.take(2, CT, DM)
        xat = a2.take(2, DK, C)
        qf = a2.take(2, DK, C)
        qp = [a2.take(2, DK * C, dt=BF16) for _ in range(3)]
        a3 = Stack(region)
        prob = a3.take(2, G, C)
        ot = a3.take(NG, C)
        at = a3.take(CT, DM)
        att = a3.take(DK, C)
        orec = a3.take(CT, NH)
        a4 = Stack(region)
        nmax = a4.take(NH)
        nrow = a4.take(P, dt=BF16)

        e1 = Stack()
        lg = e1.take(TT, MS)
        cwt = e1.take(NE, T)
        xn = e1.take(TT, DM + 1)
        region = e1.at
        snt = e1.take(DK, MS)
        ex = e1.take(2, MS)
        xnt = e1.take(2, DK, P)
        mrun = e1.take(MS)
        mdiag = e1.take(NE, P)
        junk3 = e1.take(DM)
        e2 = Stack(region)
        slot = e2.take(2, DM)
        slt = e2.take(NE, DK, P)
        hid = e2.take(2, FB, P)
        eo = e2.take(NE, DM)
        b2 = e2.take(NE, DM)
        mcol = sb("mcol", [P, NE])
        srec = sb("srec", [P, NE])
        sqs = sb("sqs", [P, NE])
        nmx = sb("nmx", [P, TT])
        csum = sb("csum", [P, TT])
        crec = sb("crec", [P, TT])
        e3 = Stack()
        se = e3.take(NE, DM)
        sn = e3.take(NE, DM)
        junk4 = e3.take(NE, DM)
        e4 = Stack()
        mw1 = e4.take(NW, DK, FH)
        mw2 = e4.take(NW, FB, DM)
        assert e4.at <= TT * MS

        S = {name: sem(name) for name in """
            w_mamba x_in consts prep_act prep_dve chunk_done1
            mark1 st1 mv1 ve1 rs1 a0_ready a0t_ps a0t_ready proj_ps u_raw z_ready hist_in conv_step  u_ready
            xdbl_ps xdbl_ready bc_stored bc_even bc_odd dt_ps sp_in sp_act relu_ready sp_step delta_ready
            du_ready da_ready dbu_ready scan_done carry_done hc_ready y_acc y_ready
            yz_ready op_ps hsum_ready ss1 ms1 rms1 h1_ready h1t_ps h1t_ready ff1_ps g_ready ff2_ps
            r_ready ss2 ms2 rms2 rn_ready x1_ready
            w_attn  k_ps kf_ready kp_ready ksq_ready kr_ready kx_in v_ps vx_ready vx_init sel_ready
            st2  ve3 rs3 xa_ready xat_ps xat_ready q_ps qf_ready qp_ready qsq_ready qr_ready qx_even qx_odd
            kn_ps qn_ps     bound_step  root_ready bound_ready bound_ps  
            ms_ps nm_ready nt_ps nrow_ready shift_in s_ps p_ready pv_done o_evac oq_ps orec_ready at_ready
            att_ps att_ready o_ps x2_ready
            w_slots ss4 ms4 rms4 sn_ready snt_ps snt_ready
            st5  ve5 rs5 y_normed ss5 ms5 rms5 xn_ready xn_one xnt_ps xnt_ready l_ps l_copy l_max l_run
            l_exp et_ps et_ready mt_ps mcol_ready mdiag_ready mb_ps l_sub d_ready
            slot_ps srec_ready slot_ready slt_ps slt_ready w_exp0 w_exp1 w_exp2 w_exp3 w_b2
            h_ps hid_ready eo_ps eo_ready c_ps crec_ready res_ready out_done""".split()}
        w_exp = [S["w_exp0"], S["w_exp1"], S["w_exp2"], S["w_exp3"]]
        qx_in = [S["qx_even"], S["qx_odd"]]
        bc_in = [S["bc_even"], S["bc_odd"]]

        def flat(v):
            return v.rearrange("p a b -> p (a b)")

        def over(v, n):
            return v.unsqueeze(1).to_broadcast([v.shape[0], n, v.shape[1]])

        def bank(n):
            return ps[:, n, :]

        def banks(n, k):
            return ps[:, n:n + k, :].rearrange("p a b -> p (a b)")

        def tok(n):
            return slice(n * P, n * P + P)

        def part(n):
            return slice(n * DM, n * DM + DM)

        block = ctx.enter_context(nc.Block())

        @block.sync
        def _(sp):
            sp.dma_start(xt[:, :, :], x_d.rearrange("(t p) d -> p t d", p=P)).then_inc(S["x_in"], 16)
            for dst, src in ((chan[:, :], chan_d), (win, win_d), (xproj, xproj_d), (dtw[0:RANK, :], dtw_d),
                             (wout, wout_d), (w1, w1_d), (w2, w2_d),
                             (flat(scales[:, :, :]), scales_d.to_broadcast([P, 4 * DM])),
                             (flat(rows[:, :, :]), rows_d)):
                sp.dma_start(dst, src).then_inc(S["w_mamba"], 16)

            with sp.Fori(0, NC) as c:
                sp.wait_ge(S["xdbl_ready"], c + 1)
                sp.dma_start(bc_scratch[bass.ds(c, 1), :, :].rearrange("o n t -> (o n) t"),
                             xdbl[RANK:RANK + 2 * NS, :]).then_inc(S["bc_stored"], 16)
                sp.wait_ge(S["bc_stored"], c * 16 + 16)
                for q in range(NBG):
                    if q >= 2:
                        sp.wait_ge(S["dbu_ready"], c * NS + BG * (q - 1))
                        sp.wait_ge(S["hc_ready"], c * NS + BG * (q - 1))
                    for dst, n in ((bg, q * BG), (cg, NS + q * BG)):
                        row = bc_scratch[bass.ds(c, 1), n:n + BG, :].rearrange("o n t -> o (n t)")
                        sp.dma_start(flat(dst[:, q % 2]), row.to_broadcast([P, BG * C])).then_inc(bc_in[q % 2], 16)
                sp.sem_inc(S["chunk_done1"], 1)

            sp.wait_ge(S["chunk_done1"], ENGINES * NC + 1)
            sp.dma_start(ctxt[0:CP], ctx_d).then_inc(S["w_attn"], 16)
            for dst, src in ((wk[0:CP], wk_d), (wv[0:CP], wv_d), (wq, wq_d), (wo, wo_d)):
                sp.dma_start(dst, src).then_inc(S["w_attn"], 16)
            for n in range(3):
                sp.wait_ge(S["kp_ready"], n + 1)
                for j, (_, b) in enumerate(TERMS):
                    if b == n:
                        for k in range(DK):
                            sp.dma_start(kx[HD * j:HD * j + HD, HALF * k:HALF * k + HALF, :],
                                         kp[n][:, k, :]).then_inc(S["kx_in"], 16)
            sp.wait_ge(S["kx_in"], 16 * DK * len(TERMS))
            sp.wait_ge(S["kn_ps"], 1)
            for c in range(NC):
                for n in range(3):
                    sp.wait_ge(S["qp_ready"], c * 3 + n + 1)
                    for j, (b, _) in enumerate(TERMS):
                        if b == n:
                            for k in range(DK):
                                sp.dma_start(qx[HD * j:HD * j + HD, HALF * k:HALF * k + HALF, c * C:c * C + C],
                                             qp[n][:, c % 2, k * C:k * C + C]).then_inc(qx_in[c % 2], 16)
            sp.wait_ge(S["bound_ready"], 1)
            with sp.If(sp.value_load(loose[0:1, 0:1], min_val=0, max_val=1) > 0):
                sp.wait_ge(S["vx_init"], 4)
                with sp.Fori(0, TT) as t:
                    sp.wait_ge(S["nrow_ready"], t + 1)
                    sp.dma_start(qx[XR:XR + 1, :, bass.ds(t * P, P)], nrow[0:NH, :]).then_inc(S["shift_in"], 16)

            sp.wait_ge(S["x2_ready"], 2 * NC)
            sp.dma_start(se, slots_d).then_inc(S["w_slots"], 16)
            sp.wait_ge(S["mb_ps"], 2)
            sp.wait_ge(S["et_ready"], TT)
            sp.dma_start(flat(b2[0:1]), mb2_d).then_inc(S["w_b2"], 16)
            for x in range(NE):
                if x < NW:
                    sp.wait_ge(S["slot_ps"], NE)
                else:
                    sp.wait_ge(S["eo_ps"], x - NW + 1)
                sp.dma_start(mw1[:, x % NW], mw1_d[x]).then_inc(w_exp[x % NW], 16)
                sp.dma_start(mw2[:, x % NW], mw2_d[x]).then_inc(w_exp[x % NW], 16)
            for t in range(0, TT, CT):
                sp.wait_ge(S["res_ready"], t + CT)
                sp.dma_start(out_d[t * P:(t + CT) * P, :].rearrange("(t p) d -> p t d", p=P),
                             xt[:, t:t + CT, :]).then_inc(S["out_done"], 16)
            sp.wait_ge(S["out_done"], 16 * (TT // CT))

        @block.gpsimd
        def _(pool):
            pool.memset(ident[:, :], 0.0).then_inc(S["consts"], 1)
            pool.memset(ones[:, :], 1.0).then_inc(S["consts"], 1)
            pool.memset(mhalf[:, :], -0.5).then_inc(S["consts"], 1)
            pool.memset(flat(carry), 0.0).then_inc(S["consts"], 1)
            pool.memset(flat(hist), 0.0).then_inc(S["consts"], 1)
            pool.wait_ge(S["consts"], 1)
            pool.affine_select(out=ident[:, :], in_=ident[:, :], compare_op=ALU.not_equal, fill=1.0, base=0,
                               pattern=[[-1, P]], channel_multiplier=1).then_inc(S["consts"], 1)

            def rsqrt(dst, src, n):
                return pool.tensor_tensor(dst[:, 0:n], src[:, 0:n], mhalf[:, 0:n], ALU.pow)

            pool.wait_ge(S["consts"], 6)
            with pool.Fori(0, NC) as c:
                pool.wait_ge(S["ve1"], c + 1)
                rsqrt(rstd, ve, CT).then_inc(S["rs1"], 1)
                for n in range(NS):
                    q = n // BG
                    if n == 0:
                        pool.wait_ge(S["du_ready"], c + 1)
                    if n % BG == 0:
                        pool.wait_ge(bc_in[q % 2], c * 64 + 32 * (q // 2 + 1))
                    if n >= 2:
                        pool.wait_ge(S["scan_done"], c * NS * DB + DB * (n - 1))
                    pool.tensor_tensor(dbu[:, n % 2], du, over(bg[:, q % 2, n % BG], DB),
                                       ALU.mult).then_inc(S["dbu_ready"], 1)
                pool.wait_ge(S["ms1"], c + 1)
                rsqrt(rstd2, ve2, CT).then_inc(S["rms1"], 1)
                pool.wait_ge(S["ms2"], c + 1)
                rsqrt(rstd, ve, CT).then_inc(S["rms2"], 1)
                pool.wait_ge(S["rms2"], c + 1)
                pool.sem_inc(S["chunk_done1"], 1)

            pool.wait_ge(S["chunk_done1"], ENGINES * NC + 1)
            pool.wait_ge(S["ve3"], 1)
            rsqrt(rstd, ve, TT).then_inc(S["rs3"], 1)
            pool.memset(vx, 0.0).then_inc(S["vx_init"], 1)
            pool.wait_ge(S["vx_init"], 1)
            pool.memset(vx[:, :, :, HD:HD + 1], 1.0).then_inc(S["vx_init"], 1)
            pool.wait_ge(S["vx_init"], 2)
            pool.memset(kx[XR:XR + 1, :, :], 1.0).then_inc(S["vx_init"], 1)
            pool.wait_ge(S["vx_init"], 3)
            pool.memset(half[:, :], 0.5).then_inc(S["consts"], 1)
            pool.wait_ge(S["consts"], 7)
            pool.wait_ge(S["kx_in"], 16 * DK * len(TERMS))
            pool.wait_ge(S["kn_ps"], 1)
            pool.memset(arena[XR:XR + 1, qx_at:qx_at + NH * T // 2], 0.0).then_inc(S["vx_init"], 1)
            pool.wait_ge(S["vx_init"], 4)
            pool.wait_ge(S["bound_step"], 7)
            pool.tensor_tensor(bound[:, 1:2], bound[:, 0:1], half[:, :], ALU.pow).then_inc(S["root_ready"], 1)

            pool.wait_ge(S["ms4"], 1)
            rsqrt(rstd2, ve2, NE).then_inc(S["rms4"], 1)
            pool.wait_ge(S["ve5"], 1)
            rsqrt(rstd, ve, TT).then_inc(S["rs5"], 1)
            pool.wait_ge(S["ms5"], 1)
            rsqrt(rstd2, ve2, TT).then_inc(S["rms5"], 1)

        @block.scalar
        def _(act):
            act.wait_ge(S["w_mamba"], 16 * 9)
            act.activation(flat(neg_a), ch("a_log"), ACT.Exp).then_inc(S["prep_act"], 1)

            with act.Fori(0, NC) as c:
                for k in range(DK):
                    act.wait_ge(S["a0t_ps"], c * DK + k + 1)
                    act.activation(a0t[:, k], bank(k), ACT.Copy).then_inc(S["a0t_ready"], 1)
                for d in range(DB):
                    act.wait_ge(S["proj_ps"], c * 2 * DB + DB + d + 1)
                    act.activation(zs[:, d], bank(2 + (DB + d) % 6), ACT.Silu).then_inc(S["z_ready"], 1)
                for d in range(DB):
                    act.wait_ge(S["conv_step"], c * TAPS * DB + (TAPS - 1) * DB + d + 1)
                    act.activation(u[:, d], conv[:, d], ACT.Silu).then_inc(S["u_ready"], 1)
                act.wait_ge(S["sp_in"], c * DB + DB)
                act.activation(flat(sp_abs), flat(delta), ACT.Abs).then_inc(S["sp_act"], 1)
                act.wait_ge(S["sp_act"], c * 3 + 1)
                act.activation(flat(sp_exp), flat(sp_abs), ACT.Exp, scale=-1.0).then_inc(S["sp_act"], 1)
                act.wait_ge(S["sp_act"], c * 3 + 2)
                act.activation(flat(sp_ln), flat(sp_exp), ACT.Ln, bias=1.0).then_inc(S["sp_act"], 1)

                def carry_over(n):
                    act.wait_ge(S["scan_done"], c * NS * DB + DB * (n + 1))
                    act.activation(carry[:, :, n:n + 1], hs[:, n % 2, :, C - 1:C], ACT.Copy).then_inc(S["carry_done"], 1)

                act.wait_ge(S["prep_dve"], 1 + DB)
                for n in range(NS):
                    if n == 0:
                        act.wait_ge(S["delta_ready"], c + 1)
                    if n >= 2:
                        act.wait_ge(S["scan_done"], c * NS * DB + DB * (n - 1))
                    for d in range(DB):
                        act.activation(da[:, n % 2, d], delta[:, d], ACT.Exp,
                                       scale=neg_a[:, d, n:n + 1]).then_inc(S["da_ready"], 1)
                    if n >= 1:
                        carry_over(n - 1)
                carry_over(NS - 1)
                act.wait_ge(S["carry_done"], c * NS + NS)

                for i in range(CT):
                    act.wait_ge(S["hsum_ready"], c * 2 + i // 2 + 1)
                    act.activation(junk[:, i], hsum[:, i], ACT.Square, accum_out=sq[:, i:i + 1]).then_inc(S["ss1"], 1)
                for k in range(DK):
                    act.wait_ge(S["h1t_ps"], c * DK + k + 1)
                    act.activation(h1t[:, k], bank(6 + k), ACT.Copy).then_inc(S["h1t_ready"], 1)
                for f in range(FB):
                    act.wait_ge(S["ff1_ps"], c * FB + f + 1)
                    act.activation(gate[:, f], bank(f % 4), ACT.Gelu,
                                   bias=ch("ffn_b1")[:, f:f + 1]).then_inc(S["g_ready"], 1)
                act.wait_ge(S["ms1"], c + 1)
                for i in range(CT):
                    act.wait_ge(S["r_ready"], c * 2 + i // 2 + 1)
                    act.activation(junk2[:, i], rsum[:, i], ACT.Square, accum_out=sq[:, i:i + 1]).then_inc(S["ss2"], 1)
                act.wait_ge(S["ss2"], c * CT + CT)
                act.sem_inc(S["chunk_done1"], 1)

            act.wait_ge(S["kf_ready"], DK * len(KCOLS))
            act.activation(flat(kp[0]), flat(kf), ACT.Copy).then_inc(S["kp_ready"], 1)
            act.activation(flat(ksq), flat(kf), ACT.Square).then_inc(S["ksq_ready"], 1)

            def v_blocks(first, last):
                for b in range(first, last, 2):
                    nb, n = min(2, KB - b), min(P, KV - b * P)
                    act.wait_ge(S["v_ps"], b // 2 + 1)
                    act.activation(vx[0:n, b:b + nb, :, 0:HD],
                                   ps[0:n, b // 2, 0:nb * DM].rearrange("p (b h d) -> p b h d", b=nb, d=HD),
                                   ACT.Copy).then_inc(S["vx_ready"], 1)

            act.wait_ge(S["vx_init"], 2)
            v_blocks(0, 6)
            act.wait_ge(S["kr_ready"], 1)
            act.activation(flat(kp[1]), flat(kf), ACT.Copy).then_inc(S["kp_ready"], 1)
            v_blocks(6, KB)
            act.wait_ge(S["kr_ready"], 2)
            act.activation(flat(kp[2]), flat(kf), ACT.Copy).then_inc(S["kp_ready"], 1)

            def q_input(c):
                for k in range(DK):
                    act.wait_ge(S["xat_ps"], c * DK + k + 1)
                    if c >= 2:
                        act.wait_ge(S["qn_ps"], c - 1)
                    act.activation(xat[:, c % 2, k], bank(k), ACT.Copy).then_inc(S["xat_ready"], 1)

            q_input(0)
            for c in range(NC):
                act.wait_ge(S["qf_ready"], c * DK + DK)
                if c >= 2:
                    act.wait_ge(qx_in[c % 2], c // 2 * QX_SENT)
                act.activation(qp[0][:, c % 2], flat(qf[:, c % 2]), ACT.Copy).then_inc(S["qp_ready"], 1)
                act.activation(flat(xat[:, c % 2]), flat(qf[:, c % 2]), ACT.Square).then_inc(S["qsq_ready"], 1)
                if c + 1 < NC:
                    q_input(c + 1)
                for n in range(1, 3):
                    act.wait_ge(S["qr_ready"], c * 2 + n)
                    act.activation(qp[n][:, c % 2], flat(qf[:, c % 2]), ACT.Copy).then_inc(S["qp_ready"], 1)

            def probabilities(c, first=False):
                for v in range(NV):
                    n = min(P, KV - v % KB * P)
                    if v >= 2 or not first:
                        act.wait_ge(S["pv_done"], c * NV + v - 1)
                    for h in range(2):
                        r = 2 * v + h
                        act.wait_ge(S["s_ps"], c * 2 * NV + r + 1)
                        act.activation(flat(prob[0:n, v % 2, 2 * h:2 * h + 2]),
                                       ps[0:n, 2 * h:2 * h + 2, :].rearrange("p a b -> p (a b)"),
                                       ACT.Exp, bias=bound[0:n, 3:4], scale=HD ** -0.5).then_inc(S["p_ready"], 1)

            act.wait_ge(S["bound_ready"], 2)
            probabilities(0, first=True)
            with act.Fori(1, NC) as c:
                probabilities(c)

            act.wait_ge(S["w_slots"], 16)
            for x in range(NE):
                act.activation(junk4[:, x], se[:, x], ACT.Square, accum_out=sqs[:, x:x + 1]).then_inc(S["ss4"], 1)
            for r in range(4):
                act.wait_ge(S["snt_ps"], r + 1)
                act.activation(snt[:, r // 2, r % 2 * 512:r % 2 * 512 + 512], bank(r), ACT.Copy).then_inc(S["snt_ready"], 1)
            for t in range(TT):
                act.wait_ge(S["y_normed"], t + 1)
                if t >= 1:
                    act.wait_ge(S["ss5"], t)
                act.activation(junk3, xn[:, t, 0:DM], ACT.Square, accum_out=sq[:, t:t + 1]).then_inc(S["ss5"], 1)

            def turned(t):
                act.wait_ge(S["et_ps"], t + 1)
                act.activation(cwt[:, :, tok(t)], banks(4, 2).rearrange("p (e n) -> p e n", n=P),
                               ACT.Copy).then_inc(S["et_ready"], 1)

            def combine_weights(t):
                act.wait_ge(S["l_max"], t + 1)
                if t >= 2:
                    act.wait_ge(S["et_ps"], t - 1)
                act.activation(ex[:, t % 2], lg[:, t], ACT.Exp, bias=nmx[:, t:t + 1],
                               accum_out=csum[:, t:t + 1]).then_inc(S["l_exp"], 1)

            for t in range(TT + 2):
                if t < TT:
                    act.wait_ge(S["xnt_ps"], t + 1)
                    if t >= 2:
                        act.wait_ge(S["l_ps"], t - 1)
                    act.activation(flat(xnt[:, t % 2]), ps[:, 6 + t % 2, 0:DK * P], ACT.Copy).then_inc(S["xnt_ready"], 1)
                    act.wait_ge(S["l_ps"], t + 1)
                    act.activation(lg[:, t], banks(2 * (t % 2), 2), ACT.Copy).then_inc(S["l_copy"], 1)
                if 1 <= t <= TT:
                    combine_weights(t - 1)
                if t >= 2:
                    turned(t - 2)
            for t in range(TT):
                act.wait_ge(S["l_sub"], t + 1)
                act.activation(lg[:, t], lg[:, t], ACT.Exp).then_inc(S["d_ready"], 1)
            for x in range(NE):
                act.wait_ge(S["slt_ps"], x + 1)
                act.activation(flat(slt[:, x]), ps[:, 6 + x % 2, 0:DK * P], ACT.Copy).then_inc(S["slt_ready"], 1)
            for x in range(NE):
                if x >= 2:
                    act.wait_ge(S["eo_ps"], x - 1)
                for f in range(FB):
                    if f % 4 == 0:
                        act.wait_ge(S["h_ps"], 2 * x + f // 4 + 1)
                    act.activation(hid[:, x % 2, f], ps[:, 2 * (x % 2) + f // 4, tok(f % 4)], ACT.Gelu,
                                   bias=ch("moe_b1")[:, x * FB + f:x * FB + f + 1]).then_inc(S["hid_ready"], 1)

        @block.vector
        def _(dve):
            dve.wait_ge(S["prep_act"], 1)
            dve.tensor_scalar(flat(neg_a), flat(neg_a), -1.0, None, ALU.mult).then_inc(S["prep_dve"], 1)
            dve.wait_ge(S["consts"], 6)
            for d in range(DB):
                dve.tensor_scalar(diag_skip[:, d], ident[:, :], ch("skip")[:, d:d + 1], None,
                                  ALU.mult).then_inc(S["prep_dve"], 1)
            dve.wait_ge(S["x_in"], 16)
            dve.sem_inc(S["chunk_done1"], 1)

            def xtile(t, n=1):
                v = xt[:, bass.ds(t, n), :]
                return flat(v) if n == 1 else v

            conv_w = ch("conv_w", TAPS)
            with dve.Fori(0, NC) as c:
                dve.wait_ge(S["chunk_done1"], c * ENGINES + 1)
                dve.tensor_copy(upad[:, :, 0:TAPS - 1], hist).then_inc(S["hist_in"], 1)
                for i in range(CT):
                    dve.bn_stats(stat[:, i, :], xtile(c * CT + i)).then_inc(S["st1"], 1)
                dve.wait_ge(S["st1"], c * CT + CT)
                dve.memset(mark[:, :], 0.0).then_inc(S["mark1"], 1)
                for i in range(CT):
                    dve.bn_aggr(mv[:, i, :], stat[:, i, :]).then_inc(S["mv1"], 1)
                dve.wait_ge(S["mv1"], c * CT + CT)
                dve.tensor_scalar(ve[:, 0:CT], mv[:, 0:CT, 1], 1e-5, None, ALU.add).then_inc(S["ve1"], 1)
                dve.wait_ge(S["rs1"], c + 1)
                for i in range(CT):
                    dve.tensor_scalar(a0[:, i], xtile(c * CT + i), mv[:, i, 0:1], rstd[:, i:i + 1],
                                      ALU.subtract, ALU.mult).then_inc(S["a0_ready"], 1)
                for d in range(DB):
                    dve.wait_ge(S["proj_ps"], c * 2 * DB + d + 1)
                    dve.tensor_copy(upad[:, d, TAPS - 1:TAPS - 1 + C], bank(2 + d)).then_inc(S["u_raw"], 1)
                dve.wait_ge(S["hist_in"], c + 1)
                for step, j in enumerate(reversed(range(TAPS))):
                    for d in range(DB):
                        if step == 0:
                            dve.wait_ge(S["u_raw"], c * DB + d + 1)
                            dve.tensor_scalar(conv[:, d], upad[:, d, j:j + C], conv_w[:, d, j:j + 1],
                                              ch("conv_b")[:, d:d + 1], ALU.mult, ALU.add).then_inc(S["conv_step"], 1)
                        else:
                            dve.wait_ge(S["conv_step"], c * TAPS * DB + (step - 1) * DB + d + 1)
                            dve.scalar_tensor_tensor(conv[:, d], upad[:, d, j:j + C], conv_w[:, d, j:j + 1],
                                                     conv[:, d], ALU.mult, ALU.add).then_inc(S["conv_step"], 1)
                dve.tensor_copy(hist, upad[:, :, C:C + TAPS - 1])
                dve.wait_ge(S["xdbl_ps"], c + 1)
                dve.tensor_copy(xdbl[0:RANK + 2 * NS, :], ps[0:RANK + 2 * NS, 0, :]).then_inc(S["xdbl_ready"], 1)
                for d in range(DB):
                    dve.wait_ge(S["dt_ps"], c * DB + d + 1)
                    dve.tensor_scalar(delta[:, d], bank(4 + d), ch("dt_b")[:, d:d + 1], None,
                                      ALU.add).then_inc(S["sp_in"], 1)
                dve.wait_ge(S["sp_in"], c * DB + DB)
                dve.wait_ge(S["sp_act"], c * 3 + 1)
                dve.tensor_scalar(flat(delta), flat(delta), 0.0, None, ALU.max).then_inc(S["relu_ready"], 1)
                dve.wait_ge(S["sp_act"], c * 3 + 2)
                dve.tensor_scalar(flat(sp_cor), flat(sp_exp), 1.0, 1.0, ALU.add, ALU.subtract).then_inc(S["sp_step"], 1)
                dve.wait_ge(S["sp_step"], c * 3 + 1)
                dve.tensor_tensor(flat(sp_cor), flat(sp_exp), flat(sp_cor), ALU.subtract).then_inc(S["sp_step"], 1)
                dve.wait_ge(S["sp_act"], c * 3 + 3)
                dve.wait_ge(S["sp_step"], c * 3 + 2)
                dve.tensor_tensor(flat(sp_cor), flat(sp_cor), flat(sp_ln), ALU.add).then_inc(S["sp_step"], 1)
                dve.wait_ge(S["relu_ready"], c + 1)
                dve.wait_ge(S["sp_step"], c * 3 + 3)
                dve.tensor_tensor(flat(delta), flat(delta), flat(sp_cor), ALU.add).then_inc(S["delta_ready"], 1)
                dve.wait_ge(S["delta_ready"], c + 1)
                dve.wait_ge(S["u_ready"], c * DB + DB)
                dve.tensor_tensor(flat(du), flat(delta), flat(u), ALU.mult).then_inc(S["du_ready"], 1)

                for n in range(NS + 1):
                    if n < NS:
                        dve.wait_ge(S["dbu_ready"], c * NS + n + 1)
                        if n >= 2:
                            dve.wait_ge(S["hc_ready"], c * NS + n - 1)
                            dve.wait_ge(S["carry_done"], c * NS + n - 1)
                        for d in range(DB):
                            dve.wait_ge(S["da_ready"], c * NS * DB + n * DB + d + 1)
                            dve.tensor_tensor_scan(hs[:, n % 2, d], da[:, n % 2, d], dbu[:, n % 2, d],
                                                   carry[:, d, n:n + 1], ALU.mult, ALU.add).then_inc(S["scan_done"], 1)
                    if n >= 1:
                        k, q = n - 1, (n - 1) // BG
                        if k % BG == 0:
                            dve.wait_ge(bc_in[q % 2], c * 64 + 32 * (q // 2 + 1))
                        if k >= 2:
                            dve.wait_ge(S["y_acc"], c * NS + k - 1)
                        dve.wait_ge(S["scan_done"], c * NS * DB + n * DB)
                        dve.tensor_tensor(hc[:, k % 2], hs[:, k % 2], over(cg[:, q % 2, k % BG], DB),
                                          ALU.mult).then_inc(S["hc_ready"], 1)

                dve.wait_ge(S["y_ready"], c + 1)
                dve.wait_ge(S["z_ready"], c * DB + DB)
                dve.tensor_tensor(flat(yz), banks(0, DB), flat(zs), ALU.mult).then_inc(S["yz_ready"], 1)
                for b in range(2):
                    dve.wait_ge(S["op_ps"], c * 2 + b + 1)
                    dve.tensor_tensor(flat(hsum[:, 2 * b:2 * b + 2]), bank(4 + b), flat(a0[:, 2 * b:2 * b + 2]),
                                      ALU.add).then_inc(S["hsum_ready"], 1)
                dve.wait_ge(S["ss1"], c * CT + CT)
                dve.tensor_scalar(ve2[:, 0:CT], sq[:, 0:CT], 1.0 / DM, 1e-12, ALU.mult, ALU.add).then_inc(S["ms1"], 1)
                dve.wait_ge(S["hsum_ready"], c * 2 + 2)
                dve.wait_ge(S["rms1"], c + 1)
                for i in range(CT):
                    dve.scalar_tensor_tensor(h1[:, i], hsum[:, i], rstd2[:, i:i + 1], scales[:, 0, :],
                                             ALU.mult, ALU.mult).then_inc(S["h1_ready"], 1)
                dve.wait_ge(S["h1_ready"], c * CT + CT)
                for b in range(2):
                    dve.wait_ge(S["ff2_ps"], c * 2 + b + 1)
                    dve.tensor_tensor(flat(rsum[:, 2 * b:2 * b + 2]), bank(4 + b), flat(h1[:, 2 * b:2 * b + 2]),
                                      ALU.add).then_inc(S["r_ready"], 1)
                dve.wait_ge(S["ss2"], c * CT + CT)
                dve.tensor_scalar(ve[:, 0:CT], sq[:, 0:CT], 1.0 / DM, 1e-12, ALU.mult, ALU.add).then_inc(S["ms2"], 1)
                dve.wait_ge(S["r_ready"], c * 2 + 2)
                dve.wait_ge(S["rms2"], c + 1)
                for i in range(CT):
                    dve.scalar_tensor_tensor(rnorm[:, i], rsum[:, i], rstd[:, i:i + 1], scales[:, 1, :],
                                             ALU.mult, ALU.mult).then_inc(S["rn_ready"], 1)
                dve.wait_ge(S["rn_ready"], c * CT + CT)
                dve.tensor_tensor(xtile(c * CT, CT), xtile(c * CT, CT), rnorm, ALU.add).then_inc(S["x1_ready"], 1)
                dve.wait_ge(S["x1_ready"], c + 1)
                dve.sem_inc(S["chunk_done1"], 1)

            for t in range(TT):
                dve.bn_stats(stat[:, t, :], xt[:, t, :]).then_inc(S["st2"], 1)
            for t in range(TT):
                dve.wait_ge(S["st2"], t + 1)
                dve.bn_aggr(mv[:, t, :], stat[:, t, :]).then_inc(S["st2"], 1)
            dve.wait_ge(S["st2"], 2 * TT)
            dve.tensor_scalar(ve[:, :], mv[:, :, 1], 1e-5, None, ALU.add).then_inc(S["ve3"], 1)
            dve.tensor_reduce(sel[:, :], ident.rearrange("p (d m) -> p m d", m=HALF), AX, ALU.add).then_inc(S["sel_ready"], 1)
            for k in range(DK):
                for j, (o, w) in enumerate(KCOLS):
                    dve.wait_ge(S["k_ps"], k * len(KCOLS) + j + 1)
                    dve.tensor_scalar(kf[:, k, o:o + w], ps[:, 4 * k + j, 0:w], ch("bk")[:, k:k + 1], None,
                                      ALU.add).then_inc(S["kf_ready"], 1)

            def normed(c):
                for i in range(CT):
                    t = c * CT + i
                    if c >= 2:
                        dve.wait_ge(S["xat_ps"], (c - 1) * DK)
                    dve.tensor_scalar(xa[:, c % 2, i], xt[:, t, :], mv[:, t, 0:1], rstd[:, t:t + 1],
                                      ALU.subtract, ALU.mult).then_inc(S["xa_ready"], 1)

            dve.wait_ge(S["rs3"], 1)
            normed(0)
            dve.wait_ge(S["kf_ready"], DK * len(KCOLS))
            dve.wait_ge(S["ksq_ready"], 1)
            for n in range(2):
                dve.wait_ge(S["kp_ready"], n + 1)
                if n:
                    dve.wait_ge(S["kr_ready"], n)
                dve.tensor_tensor(flat(kf), flat(kf), flat(kp[n]), ALU.subtract).then_inc(S["kr_ready"], 1)
                normed(n + 1)
            for c in range(NC):
                for k in range(DK):
                    dve.wait_ge(S["q_ps"], c * DK + k + 1)
                    if c >= 2:
                        dve.wait_ge(S["qp_ready"], 3 * (c - 1))
                    dve.tensor_scalar(qf[:, c % 2, k], bank(2 + 2 * (c % 2) + k), ch("bq")[:, k:k + 1], None,
                                      ALU.add).then_inc(S["qf_ready"], 1)
                dve.wait_ge(S["qf_ready"], c * DK + DK)
                for n in range(2):
                    dve.wait_ge(S["qp_ready"], c * 3 + n + 1)
                    if n:
                        dve.wait_ge(S["qr_ready"], c * 2 + n)
                    else:
                        dve.wait_ge(S["qsq_ready"], c + 1)
                    dve.tensor_tensor(flat(qf[:, c % 2]), flat(qf[:, c % 2]), qp[n][:, c % 2],
                                      ALU.subtract).then_inc(S["qr_ready"], 1)
                if c == 0:
                    normed(3)
                if c == 1:
                    dve.wait_ge(S["kn_ps"], 1)
                    dve.tensor_reduce(norm2[:, 0, :], ps[:, 6, 0:(KB - 1) * NH].rearrange("p (b h) -> p h b", h=NH),
                                      AX, ALU.max).then_inc(S["bound_step"], 1)
                    dve.wait_ge(S["bound_step"], 1)
                    dve.tensor_tensor(norm2[0:LAST, 0, :], norm2[0:LAST, 0, :], ps[0:LAST, 6, (KB - 1) * NH:KB * NH],
                                      ALU.max).then_inc(S["bound_step"], 1)
            dve.wait_ge(S["qn_ps"], NC)
            dve.tensor_reduce(norm2[:, 1, :], ps[:, 7, 0:TT * NH].rearrange("p (b h) -> p h b", h=NH),
                              AX, ALU.max).then_inc(S["bound_step"], 1)
            dve.wait_ge(S["bound_ps"], 1)
            dve.tensor_reduce(ncol[0:NH, 0:2], ps[0:NH, 0, 0:2 * P].rearrange("p (a b) -> p a b", b=P), AX,
                              ALU.max).then_inc(S["bound_step"], 1)
            dve.wait_ge(S["bound_step"], 4)
            dve.tensor_tensor(ncol[0:NH, 2:3], ncol[0:NH, 0:1], ncol[0:NH, 1:2], ALU.mult).then_inc(S["bound_step"], 1)
            dve.wait_ge(S["bound_ps"], 2)
            dve.tensor_reduce(ncol[0:1, 3:4], ps[0:1, 1, 0:NH], AX, ALU.max).then_inc(S["bound_step"], 1)
            dve.wait_ge(S["bound_ps"], 3)
            dve.tensor_copy(bound[:, 0:1], ps[:, 2, 0:1]).then_inc(S["bound_step"], 1)
            dve.tensor_scalar(bound[:, 2:3], ps[:, 2, 0:1], SMALL ** 2, None, ALU.is_le).then_inc(S["bound_step"], 1)
            dve.wait_ge(S["bound_step"], 8)
            dve.tensor_scalar(loose[:, :], bound[0:1, 2:3], -1.0, 1.0, ALU.mult, ALU.add).then_inc(S["bound_ready"], 1)
            dve.wait_ge(S["root_ready"], 1)
            dve.scalar_tensor_tensor(bound[:, 3:4], bound[:, 1:2], -HD ** -0.5, bound[:, 2:3], ALU.mult,
                                     ALU.mult).then_inc(S["bound_ready"], 1)
            dve.wait_ge(S["bound_ready"], 1)
            with dve.If(dve.value_load(loose[0:1, 0:1], min_val=0, max_val=1) > 0):
                for sent in qx_in:
                    dve.wait_ge(sent, NC // 2 * QX_SENT)
                with dve.Fori(0, TT) as t:
                    for h in range(NH):
                        dve.wait_ge(S["ms_ps"], t * NH + h + 1)
                        dve.tensor_reduce(nmax[:, h:h + 1], banks(4 * (h % 2), 4)[:, 0:KV], AX, ALU.max,
                                          negate=True).then_inc(S["nm_ready"], 1)
                    dve.wait_ge(S["nt_ps"], t + 1)
                    dve.tensor_copy(nrow[0:NH, :], ps[0:NH, 0, 0:P]).then_inc(S["nrow_ready"], 1)
                    dve.wait_ge(S["shift_in"], t * 16 + 16)

            def out_tail(c):
                for i in range(CT):
                    dve.wait_ge(S["oq_ps"], c * CT + i + 1)
                    o = bank(6 + i % 2).rearrange("p (h w) -> p h w", w=2 * HD)
                    dve.reciprocal(orec[:, i, :].unsqueeze(2), o[:, :, HD:HD + 1]).then_inc(S["orec_ready"], 1)
                    dve.wait_ge(S["orec_ready"], c * CT + i + 1)
                    dve.tensor_tensor(at[:, i].rearrange("p (h w) -> p h w", w=HD), o[:, :, 0:HD],
                                      orec[:, i, :].unsqueeze(2).to_broadcast([P, NH, HD]), ALU.mult).then_inc(S["at_ready"], 1)
                for k in range(DK):
                    dve.wait_ge(S["att_ps"], c * DK + k + 1)
                    dve.tensor_copy(att[:, k], bank(6 + k)).then_inc(S["att_ready"], 1)
                for b in range(2):
                    dve.wait_ge(S["o_ps"], c * 2 + b + 1)
                    dve.tensor_tensor(xtile(c * CT + 2 * b, 2), xtile(c * CT + 2 * b, 2),
                                      bank(6 + b).rearrange("p (a d) -> p a d", d=DM), ALU.add).then_inc(S["x2_ready"], 1)

            def heads_out(c):
                for g in range(NG):
                    dve.wait_ge(S["pv_done"], c * NV + KB * (g + 1))
                    dve.tensor_copy(ot[:, g], bank(4 + g % 2)).then_inc(S["o_evac"], 1)

            heads_out(0)
            with dve.Fori(1, NC) as c:
                out_tail(c - 1)
                heads_out(c)
            out_tail(NC - 1)
            dve.wait_ge(S["x2_ready"], 2 * NC)

            dve.wait_ge(S["ss4"], NE)
            dve.tensor_scalar(ve2[:, 0:NE], sqs[:, :], 1e-24, 1.0 / DM, ALU.max, ALU.mult).then_inc(S["ms4"], 1)
            for t in range(TT):
                dve.bn_stats(stat[:, t, :], xt[:, t, :]).then_inc(S["st5"], 1)
            for t in range(TT):
                dve.wait_ge(S["st5"], t + 1)
                dve.bn_aggr(mv[:, t, :], stat[:, t, :]).then_inc(S["st5"], 1)
            dve.wait_ge(S["st5"], 2 * TT)
            dve.tensor_scalar(ve[:, :], mv[:, :, 1], 1e-5, None, ALU.add).then_inc(S["ve5"], 1)
            dve.wait_ge(S["rms4"], 1)
            for x in range(NE):
                dve.scalar_tensor_tensor(sn[:, x], se[:, x], rstd2[:, x:x + 1], scales[:, 3, :],
                                         ALU.mult, ALU.mult).then_inc(S["sn_ready"], 1)
            dve.wait_ge(S["rs5"], 1)
            for t in range(TT):
                dve.tensor_scalar(xn[:, t, 0:DM], xt[:, t, :], mv[:, t, 0:1], rstd[:, t:t + 1],
                                  ALU.subtract, ALU.mult).then_inc(S["y_normed"], 1)
            dve.memset(xn[:, :, DM:DM + 1], 1.0).then_inc(S["xn_one"], 1)
            dve.memset(mrun, -3.0e38).then_inc(S["xn_one"], 1)
            dve.wait_ge(S["ss5"], TT)
            dve.wait_ge(S["sn_ready"], NE)
            dve.tensor_scalar(ve2[:, :], sq[:, :], 1e-24, 1.0 / DM, ALU.max, ALU.mult).then_inc(S["ms5"], 1)
            dve.wait_ge(S["rms5"], 1)
            for t in range(TT):
                dve.wait_ge(S["y_normed"], t + 1)
                dve.scalar_tensor_tensor(xn[:, t, 0:DM], xn[:, t, 0:DM], rstd2[:, t:t + 1], scales[:, 2, :],
                                         ALU.mult, ALU.mult).then_inc(S["xn_ready"], 1)
            dve.wait_ge(S["xn_one"], 2)
            for t in range(TT):
                dve.wait_ge(S["l_copy"], t + 1)
                dve.tensor_reduce(nmx[:, t:t + 1], lg[:, t], AX, ALU.max, negate=True).then_inc(S["l_max"], 1)
                if t >= 1:
                    dve.wait_ge(S["l_run"], t)
                dve.tensor_tensor(mrun, mrun, lg[:, t], ALU.max).then_inc(S["l_run"], 1)
            dve.wait_ge(S["mt_ps"], 1)
            dve.tensor_reduce(mcol[:, :], banks(0, 2).rearrange("p (e n) -> p e n", n=P), AX, ALU.max).then_inc(S["mcol_ready"], 1)
            dve.wait_ge(S["mcol_ready"], 1)
            for x in range(NE):
                dve.tensor_scalar(mdiag[:, x], ident[:, :], mcol[:, x:x + 1], None, ALU.mult).then_inc(S["mdiag_ready"], 1)
            dve.wait_ge(S["mb_ps"], 2)
            for t in range(TT):
                dve.wait_ge(S["l_exp"], t + 1)
                dve.tensor_tensor(lg[:, t], lg[:, t], banks(2, 2), ALU.subtract).then_inc(S["l_sub"], 1)
            for x in range(NE):
                dve.wait_ge(S["slot_ps"], x + 1)
                dve.reciprocal(srec[:, x:x + 1], ps[:, 4 + x % 2, DM:DM + 1]).then_inc(S["srec_ready"], 1)
                dve.wait_ge(S["srec_ready"], x + 1)
                if x >= 2:
                    dve.wait_ge(S["slt_ps"], x - 1)
                dve.tensor_scalar(slot[:, x % 2], ps[:, 4 + x % 2, 0:DM], srec[:, x:x + 1], None,
                                  ALU.mult).then_inc(S["slot_ready"], 1)
            for x in range(NE):
                dve.wait_ge(S["eo_ps"], x + 1)
                dve.tensor_copy(eo[:, x], ps[:, 4 + x % 2, 0:DM]).then_inc(S["eo_ready"], 1)
            dve.reciprocal(crec[:, :], csum[:, :]).then_inc(S["crec_ready"], 1)
            dve.wait_ge(S["crec_ready"], 1)
            for t in range(TT):
                dve.wait_ge(S["c_ps"], t + 1)
                dve.scalar_tensor_tensor(xt[:, t, :], ps[:, t % 8, 0:DM], crec[:, t:t + 1], xt[:, t, :],
                                         ALU.mult, ALU.add).then_inc(S["res_ready"], 1)

        @block.tensor
        def _(pe):
            mm = pe.matmul
            pe.wait_ge(S["consts"], 6)
            pe.wait_ge(S["w_mamba"], 16 * 9)
            pe.wait_ge(S["prep_dve"], 1 + DB)

            def turn(dst, src):
                return pe.transpose(dst, src, ident[:, :])

            with pe.Fori(0, NC) as c:
                for k in range(DK):
                    for i in range(CT):
                        if k == 0:
                            pe.wait_ge(S["a0_ready"], c * CT + i + 1)
                        last = turn(bank(k)[:, tok(i)], a0[:, i, tok(k)])
                    last.then_inc(S["a0t_ps"], 1)
                for o in range(2 * DB):
                    if o >= 6:
                        pe.wait_ge(S["u_raw"], c * DB + o - 5)
                    for k in range(DK):
                        if o == 0:
                            pe.wait_ge(S["a0t_ready"], c * DK + k + 1)
                        last = mm(bank(2 + o % 6), win[:, k, tok(o)], a0t[:, k], start=(k == 0), stop=(k == DK - 1))
                    last.then_inc(S["proj_ps"], 1)
                for d in range(DB):
                    pe.wait_ge(S["u_ready"], c * DB + d + 1)
                    last = mm(ps[0:RANK + 2 * NS, 0, :], xproj[:, d], u[:, d], start=(d == 0), stop=(d == DB - 1))
                last.then_inc(S["xdbl_ps"], 1)
                pe.wait_ge(S["xdbl_ready"], c + 1)
                pe.wait_ge(S["z_ready"], c * DB + DB)
                for d in range(DB):
                    mm(bank(4 + d), dtw[0:RANK, tok(d)], xdbl[0:RANK, :], start=True, stop=True).then_inc(S["dt_ps"], 1)
                for n in range(NS):
                    pe.wait_ge(S["hc_ready"], c * NS + n + 1)
                    for d in range(DB):
                        last = mm(bank(d), ident[:, :], hc[:, n % 2, d], start=(n == 0), stop=False)
                    last.then_inc(S["y_acc"], 1)
                for d in range(DB):
                    last = mm(bank(d), diag_skip[:, d], u[:, d], start=False, stop=True)
                last.then_inc(S["y_ready"], 1)
                pe.wait_ge(S["yz_ready"], c + 1)
                for i in range(CT):
                    for d in range(DB):
                        last = mm(bank(4 + i // 2)[:, part(i % 2)], yz[:, d, tok(i)], wout[:, d],
                                  start=(d == 0), stop=(d == DB - 1))
                    if i % 2:
                        last.then_inc(S["op_ps"], 1)
                for k in range(DK):
                    for i in range(CT):
                        if k == 0:
                            pe.wait_ge(S["h1_ready"], c * CT + i + 1)
                        last = turn(bank(6 + k)[:, tok(i)], h1[:, i, tok(k)])
                    last.then_inc(S["h1t_ps"], 1)
                for f in range(FB):
                    if f >= 4:
                        pe.wait_ge(S["g_ready"], c * FB + f - 3)
                    for k in range(DK):
                        if f == 0:
                            pe.wait_ge(S["h1t_ready"], c * DK + k + 1)
                        last = mm(bank(f % 4), w1[:, k, tok(f)], h1t[:, k], start=(k == 0), stop=(k == DK - 1))
                    last.then_inc(S["ff1_ps"], 1)
                for i in range(CT):
                    acc = bank(4 + i // 2)[:, part(i % 2)]
                    for f in range(FB):
                        if i == 0:
                            pe.wait_ge(S["g_ready"], c * FB + f + 1)
                        mm(acc, gate[:, f, tok(i)], w2[:, f], start=(f == 0), stop=False)
                    last = mm(acc, ones[0:1, :], rows[0:1, 0, :], start=False, stop=True)
                    if i % 2:
                        last.then_inc(S["ff2_ps"], 1)
                pe.wait_ge(S["ff2_ps"], c * 2 + 2)
                pe.sem_inc(S["chunk_done1"], 1)

            pe.wait_ge(S["chunk_done1"], ENGINES * NC + 1)
            pe.wait_ge(S["w_attn"], 16 * 5)
            for k in range(DK):
                for j, (o, w) in enumerate(KCOLS):
                    for x in range(2):
                        last = mm(ps[:, 4 * k + j, 0:w], wk[0:CP, x, tok(k)], ctxt[0:CP, x, o:o + w],
                                  start=(x == 0), stop=(x == 1))
                    last.then_inc(S["k_ps"], 1)
            for b in range(KB):
                n = min(P, KV - b * P)
                if b % 2 == 0:
                    pe.wait_ge(S["kf_ready"], b // 2 + 1)
                acc = ps[0:n, b // 2, part(b % 2)]
                for x in range(2):
                    mm(acc, ctxt[0:CP, x, b * P:b * P + n], wv[0:CP, x], start=(x == 0), stop=False)
                last = mm(acc, ones[0:1, 0:n], rows[0:1, 1, :], start=False, stop=True)
                if b % 2 or b == KB - 1:
                    last.then_inc(S["v_ps"], 1)

            def q_chunk(c):
                for k in range(DK):
                    if c >= 1:
                        pe.wait_ge(S["xat_ready"], c * DK)
                    for i in range(CT):
                        if k == 0:
                            pe.wait_ge(S["xa_ready"], c * CT + i + 1)
                        last = turn(bank(k)[:, tok(i)], xa[:, c % 2, i, tok(k)])
                    last.then_inc(S["xat_ps"], 1)
                if c >= 2:
                    pe.wait_ge(S["qf_ready"], (c - 1) * DK)
                for k in range(DK):
                    for x in range(DK):
                        if k == 0:
                            pe.wait_ge(S["xat_ready"], c * DK + x + 1)
                        last = mm(bank(2 + 2 * (c % 2) + k), wq[:, x, tok(k)], xat[:, c % 2, x], start=(x == 0), stop=(x == DK - 1))
                    last.then_inc(S["q_ps"], 1)

            def q_lengths(c):
                pe.wait_ge(S["qsq_ready"], c + 1)
                for i in range(CT):
                    for k in range(DK):
                        at_col = (c * CT + i) * NH + k * HALF
                        last = mm(ps[:, 7, at_col:at_col + HALF], xat[:, c % 2, k, tok(i)], sel[:, :], start=True, stop=True)
                last.then_inc(S["qn_ps"], 1)

            pe.wait_ge(S["vx_ready"], -(-KB // 2))
            pe.wait_ge(S["sel_ready"], 1)
            q_chunk(0)
            q_chunk(1)
            for b in range(KB):
                for k in range(DK):
                    n = min(P, KV - b * P)
                    last = mm(ps[0:n, 6, b * NH + k * HALF:b * NH + k * HALF + HALF], ksq[:, k, b * P:b * P + n], sel[:, :],
                              start=True, stop=True)
            last.then_inc(S["kn_ps"], 1)
            q_lengths(0)
            q_chunk(2)
            q_lengths(1)
            q_chunk(3)
            q_lengths(2)
            q_lengths(3)
            pe.wait_ge(S["xat_ready"], DK * NC)
            for x in range(2):
                pe.wait_ge(S["bound_step"], 2 + x)
                last = turn(ps[0:NH, 0, tok(x)], norm2[:, x, :])
            last.then_inc(S["bound_ps"], 1)
            pe.wait_ge(S["bound_step"], 5)
            pe.transpose(ps[0:1, 1, 0:NH], ncol[0:NH, 2:3], ident[0:NH, 0:NH]).then_inc(S["bound_ps"], 1)
            pe.wait_ge(S["qf_ready"], DK * NC)
            pe.wait_ge(S["bound_step"], 6)
            mm(ps[:, 2, 0:1], ones[0:1, :], ncol[0:1, 3:4], start=True, stop=True).then_inc(S["bound_ps"], 1)

            for sent in qx_in:
                pe.wait_ge(sent, NC // 2 * QX_SENT)
            pe.wait_ge(S["vx_init"], 4)
            pe.wait_ge(S["bound_ready"], 1)
            with pe.If(pe.value_load(loose[0:1, 0:1], min_val=0, max_val=1) > 0):
                pe.wait_ge(S["bound_ready"], 2)
                with pe.Fori(0, TT) as t:
                    for h in range(NH):
                        if h >= 2:
                            pe.wait_ge(S["nm_ready"], t * NH + h - 1)
                        for j, (o, n) in enumerate(KCOLS):
                            last = mm(ps[:, 4 * (h % 2) + j, 0:n], qx[0:XR, h, bass.ds(t * P, P)], kx[0:XR, h, o:o + n],
                                      start=True, stop=True)
                        last.then_inc(S["ms_ps"], 1)
                    pe.wait_ge(S["nm_ready"], t * NH + NH)
                    turn(ps[0:NH, 0, 0:P], nmax[:, :]).then_inc(S["nt_ps"], 1)
                    pe.wait_ge(S["shift_in"], t * 16 + 16)

            def scores(c, v, first):
                g, b = v // KB, v % KB
                n = min(P, KV - b * P)
                for h in range(2):
                    r = 2 * v + h
                    if r >= 2 or not first:
                        pe.wait_ge(S["p_ready"], c * 2 * NV + r - 1)
                    for x in range(2):
                        head = G * g + 2 * h + x
                        last = mm(ps[0:n, 2 * h + x, :], kx[0:XR + 1, head, b * P:b * P + n],
                                  qx[0:XR + 1, head, c * C:c * C + C] if first else qx[0:XR + 1, head, bass.ds(c * C, C)],
                                  start=True, stop=True)
                    last.then_inc(S["s_ps"], 1)

            def values(c, v, first):
                g, b = v % NV // KB, v % KB
                n = min(P, KV - b * P)
                if b == 0 and (g >= 2 or not first):
                    pe.wait_ge(S["o_evac"], c * NG + g - 1)
                pe.wait_ge(S["p_ready"], c * 2 * NV + 2 * v + 2)
                for x in range(G):
                    last = mm(ps[2 * HD * x:2 * HD * x + 2 * HD, 4 + g % 2, :], vx[0:n, b, G * g + x, :],
                              prob[0:n, v % 2, x], start=(b == 0), stop=(b == KB - 1))
                last.then_inc(S["pv_done"], 1)

            def out_piece(c, s):
                if s < CT:
                    if s == 0:
                        pe.wait_ge(S["o_evac"], c * NG + NG)
                    if s >= 2:
                        pe.wait_ge(S["at_ready"], c * CT + s - 1)
                    for g in range(NG):
                        last = turn(bank(6 + s % 2)[:, tok(g)], ot[:, g, tok(s)])
                    last.then_inc(S["oq_ps"], 1)
                elif s < CT + DK:
                    k = s - CT
                    pe.wait_ge(S["at_ready"], c * CT + CT)
                    for i in range(CT):
                        last = turn(bank(6 + k)[:, tok(i)], at[:, i, tok(k)])
                    last.then_inc(S["att_ps"], 1)
                elif s < PIECES:
                    i = s - CT - DK
                    if i == 0:
                        pe.wait_ge(S["att_ready"], c * DK + DK)
                    acc = bank(6 + i // 2)[:, part(i % 2)]
                    for k in range(DK):
                        mm(acc, att[:, k, tok(i)], wo[:, k], start=(k == 0), stop=False)
                    last = mm(acc, ones[0:1, :], rows[0:1, 2, :], start=False, stop=True)
                    if i % 2:
                        last.then_inc(S["o_ps"], 1)

            for v in range(NV):
                scores(0, v, True)
                if v >= 1:
                    values(0, v - 1, True)
            with pe.Fori(1, NC) as c:
                for v in range(NV):
                    scores(c, v, False)
                    values(c, v - 1, False)
                    if v >= 2:
                        out_piece(c - 1, v - 2)
            values(NC, -1, False)
            for s in range(PIECES):
                out_piece(NC - 1, s)

            for r in range(4):
                for x in range(4):
                    if r < 2:
                        pe.wait_ge(S["sn_ready"], 4 * r + x + 1)
                    last = turn(bank(r)[:, tok(x)], sn[:, 4 * (r % 2) + x, tok(r // 2)])
                last.then_inc(S["snt_ps"], 1)
            pe.wait_ge(S["snt_ready"], 4)

            def turn_tokens(t):
                pe.wait_ge(S["xn_ready"], t + 1)
                if t >= 2:
                    pe.wait_ge(S["xnt_ready"], t - 1)
                for k in range(DK):
                    last = turn(ps[:, 6 + t % 2, tok(k)], xn[:, t, tok(k)])
                last.then_inc(S["xnt_ps"], 1)

            turn_tokens(0)
            for t in range(TT + 1):
                if t + 1 < TT:
                    turn_tokens(t + 1)
                if t < TT:
                    pe.wait_ge(S["xnt_ready"], t + 1)
                    if t >= 2:
                        pe.wait_ge(S["l_copy"], t - 1)
                    for n in range(2):
                        for k in range(DK):
                            last = mm(bank(2 * (t % 2) + n), xnt[:, t % 2, k], snt[:, k, n * 512:n * 512 + 512],
                                      start=(k == 0), stop=(k == DK - 1))
                    last.then_inc(S["l_ps"], 1)
                if t >= 1:
                    pe.wait_ge(S["l_exp"], t)
                    if t >= 2:
                        pe.wait_ge(S["et_ready"], t - 1)
                    for x in range(NE):
                        last = turn(bank(4 + x // 4)[:, tok(x % 4)], ex[:, (t - 1) % 2, tok(x)])
                    last.then_inc(S["et_ps"], 1)
            pe.wait_ge(S["l_run"], TT)
            pe.wait_ge(S["l_copy"], TT)
            for x in range(NE):
                last = turn(bank(x // 4)[:, tok(x % 4)], mrun[:, tok(x)])
            last.then_inc(S["mt_ps"], 1)
            for n in range(2):
                pe.wait_ge(S["mdiag_ready"], 4 * n + 4)
                mm(bank(2 + n), ones[:, :], mdiag[:, 4 * n:4 * n + 4], start=True, stop=True).then_inc(S["mb_ps"], 1)

            def turn_slots(x):
                pe.wait_ge(S["slot_ready"], x + 1)
                if x >= 2:
                    pe.wait_ge(S["slt_ready"], x - 1)
                for k in range(DK):
                    last = turn(ps[:, 6 + x % 2, tok(k)], slot[:, x % 2, tok(k)])
                last.then_inc(S["slt_ps"], 1)

            pe.wait_ge(S["xnt_ready"], TT)
            pe.wait_ge(S["et_ready"], TT)
            for x in range(NE):
                if x >= 2:
                    pe.wait_ge(S["slot_ready"], x - 1)
                for t in range(TT):
                    if x == 0:
                        pe.wait_ge(S["d_ready"], t + 1)
                    last = mm(ps[:, 4 + x % 2, 0:DM + 1], lg[:, t, tok(x)], xn[:, t, :], start=(t == 0), stop=(t == TT - 1))
                last.then_inc(S["slot_ps"], 1)
                if x >= 1:
                    turn_slots(x - 1)
            turn_slots(NE - 1)
            pe.wait_ge(S["w_b2"], 16)
            for x in range(NE + 1):
                if x < NE:
                    pe.wait_ge(S["slt_ready"], x + 1)
                    pe.wait_ge(w_exp[x % NW], 32 * (x // NW + 1))
                    if x >= 2:
                        pe.wait_ge(S["hid_ready"], FB * (x - 1))
                    for f in range(FB):
                        for k in range(DK):
                            last = mm(ps[:, 2 * (x % 2) + f // 4, tok(f % 4)], mw1[:, x % NW, k, tok(f)], slt[:, x, k],
                                      start=(k == 0), stop=(k == DK - 1))
                        if f % 4 == 3:
                            last.then_inc(S["h_ps"], 1)
                if x >= 1:
                    y = x - 1
                    if y >= 2:
                        pe.wait_ge(S["eo_ready"], y - 1)
                    acc = ps[:, 4 + y % 2, 0:DM]
                    for f in range(FB):
                        pe.wait_ge(S["hid_ready"], FB * y + f + 1)
                        mm(acc, hid[:, y % 2, f], mw2[:, y % NW, f], start=(f == 0), stop=False)
                    mm(acc, ones[0:1, :], b2[0:1, y, :], start=False, stop=True).then_inc(S["eo_ps"], 1)
            for t in range(TT):
                if t >= 8:
                    pe.wait_ge(S["res_ready"], t - 7)
                if t == 0:
                    pe.wait_ge(S["hid_ready"], FB * NE)
                if t == 4:
                    pe.wait_ge(S["eo_ready"], NE)
                for x in range(NE):
                    if t == 0:
                        pe.wait_ge(S["eo_ready"], x + 1)
                    last = mm(ps[:, t % 8, 0:DM], cwt[:, x, tok(t)], eo[:, x], start=(x == 0), stop=(x == NE - 1))
                last.then_inc(S["c_ps"], 1)


def kernel(x, ctx_768, L0_attn_in_proj_w, L0_attn_conv_w, L0_attn_conv_b, L0_attn_x_proj_w, L0_attn_dt_proj_w,
           L0_attn_dt_proj_b, L0_attn_A_log, L0_attn_D, L0_attn_out_proj_w, L0_attn_norm_w, L0_attn_ffn_w1,
           L0_attn_ffn_b1, L0_attn_ffn_w2, L0_attn_ffn_b2, L0_attn_ffn_norm_w, L0_xattn_Wq, L0_xattn_bq,
           L0_xattn_Wk, L0_xattn_bk, L0_xattn_Wv, L0_xattn_bv, L0_xattn_Wo, L0_xattn_bo, L0_ffn_norm_gamma,
           L0_ffn_slot_norm_gamma, L0_ffn_slot_embeds, L0_ffn_w1, L0_ffn_b1, L0_ffn_w2, L0_ffn_b2):
    import numpy as np
    import concourse.bacc as bacc
    from concourse.bass_utils import run_bass_kernel_spmd as run

    def blocks(w, p=P):
        w = np.asarray(w)
        return w.reshape(w.shape[0] // p, p, -1).transpose(1, 0, 2)

    def cols(v):
        return blocks(np.asarray(v).reshape(-1, 1))[:, :, 0]

    def spread(w):
        w = np.asarray(w)
        lead = w.shape[:-1]
        return w.reshape(*lead, DK, HALF, HD).swapaxes(-1, -2).reshape(*lead, DM)

    ins = {
        "x": np.asarray(x)[0],
        "ctx": blocks(np.asarray(ctx_768)[0].T, CP),
        "win": blocks(np.asarray(L0_attn_in_proj_w).T),
        "xproj": blocks(np.asarray(L0_attn_x_proj_w).T),
        "dtw": np.asarray(L0_attn_dt_proj_w).T,
        "wout": blocks(np.asarray(L0_attn_out_proj_w).T),
        "w1": blocks(np.asarray(L0_attn_ffn_w1).T),
        "w2": blocks(np.asarray(L0_attn_ffn_w2).T),
        "wq": blocks(spread(L0_xattn_Wq)),
        "wk": blocks(spread(L0_xattn_Wk), CP),
        "wv": blocks(L0_xattn_Wv, CP),
        "wo": blocks(L0_xattn_Wo),
        "chan": np.concatenate([
            blocks(L0_attn_conv_w).reshape(P, -1), cols(L0_attn_conv_b), cols(L0_attn_dt_proj_b),
            blocks(L0_attn_A_log).reshape(P, -1), cols(L0_attn_D), cols(L0_attn_ffn_b1),
            cols(spread(L0_xattn_bq)), cols(spread(L0_xattn_bk)), cols(np.asarray(L0_ffn_b1).reshape(-1))], axis=1),
        "scales": np.concatenate([np.asarray(v) for v in (L0_attn_norm_w, L0_attn_ffn_norm_w, L0_ffn_norm_gamma,
                                                          L0_ffn_slot_norm_gamma)])[None],
        "rows": np.concatenate([np.asarray(v) for v in (L0_attn_ffn_b2, L0_xattn_bv, L0_xattn_bo)])[None],
        "slots": np.asarray(L0_ffn_slot_embeds).transpose(1, 0, 2),
        "mw1": np.asarray(L0_ffn_w1).reshape(NE, DK, P, FH).transpose(0, 2, 1, 3),
        "mw2": np.asarray(L0_ffn_w2).reshape(NE, FB, P, DM).transpose(0, 2, 1, 3),
        "mb2": np.asarray(L0_ffn_b2).reshape(1, -1),
    }
    nc = bacc.Bacc("TRN2", target_bir_lowering=False, num_devices=1)
    arrays = {"in_" + k: np.ascontiguousarray(v) for k, v in ins.items()}
    args = [nc.dram_tensor(k, v.shape, mybir.dt.from_np(v.dtype), kind="ExternalInput").ap()
            for k, v in arrays.items()]
    out = nc.dram_tensor("out", (T, DM), F32, kind="ExternalOutput").ap()
    scratch = nc.dram_tensor("bc_scratch", (NC, 2 * NS, C), F32, kind="Internal").ap()
    decoder_layer(nc, *args, out, scratch)
    r = run(nc, [arrays], core_ids=[0])
    return r.results[0]["out"].reshape(1, T, DM)
```

```python
from contextlib import ExitStack

import concourse.bass as bass
from concourse import mybir

F32 = mybir.dt.float32
BF16 = mybir.dt.bfloat16
ALU = mybir.AluOpType
ACT = mybir.ActivationFunctionType
AX = mybir.AxisListType.X

P = 128
T = 2048
DM = 256
DK = DM // P
DI = 512
DB = DI // P
NS = 16
RANK = 16
TAPS = 4
FH = 1024
FB = FH // P
NH, HD = 16, 16
KV = 1601
KB = -(-KV // P)
CW = 192
CP = CW // 2
NE, SL = 8, 128
MS = NE * SL
C = 512
NC = T // C
CT = C // P
TT = T // P
EARLY_LATE = [(0, TT - CT), (TT - CT, TT)]
G = 4
NG = NH // G
NV = NG * KB
LAST = KV - (KB - 1) * P
PIECES = 2 * CT + DK
HALF = NH // DK
BG = 2
NBG = NS // BG
NW = 5
ARENA = 50240
SMALL = 120.0
ENGINES = 4
DP = DB // 2
NU = NS * DP
NP = NU // 2
SUMMED = [j for j in range(NP - 1) if j % 3 == 0]
RING = 3
AHEAD = 4
UB = [6, 7, 6, 7]
VB = [0, 1, 2, 3, 6, 7, 0]
VE = 3
DTB = [7, 6, 7, 6]

TERMS = [(0, 0), (0, 1), (1, 0), (1, 1), (0, 2), (2, 0)]
XR = len(TERMS) * HD
QX_SENT = 16 * DK * len(TERMS)
KCOLS = [(o, min(512, KV - o)) for o in range(0, KV, 512)]

CH = {}
_at = 0
for _n, _w in (("conv_w", DB * TAPS), ("conv_b", DB), ("dt_b", DB), ("a_log", DB * NS), ("skip", DB),
               ("ffn_b1", FB), ("bq", DK), ("bk", DK), ("moe_b1", NE * FB)):
    CH[_n] = (_at, _at + _w)
    _at += _w
CHW = _at


def decoder_layer(nc, x_d, ctx_d, win_d, xproj_d, dtw_d, wout_d, w1_d, w2_d, wq_d, wk_d, wv_d, wo_d,
                  chan_d, scales_d, rows_d, slots_d, mw1_d, mw2_d, mb2_d, out_d, bc_scratch):
    with ExitStack() as ctx:
        def sb(name, shape, dt=F32):
            return ctx.enter_context(nc.sbuf_tensor(name, shape, dt))

        def sem(name):
            return ctx.enter_context(nc.semaphore(name))

        ps = ctx.enter_context(nc.psum_tensor("ps", [P, 8, 512], F32))
        xt = sb("xt", [P, TT, DM])
        ident = sb("ident", [P, P])
        ones = sb("ones", [P, P])
        mhalf = sb("mhalf", [P, TT])
        chan = sb("chan", [P, CHW])
        scales = sb("scales", [P, 4, DM])
        rows = sb("rows", [1, 3, DM])
        stat = sb("stat", [P, TT, 6])
        mv = sb("mv", [P, TT, 2])
        sq = sb("sq", [P, TT])
        ve = sb("ve", [P, TT])
        rstd = sb("rstd", [P, TT])
        ve2 = sb("ve2", [P, TT])
        rstd2 = sb("rstd2", [P, TT])
        sq3 = sb("sq3", [P, CT])
        ve3 = sb("ve3", [P, CT])
        rstd3 = sb("rstd3", [P, CT])
        mark = sb("mark", [P, 1])
        sel = sb("sel", [P, HALF])
        norm2 = sb("norm2", [P, 2, NH])
        ncol = sb("ncol", [P, 4])
        half = sb("half", [P, 1])
        bound = sb("bound", [P, 4])
        loose = sb("loose", [1, 1], mybir.dt.int32)
        arena = sb("arena", [P, ARENA])

        def ch(name, *dims):
            a, b = CH[name]
            v = chan[:, a:b]
            return v.rearrange("p (a b) -> p a b", b=dims[0]) if dims else v

        class Stack:
            def __init__(self, at=0):
                self.at = at

            def take(self, *shape, dt=F32):
                n = 1
                for s in shape:
                    n *= s
                words = n if dt == F32 else (n + 1) // 2
                v = arena[:, self.at:self.at + words]
                self.at += words
                assert self.at <= ARENA, self.at
                if dt != F32:
                    v = v.bitcast(dt)[:, 0:n]
                if len(shape) == 2:
                    v = v.rearrange("p (a b) -> p a b", b=shape[1])
                if len(shape) == 3:
                    v = v.rearrange("p (a b c) -> p a b c", b=shape[1], c=shape[2])
                if len(shape) == 4:
                    v = v.rearrange("p (a b c d) -> p a b c d", b=shape[1], c=shape[2], d=shape[3])
                return v

        m = Stack()
        win = m.take(DK, 2 * DI)
        xproj = m.take(DB, RANK + 2 * NS)
        dtw = m.take(DI)
        wout = m.take(DB, DM)
        w1 = m.take(DK, FH)
        w2 = m.take(FB, DM)
        neg_a = m.take(DB, NS)
        diag_skip = m.take(DB, P)
        carry = m.take(DB, NS)
        hist = m.take(DB, TAPS - 1)
        a0n = m.take(CT, DM)
        a0 = m.take(CT, DM)
        a0t = m.take(DK, C)
        u = m.take(DB, C)
        zs = m.take(DB, C)
        xdbl = m.take(C)
        delta = m.take(DB, C)
        delta_next = m.take(DB, C)
        du = m.take(DB, C)
        bg = m.take(2, BG, C)
        cg = m.take(2, BG, C)
        da = m.take(AHEAD, 2, C)
        dbu = m.take(2, 2, C)
        hs = m.take(2 * RING, 2, C)
        at_conv = m.at
        conv = m.take(DB, C)
        at_upad = m.at
        upad = m.take(DB, TAPS - 1 + C)
        m2 = Stack(at_conv)
        sp_exp = m2.take(DB, C)
        m2 = Stack(at_upad)
        sp_ln = m2.take(DB, C)
        at_gate = m.at
        gate = m.take(FB, C)
        h1 = m.take(CT, DM)
        at_hsum = m.at
        hsum = m.take(CT, DM)
        h1t = m.take(DK, C)
        at_junk = m.at - DK * C
        m3 = Stack(at_gate)
        yz = m3.take(DB, C)
        m3 = Stack(at_junk)
        junk = m3.take(CT, DM)
        m3 = Stack(at_hsum)
        sp_cor = m3.take(DB, C)

        a = Stack()
        kx = a.take(NH, KV, dt=BF16)
        qx_at = a.at
        qx = a.take(NH, T, dt=BF16)
        vx = a.take(KB, NH, 2 * HD)
        wq = a.take(DK, DM)
        wo = a.take(DK, DM)
        region = a.at
        a1 = Stack(qx_at)
        ctxt = a1.take(2, KV)
        wk = a1.take(2, DM)
        wv = a1.take(2, DM)
        kf = a1.take(DK, KV)
        kp = [a1.take(DK, KV, dt=BF16) for _ in range(3)]
        ksq = a1.take(DK, KV)
        assert a1.at <= qx_at + NH * T // 2
        a2 = Stack(region)
        xa = a2.take(2, CT, DM)
        xat = a2.take(2, DK, C)
        qf = a2.take(2, DK, C)
        qp = [a2.take(2, DK * C, dt=BF16) for _ in range(3)]
        a3 = Stack(region)
        prob = a3.take(2, G, C)
        ot = a3.take(NG, C)
        at = a3.take(CT, DM)
        att = a3.take(DK, C)
        orec = a3.take(CT, NH)
        a4 = Stack(region)
        nmax = a4.take(NH)
        nrow = a4.take(P, dt=BF16)

        at_slots = ARENA - NE * DM - DK * MS
        assert max(a2.at, a3.at) <= at_slots
        e0 = Stack(at_slots)
        se = e0.take(NE, DM)
        snt = e0.take(DK, MS)
        e1 = Stack()
        xn = e1.take(TT, DM + 1)
        at_lg = e1.at
        lg = e1.take(TT, MS)
        cwt = e1.take(NE, T)
        region = e1.at
        ex = e1.take(2, MS)
        xnt = e1.take(2, DK, P)
        mrun = e1.take(MS)
        mdiag = e1.take(NE, P)
        e2 = Stack(region)
        slot = e2.take(4, DM)
        slt = e2.take(NE, DK, P)
        hid = e2.take(2, FB, P)
        eo = e2.take(NE, DM)
        b2 = e2.take(NE, DM)
        assert max(e1.at, e2.at) <= at_slots
        mcol = sb("mcol", [P, NE])
        srec = sb("srec", [P, NE])
        sqs = sb("sqs", [P, NE])
        nmx = sb("nmx", [P, TT])
        csum = sb("csum", [P, TT])
        crec = sb("crec", [P, TT])
        tscale = sb("tscale", [P, TT])
        mw = []
        for n in range(NW):
            e4 = Stack(at_slots if n == 0 else at_lg + (n - 1) * (DK * FH + FB * DM))
            mw.append((e4.take(DK, FH), e4.take(FB, DM)))
        e5 = Stack(at_slots + NE * DM)
        junk4 = e5.take(NE, DM)

        S = {name: sem(name) for name in """
            x_first w_first w_mamba consts prep_act prep_dve mamba_done
mark1 st1 ve1 rs1 a0_ready a0_kept a0t_ps a0t_ready z_ps u_ps u_raw z_ready hist_in conv_step u_ready
            xdbl_ps xdbl_ready bc_stored bc_even bc_odd dt_ps sp_in sp_act sp_step delta_ready
            du_ready da_ready dbu_ready scan_done carry_done hc_ready pair_ready y_acc
            yz_ready op_ps hsum_ready ss1 ms1 rms1 h1_ready h1t_ps h1t_ready ff1_ps g_ready ff2_ps
            r_ready ss2 ms2 rms2 rn_ready x1_ready
            w_attn  k_ps kf_ready kp_ready ksq_ready kr_ready kx_in v_ps vx_ready vx_init sel_ready
            st2  ve3 rs3 xa_ready xat_ps xat_ready q_ps qf_ready qp_ready qsq_ready qr_ready qx_even qx_odd
            kn_ps qn_ps     bound_step  root_ready bound_ready bound_ps  
            ms_ps nm_ready nt_ps nrow_ready shift_in s_ps p_ready pv_done o_evac oq_ps orec_ready at_ready
            att_ps att_ready o_ps x2_ready
            w_slots ss4 ms4 rms4 sn_ready snt_ps snt_ready
            st5  ve5 rs5 y_normed tscale_step ms5 rms5 xn_ready xn_one xnt_ps xnt_ready l_ps l_copy l_max l_run
            l_exp et_ps et_ready mt_ps mcol_ready mdiag_ready mb_ps l_sub d_ready
            slot_ps srec_ready slot_ready slt_ps slt_ready w_exp0 w_exp1 w_exp2 w_exp3 w_exp4 w_b2
            h_ps hid_ready eo_ps eo_ready c_ps crec_ready res_ready out_done""".split()}
        w_exp = [S["w_exp0"], S["w_exp1"], S["w_exp2"], S["w_exp3"], S["w_exp4"]]
        qx_in = [S["qx_even"], S["qx_odd"]]
        bc_in = [S["bc_even"], S["bc_odd"]]

        def step(w):
            return 2 * (w // (2 * DP)) + w % 2, w // 2 % DP

        def pair_buffer(j):
            return j % RING if j < NP - 1 else 1

        def slot_free(c, j):
            before = {0: NP - 4 - NP, 1: -1, 2: NP - 2 - NP, NP - 1: NP - 3}
            return c * NP + (before[j] if j in before else j - RING) + 1

        def state(w):
            return hs[:, 2 * pair_buffer(w // 2) + w % 2]

        def flat(v):
            return v.rearrange("p a b -> p (a b)")

        def over(v, n):
            return v.unsqueeze(1).to_broadcast([v.shape[0], n, v.shape[1]])

        def bank(n):
            return ps[:, n, :]

        def banks(n, k):
            return ps[:, n:n + k, :].rearrange("p a b -> p (a b)")

        def tok(n):
            return slice(n * P, n * P + P)

        def part(n):
            return slice(n * DM, n * DM + DM)

        block = ctx.enter_context(nc.Block())

        @block.sync
        def _(sp):
            x_tiles = x_d.rearrange("(t p) d -> p t d", p=P)
            sp.dma_start(xt[:, 0:CT, :], x_tiles[:, 0:CT, :]).then_inc(S["x_first"], 16)
            sp.dma_start(chan[:, :], chan_d).then_inc(S["x_first"], 16)
            for dst, src in ((win, win_d), (xproj, xproj_d), (dtw[0:RANK, :], dtw_d)):
                sp.dma_start(dst, src).then_inc(S["w_first"], 16)
            for dst, src in ((xt[:, CT:TT, :], x_tiles[:, CT:TT, :]), (wout, wout_d), (w1, w1_d), (w2, w2_d),
                             (flat(scales[:, :, :]), scales_d.to_broadcast([P, 4 * DM])),
                             (flat(rows[:, :, :]), rows_d)):
                sp.dma_start(dst, src).then_inc(S["w_mamba"], 16)

            def load_bc(c, q, first=False):
                if q >= 2 or not first:
                    sp.wait_ge(S["dbu_ready"], c * NU + BG * DP * (q - 1))
                    sp.wait_ge(S["hc_ready"], c * NU + BG * DP * (q - 1))
                for dst, n in ((bg, q * BG), (cg, NS + q * BG)):
                    row = bc_scratch[0:1, n:n + BG, :] if first else bc_scratch[bass.ds(c, 1), n:n + BG, :]
                    sp.dma_start(flat(dst[:, q % 2]), row.rearrange("o n t -> o (n t)").to_broadcast([P, BG * C])).then_inc(bc_in[q % 2], 16)

            def next_bc(c, first=False):
                sp.wait_ge(S["xdbl_ready"], c + 1)
                row = bc_scratch[0:1, :, :] if first else bc_scratch[bass.ds(c, 1), :, :]
                sp.dma_start(row.rearrange("o n t -> (o n) t"), xdbl[RANK:RANK + 2 * NS, :]).then_inc(S["bc_stored"], 16)
                sp.wait_ge(S["bc_stored"], c * 16 + 16)
                for q in range(2):
                    load_bc(c, q, first)

            next_bc(0, True)
            with sp.Fori(0, NC - 1) as c:
                for q in range(2, NBG):
                    load_bc(c, q)
                next_bc(c + 1)
            for q in range(2, NBG):
                load_bc(NC - 1, q)

            sp.wait_ge(S["yz_ready"], NC)
            sp.dma_start(ctxt[0:CP], ctx_d).then_inc(S["w_attn"], 16)
            for dst, src in ((wk[0:CP], wk_d), (wv[0:CP], wv_d), (wq, wq_d), (wo, wo_d)):
                sp.dma_start(dst, src).then_inc(S["w_attn"], 16)
            sp.wait_ge(S["mamba_done"], ENGINES)
            sp.dma_start(se, slots_d).then_inc(S["w_slots"], 16)
            for n in range(3):
                sp.wait_ge(S["kp_ready"], n + 1)
                for j, (_, b) in enumerate(TERMS):
                    if b == n:
                        for k in range(DK):
                            sp.dma_start(kx[HD * j:HD * j + HD, HALF * k:HALF * k + HALF, :],
                                         kp[n][:, k, :]).then_inc(S["kx_in"], 16)
            sp.wait_ge(S["kx_in"], 16 * DK * len(TERMS))
            sp.wait_ge(S["kn_ps"], 1)
            for c in range(NC):
                for n in range(3):
                    sp.wait_ge(S["qp_ready"], c * 3 + n + 1)
                    for j, (b, _) in enumerate(TERMS):
                        if b == n:
                            for k in range(DK):
                                sp.dma_start(qx[HD * j:HD * j + HD, HALF * k:HALF * k + HALF, c * C:c * C + C],
                                             qp[n][:, c % 2, k * C:k * C + C]).then_inc(qx_in[c % 2], 16)
            sp.wait_ge(S["bound_ready"], 1)
            with sp.If(sp.value_load(loose[0:1, 0:1], min_val=0, max_val=1) > 0):
                sp.wait_ge(S["vx_init"], 4)
                with sp.Fori(0, TT) as t:
                    sp.wait_ge(S["nrow_ready"], t + 1)
                    sp.dma_start(qx[XR:XR + 1, :, bass.ds(t * P, P)], nrow[0:NH, :]).then_inc(S["shift_in"], 16)

            sp.wait_ge(S["x2_ready"], 2 * NC)
            sp.dma_start(flat(b2[0:1]), mb2_d).then_inc(S["w_b2"], 16)
            for x in range(NE):
                if x == 0:
                    sp.wait_ge(S["l_ps"], TT)
                elif x < NW:
                    sp.wait_ge(S["slot_ps"], NE)
                else:
                    sp.wait_ge(S["eo_ps"], x - NW + 1)
                w1_x, w2_x = mw[x % NW]
                sp.dma_start(w1_x, mw1_d[x]).then_inc(w_exp[x % NW], 16)
                sp.dma_start(w2_x, mw2_d[x]).then_inc(w_exp[x % NW], 16)
            for t in range(0, TT, CT):
                sp.wait_ge(S["res_ready"], t + CT)
                sp.dma_start(out_d[t * P:(t + CT) * P, :].rearrange("(t p) d -> p t d", p=P),
                             xt[:, t:t + CT, :]).then_inc(S["out_done"], 16)
            sp.wait_ge(S["out_done"], 16 * (TT // CT))

        @block.gpsimd
        def _(pool):
            pool.memset(ident[:, :], 0.0).then_inc(S["consts"], 1)
            pool.memset(ones[:, :], 1.0).then_inc(S["consts"], 1)
            pool.memset(mhalf[:, :], -0.5).then_inc(S["consts"], 1)
            pool.memset(flat(carry), 0.0).then_inc(S["consts"], 1)
            pool.memset(flat(hist), 0.0).then_inc(S["consts"], 1)
            pool.wait_ge(S["consts"], 1)
            pool.affine_select(out=ident[:, :], in_=ident[:, :], compare_op=ALU.not_equal, fill=1.0, base=0,
                               pattern=[[-1, P]], channel_multiplier=1).then_inc(S["consts"], 1)

            def rsqrt(dst, src, n):
                return pool.tensor_tensor(dst[:, 0:n], src[:, 0:n], mhalf[:, 0:n], ALU.pow)

            pool.wait_ge(S["consts"], 6)
            def scan_input(c, w, first=False):
                (n, p), q = step(w), w // (BG * DP)
                if w == 0:
                    pool.wait_ge(S["du_ready"], c + 1)
                if w % (BG * DP) == 0:
                    pool.wait_ge(bc_in[q % 2], c * 16 * NBG + 32 * (q // 2 + 1))
                if w >= 2 or not first:
                    pool.wait_ge(S["scan_done"], c * 2 * NU + 2 * (w - 1))
                pool.tensor_tensor(dbu[:, w % 2], du[:, 2 * p:2 * p + 2], over(bg[:, q % 2, n % BG], 2),
                                   ALU.mult).then_inc(S["dbu_ready"], 1)

            def add_pair(c, j):
                pool.wait_ge(S["hc_ready"], c * NU + 2 * j + 2)
                pool.tensor_tensor(state(2 * j), state(2 * j), state(2 * j + 1), ALU.add).then_inc(S["pair_ready"], 1)

            def layer_norm_root(c):
                pool.wait_ge(S["ve1"], c + 1)
                rsqrt(rstd, ve, CT).then_inc(S["rs1"], 1)

            def first_root(c):
                pool.wait_ge(S["ms1"], c + 1)
                rsqrt(rstd2, ve2, CT).then_inc(S["rms1"], 1)

            def second_root(c):
                pool.wait_ge(S["ms2"], c + 1)
                rsqrt(rstd3, ve3, CT).then_inc(S["rms2"], 1)

            def scan_chunk(c, first=False, second=False, last=False):
                for w in range(NU):
                    scan_input(c, w, first)
                    if w % 2 == 0 and w // 2 - 2 in SUMMED:
                        add_pair(c, w // 2 - 2)
                    if w == 5 and not first and not second:
                        second_root(c - 2)
                    if w == 6 and not last:
                        layer_norm_root(c + 1)
                    if w == 9 and not first:
                        first_root(c - 1)
                if NP - 2 in SUMMED:
                    add_pair(c, NP - 2)

            layer_norm_root(0)
            scan_chunk(0, first=True)
            scan_chunk(1, second=True)
            with pool.Fori(2, NC - 1) as c:
                scan_chunk(c)
            scan_chunk(NC - 1, last=True)
            second_root(NC - 2)
            first_root(NC - 1)
            pool.wait_ge(S["yz_ready"], NC)
            pool.memset(vx, 0.0).then_inc(S["vx_init"], 1)
            pool.wait_ge(S["vx_init"], 1)
            pool.memset(vx[:, :, :, HD:HD + 1], 1.0).then_inc(S["vx_init"], 1)
            second_root(NC - 1)
            pool.wait_ge(S["rms2"], NC)
            pool.sem_inc(S["mamba_done"], 1)

            pool.wait_ge(S["ve3"], 1)
            rsqrt(rstd, ve, TT).then_inc(S["rs3"], 1)
            pool.wait_ge(S["rs3"], 1)
            pool.wait_ge(S["mamba_done"], ENGINES)
            pool.wait_ge(S["vx_init"], 2)
            pool.memset(kx[XR:XR + 1, :, :], 1.0).then_inc(S["vx_init"], 1)
            pool.wait_ge(S["vx_init"], 3)
            pool.memset(half[:, :], 0.5).then_inc(S["consts"], 1)
            pool.wait_ge(S["consts"], 7)
            pool.wait_ge(S["kx_in"], 16 * DK * len(TERMS))
            pool.wait_ge(S["kn_ps"], 1)
            pool.memset(arena[XR:XR + 1, qx_at:qx_at + NH * T // 2], 0.0).then_inc(S["vx_init"], 1)
            pool.wait_ge(S["vx_init"], 4)
            pool.wait_ge(S["bound_step"], 7)
            pool.tensor_tensor(bound[:, 1:2], bound[:, 0:1], half[:, :], ALU.pow).then_inc(S["root_ready"], 1)
            pool.wait_ge(S["root_ready"], 1)
            pool.wait_ge(S["ms4"], 1)
            rsqrt(rstd2, ve2, NE).then_inc(S["rms4"], 1)

            for n, (t0, t1) in enumerate(EARLY_LATE):
                pool.wait_ge(S["ve5"], n + 1)
                rsqrt(rstd[:, t0:t1], ve[:, t0:t1], t1 - t0).then_inc(S["rs5"], 1)
                pool.wait_ge(S["ms5"], n + 1)
                rsqrt(rstd2[:, t0:t1], ve2[:, t0:t1], t1 - t0).then_inc(S["rms5"], 1)

        @block.scalar
        def _(act):
            act.wait_ge(S["x_first"], 32)
            act.activation(flat(neg_a), ch("a_log"), ACT.Exp).then_inc(S["prep_act"], 1)

            def turned_input(c):
                for k in range(DK):
                    act.wait_ge(S["a0t_ps"], c * DK + k + 1)
                    act.activation(a0t[:, k], bank(6 + k), ACT.Copy).then_inc(S["a0t_ready"], 1)

            def conv_input(c, d):
                act.wait_ge(S["u_ps"], c * DB + d + 1)
                act.activation(upad[:, d, TAPS - 1:TAPS - 1 + C], bank(UB[d]), ACT.Copy).then_inc(S["u_raw"], 1)

            def channels(c, first=False):
                if not first:
                    act.wait_ge(S["y_acc"], (c - 1) * NP + 1)
                for d in range(DB):
                    act.wait_ge(S["conv_step"], c * TAPS * DB + TAPS * (d + 1))
                    act.activation(u[:, d], conv[:, d], ACT.Silu).then_inc(S["u_ready"], 1)

            def rank_b_c(c):
                act.wait_ge(S["xdbl_ps"], c + 1)
                if not isinstance(c, int):
                    act.wait_ge(S["bc_stored"], c * 16)
                act.activation(xdbl[0:RANK + 2 * NS, :], ps[0:RANK + 2 * NS, 6, :], ACT.Copy).then_inc(S["xdbl_ready"], 1)

            def step_exp(c):
                act.wait_ge(S["sp_in"], c * DB + DB)
                act.activation(flat(sp_exp), flat(delta_next), ACT.Abs).then_inc(S["sp_act"], 1)
                act.wait_ge(S["sp_act"], c * 3 + 1)
                act.activation(flat(sp_exp), flat(sp_exp), ACT.Exp, scale=-1.0).then_inc(S["sp_act"], 1)

            def step_log(c):
                act.wait_ge(S["sp_act"], c * 3 + 2)
                act.activation(flat(sp_ln), flat(sp_exp), ACT.Ln, bias=1.0).then_inc(S["sp_act"], 1)

            def decays(c, w, first=False):
                n, p = step(w)
                if w == 0:
                    act.wait_ge(S["delta_ready"], c + 1)
                if w >= AHEAD or not first:
                    act.wait_ge(S["scan_done"], c * 2 * NU + 2 * (w - AHEAD + 1))
                for x in range(2):
                    d = 2 * p + x
                    act.activation(da[:, w % AHEAD, x], delta[:, d], ACT.Exp,
                                   scale=neg_a[:, d, n:n + 1]).then_inc(S["da_ready"], 1)

            def gates(c, d0, first=False):
                if not first:
                    act.wait_ge(S["yz_ready"], c)
                for d in range(d0, d0 + 2):
                    act.wait_ge(S["z_ps"], c * DB + d + 1)
                    act.activation(zs[:, d], bank(UB[d]), ACT.Silu).then_inc(S["z_ready"], 1)

            def keep_input(c, first=False):
                if not first:
                    act.wait_ge(S["hsum_ready"], c * 2)
                act.wait_ge(S["a0_ready"], c * CT + CT)
                act.activation(flat(a0), flat(a0n), ACT.Copy).then_inc(S["a0_kept"], 1)

            def first_squares(c):
                for i in range(CT):
                    act.wait_ge(S["hsum_ready"], c * 2 + i // 2 + 1)
                    act.activation(junk[:, i], hsum[:, i], ACT.Square, accum_out=sq[:, i:i + 1]).then_inc(S["ss1"], 1)

            def turned_h1(c):
                for k in range(DK):
                    act.wait_ge(S["h1t_ps"], c * DK + k + 1)
                    act.activation(h1t[:, k], bank(4 + k), ACT.Copy).then_inc(S["h1t_ready"], 1)

            def hidden(c, f0):
                for f in range(f0, f0 + 2):
                    act.wait_ge(S["ff1_ps"], c * FB + f + 1)
                    act.activation(gate[:, f], bank(4 + f % 2), ACT.Gelu,
                                   bias=ch("ffn_b1")[:, f:f + 1]).then_inc(S["g_ready"], 1)

            def second_squares(c):
                for i in range(CT):
                    act.wait_ge(S["r_ready"], c * 2 + i // 2 + 1)
                    act.activation(junk[:, i], h1[:, i], ACT.Square, accum_out=sq3[:, i:i + 1]).then_inc(S["ss2"], 1)

            def scan_chunk(c, first=False, second=False, last=False):
                for w in range(NU):
                    for x in (range(AHEAD) if w == 0 else range(w + AHEAD - 1, min(w + AHEAD, NU))):
                        decays(c, x, first)
                    if w == 1 and not first and not second:
                        second_squares(c - 2)
                    if w in (2, 7):
                        gates(c, 2 * (w // 7), first)
                    if w == 6:
                        if not first:
                            first_squares(c - 1)
                        keep_input(c, first)
                    if w == 10 and not last:
                        turned_input(c + 1)
                    if w == 11 and not first:
                        turned_h1(c - 1)
                    if w in (12, 13, 15, 16) and not last:
                        conv_input(c + 1, w - 12 - w // 15)
                    if w == 19 and not last:
                        channels(c + 1)
                    if w in (14, 17, 20, 23) and not first:
                        hidden(c - 1, 2 * (w - 14) // 3)
                    if w == 22 and not last:
                        rank_b_c(c + 1)
                    if w == 27 and not last:
                        step_exp(c + 1)
                    if w == 28 and not last:
                        step_log(c + 1)

            act.wait_ge(S["prep_dve"], 1 + DB)
            turned_input(0)
            for d in range(DB):
                conv_input(0, d)
            channels(0, first=True)
            rank_b_c(0)
            step_exp(0)
            step_log(0)
            scan_chunk(0, first=True)
            scan_chunk(1, second=True)
            with act.Fori(2, NC - 1) as c:
                scan_chunk(c)
            scan_chunk(NC - 1, last=True)
            second_squares(NC - 2)
            first_squares(NC - 1)
            turned_h1(NC - 1)
            hidden(NC - 1, 0)

            def values(first, last):
                for v in range(first, last):
                    nb, n = min(2, KB - 2 * v), min(P, KV - 2 * v * P)
                    act.wait_ge(S["v_ps"], v + 1)
                    act.activation(vx[0:n, 2 * v:2 * v + nb, :, 0:HD],
                                   ps[0:n, VB[v], 0:nb * DM].rearrange("p (b h d) -> p b h d", b=nb, d=HD),
                                   ACT.Copy).then_inc(S["vx_ready"], 1)

            act.wait_ge(S["vx_init"], 2)
            values(0, VE)
            for f in range(2, FB, 2):
                hidden(NC - 1, f)
            second_squares(NC - 1)
            act.wait_ge(S["ss2"], NC * CT)
            act.sem_inc(S["mamba_done"], 1)
            values(VE, len(VB))

            def q_input(c):
                for k in range(DK):
                    act.wait_ge(S["xat_ps"], c * DK + k + 1)
                    if c >= 2:
                        act.wait_ge(S["qn_ps"], c - 1)
                    act.activation(xat[:, c % 2, k], bank(k), ACT.Copy).then_inc(S["xat_ready"], 1)

            act.wait_ge(S["kf_ready"], DK * len(KCOLS))
            act.activation(flat(kp[0]), flat(kf), ACT.Copy).then_inc(S["kp_ready"], 1)
            act.activation(flat(ksq), flat(kf), ACT.Square).then_inc(S["ksq_ready"], 1)
            q_input(0)

            act.wait_ge(S["kr_ready"], 1)
            act.activation(flat(kp[1]), flat(kf), ACT.Copy).then_inc(S["kp_ready"], 1)
            act.wait_ge(S["kr_ready"], 2)
            act.activation(flat(kp[2]), flat(kf), ACT.Copy).then_inc(S["kp_ready"], 1)

            for c in range(NC):
                act.wait_ge(S["qf_ready"], c * DK + DK)
                if c >= 2:
                    act.wait_ge(qx_in[c % 2], c // 2 * QX_SENT)
                act.activation(qp[0][:, c % 2], flat(qf[:, c % 2]), ACT.Copy).then_inc(S["qp_ready"], 1)
                act.activation(flat(xat[:, c % 2]), flat(qf[:, c % 2]), ACT.Square).then_inc(S["qsq_ready"], 1)
                if c + 1 < NC:
                    q_input(c + 1)
                for n in range(1, 3):
                    act.wait_ge(S["qr_ready"], c * 2 + n)
                    act.activation(qp[n][:, c % 2], flat(qf[:, c % 2]), ACT.Copy).then_inc(S["qp_ready"], 1)

            act.wait_ge(S["w_slots"], 16)
            for x in range(NE):
                act.activation(junk4[:, x], se[:, x], ACT.Square, accum_out=sqs[:, x:x + 1]).then_inc(S["ss4"], 1)

            def probabilities(c, first=False):
                for v in range(NV):
                    n = min(P, KV - v % KB * P)
                    if v >= 2 or not first:
                        act.wait_ge(S["pv_done"], c * NV + v - 1)
                    for h in range(2):
                        r = 2 * v + h
                        act.wait_ge(S["s_ps"], c * 2 * NV + r + 1)
                        act.activation(flat(prob[0:n, v % 2, 2 * h:2 * h + 2]),
                                       ps[0:n, 2 * (r % 3):2 * (r % 3) + 2, :].rearrange("p a b -> p (a b)"),
                                       ACT.Exp, bias=bound[0:n, 3:4], scale=HD ** -0.5).then_inc(S["p_ready"], 1)

            act.wait_ge(S["bound_ready"], 2)
            probabilities(0, first=True)
            with act.Fori(1, NC) as c:
                probabilities(c)

            for n in range(4):
                act.wait_ge(S["snt_ps"], n + 1)
                act.activation(snt[:, n // 2, n % 2 * 512:n % 2 * 512 + 512], bank(n), ACT.Copy).then_inc(S["snt_ready"], 1)

            def turned(t):
                act.wait_ge(S["et_ps"], t + 1)
                act.activation(cwt[:, :, tok(t)], banks(4, 2).rearrange("p (e n) -> p e n", n=P),
                               ACT.Copy).then_inc(S["et_ready"], 1)

            def combine_weights(t):
                act.wait_ge(S["l_max"], t + 1)
                if t >= 2:
                    act.wait_ge(S["et_ps"], t - 1)
                act.activation(ex[:, t % 2], lg[:, t], ACT.Exp, bias=nmx[:, t:t + 1],
                               accum_out=csum[:, t:t + 1]).then_inc(S["l_exp"], 1)

            def turned_tokens(t):
                act.wait_ge(S["xnt_ps"], t + 1)
                if t >= 2:
                    act.wait_ge(S["l_ps"], t - 1)
                act.activation(flat(xnt[:, t % 2]), ps[:, 6 + t % 2, 0:DK * P], ACT.Copy).then_inc(S["xnt_ready"], 1)

            turned_tokens(0)
            for t in range(TT + 2):
                if 1 <= t <= TT:
                    combine_weights(t - 1)
                if t >= 2:
                    turned(t - 2)
                if t + 1 < TT:
                    turned_tokens(t + 1)
                if t < TT:
                    act.wait_ge(S["l_ps"], t + 1)
                    act.activation(lg[:, t], banks(2 * (t % 2), 2), ACT.Copy).then_inc(S["l_copy"], 1)
            for t in range(TT):
                act.wait_ge(S["l_sub"], t + 1)
                act.activation(lg[:, t], lg[:, t], ACT.Exp).then_inc(S["d_ready"], 1)
            for x in range(NE):
                act.wait_ge(S["slt_ps"], x + 1)
                act.activation(flat(slt[:, x]), ps[:, 4 + x % 4, 0:DK * P], ACT.Copy).then_inc(S["slt_ready"], 1)
            for x in range(NE):
                if x >= 2:
                    act.wait_ge(S["eo_ps"], x - 1)
                for f in range(FB):
                    if f % 4 == 0:
                        act.wait_ge(S["h_ps"], 2 * x + f // 4 + 1)
                    act.activation(hid[:, x % 2, f], ps[:, 2 * (x % 2) + f // 4, tok(f % 4)], ACT.Gelu,
                                   bias=ch("moe_b1")[:, x * FB + f:x * FB + f + 1]).then_inc(S["hid_ready"], 1)

        @block.vector
        def _(dve):
            dve.wait_ge(S["prep_act"], 1)
            dve.tensor_scalar(flat(neg_a), flat(neg_a), -1.0, None, ALU.mult).then_inc(S["prep_dve"], 1)
            dve.wait_ge(S["consts"], 6)
            for d in range(DB):
                dve.tensor_scalar(diag_skip[:, d], ident[:, :], ch("skip")[:, d:d + 1], None,
                                  ALU.mult).then_inc(S["prep_dve"], 1)

            def xtile(t, n=1):
                v = xt[:, bass.ds(t, n), :]
                return flat(v) if n == 1 else v

            conv_w = ch("conv_w", TAPS)
            def norm_stats(c):
                for i in range(CT):
                    dve.bn_stats(stat[:, i, :], xtile(c * CT + i)).then_inc(S["st1"], 1)

            def norm_moments(c):
                dve.wait_ge(S["st1"], c * 2 * CT + CT)
                dve.memset(mark[:, :], 0.0).then_inc(S["mark1"], 1)
                for i in range(CT):
                    dve.bn_aggr(mv[:, i, :], stat[:, i, :]).then_inc(S["st1"], 1)

            def norm_variance(c):
                dve.wait_ge(S["st1"], c * 2 * CT + 2 * CT)
                dve.tensor_scalar(ve[:, 0:CT], mv[:, 0:CT, 1], 1e-5, None, ALU.add).then_inc(S["ve1"], 1)

            def normed_input(c, first=False):
                if not first:
                    dve.wait_ge(S["a0_kept"], c)
                    dve.wait_ge(S["a0t_ps"], c * DK)
                dve.wait_ge(S["rs1"], c + 1)
                for i in range(CT):
                    dve.tensor_scalar(a0n[:, i], xtile(c * CT + i), mv[:, i, 0:1], rstd[:, i:i + 1],
                                      ALU.subtract, ALU.mult).then_inc(S["a0_ready"], 1)

            def conv_history():
                dve.tensor_copy(upad[:, :, 0:TAPS - 1], hist).then_inc(S["hist_in"], 1)

            def convolution(c, d):
                dve.wait_ge(S["u_raw"], c * DB + d + 1)
                dve.wait_ge(S["hist_in"], c + 1)
                for step, j in enumerate(reversed(range(TAPS))):
                    if step == 0:
                        dve.tensor_scalar(conv[:, d], upad[:, d, j:j + C], conv_w[:, d, j:j + 1],
                                          ch("conv_b")[:, d:d + 1], ALU.mult, ALU.add).then_inc(S["conv_step"], 1)
                    else:
                        dve.wait_ge(S["conv_step"], c * TAPS * DB + TAPS * d + step)
                        dve.scalar_tensor_tensor(conv[:, d], upad[:, d, j:j + C], conv_w[:, d, j:j + 1],
                                                 conv[:, d], ALU.mult, ALU.add).then_inc(S["conv_step"], 1)

            def conv_keep():
                dve.tensor_copy(hist, upad[:, :, C:C + TAPS - 1])

            def step_input(c, d):
                dve.wait_ge(S["dt_ps"], c * DB + d + 1)
                dve.tensor_scalar(delta_next[:, d], bank(DTB[d]), ch("dt_b")[:, d:d + 1], None,
                                  ALU.add).then_inc(S["sp_in"], 1)

            def step_max(c):
                dve.wait_ge(S["sp_act"], c * 3 + 1)
                dve.tensor_scalar(flat(delta_next), flat(delta_next), 0.0, None, ALU.max).then_inc(S["sp_step"], 1)

            def step_rounded(c, first=False):
                if not first:
                    dve.wait_ge(S["ff1_ps"], (c - 1) * FB)
                dve.wait_ge(S["sp_act"], c * 3 + 2)
                dve.tensor_scalar(flat(sp_cor), flat(sp_exp), 1.0, 1.0, ALU.add, ALU.subtract).then_inc(S["sp_step"], 1)

            def step_rest(c):
                dve.wait_ge(S["sp_step"], c * 5 + 2)
                dve.tensor_tensor(flat(sp_cor), flat(sp_exp), flat(sp_cor), ALU.subtract).then_inc(S["sp_step"], 1)

            def step_log(c):
                dve.wait_ge(S["sp_act"], c * 3 + 3)
                dve.wait_ge(S["sp_step"], c * 5 + 3)
                dve.tensor_tensor(flat(sp_cor), flat(sp_cor), flat(sp_ln), ALU.add).then_inc(S["sp_step"], 1)

            def step_sum(c):
                dve.wait_ge(S["sp_step"], c * 5 + 4)
                dve.tensor_tensor(flat(delta_next), flat(delta_next), flat(sp_cor), ALU.add).then_inc(S["sp_step"], 1)

            def step_size(c, first=False):
                dve.wait_ge(S["sp_step"], c * 5 + 5)
                if not first:
                    dve.wait_ge(S["da_ready"], c * 2 * NU)
                dve.tensor_copy(flat(delta), flat(delta_next)).then_inc(S["delta_ready"], 1)

            def step_channels(c, first=False):
                dve.wait_ge(S["u_ready"], c * DB + DB)
                if not first:
                    dve.wait_ge(S["dbu_ready"], c * NU)
                dve.tensor_tensor(flat(du), flat(delta_next), flat(u), ALU.mult).then_inc(S["du_ready"], 1)

            def carry_over(c, w):
                n, p = step(w)
                dve.wait_ge(S["scan_done"], c * 2 * NU + 2 * (w + 1))
                dve.tensor_copy(carry[:, 2 * p:2 * p + 2, n:n + 1], state(w)[:, :, C - 1:C]).then_inc(S["carry_done"], 1)

            def scan(c, w, first=False):
                n, p = step(w)
                dve.wait_ge(S["dbu_ready"], c * NU + w + 1)
                if w >= 2 * RING or not first:
                    dve.wait_ge(S["y_acc"], slot_free(c, w // 2))
                for x in range(2):
                    d = 2 * p + x
                    dve.wait_ge(S["da_ready"], c * 2 * NU + 2 * w + x + 1)
                    dve.tensor_tensor_scan(state(w)[:, x], da[:, w % AHEAD, x], dbu[:, w % 2, x],
                                           carry[:, d, n:n + 1], ALU.mult, ALU.add).then_inc(S["scan_done"], 1)
                    if x == 0 and w >= 1:
                        carry_over(c, w - 1)

            def times_c(c, w):
                (n, p), q = step(w), w // (BG * DP)
                if w % (BG * DP) == 0:
                    dve.wait_ge(bc_in[q % 2], c * 16 * NBG + 32 * (q // 2 + 1))
                dve.wait_ge(S["carry_done"], c * NU + w + 1)
                dve.tensor_tensor(state(w), state(w), over(cg[:, q % 2, n % BG], 2),
                                  ALU.mult).then_inc(S["hc_ready"], 1)

            def gated(c):
                dve.wait_ge(S["y_acc"], c * NP + NP)
                dve.wait_ge(S["z_ready"], c * DB + DB)
                dve.tensor_tensor(flat(yz), banks(0, DB), flat(zs), ALU.mult).then_inc(S["yz_ready"], 1)

            def first_residual(c, b):
                dve.wait_ge(S["op_ps"], c * 2 + b + 1)
                dve.tensor_tensor(flat(hsum[:, 2 * b:2 * b + 2]), bank(4 + b), flat(a0[:, 2 * b:2 * b + 2]),
                                  ALU.add).then_inc(S["hsum_ready"], 1)

            def first_mean(c):
                dve.wait_ge(S["ss1"], c * CT + CT)
                dve.tensor_scalar(ve2[:, 0:CT], sq[:, 0:CT], 1.0 / DM, 1e-12, ALU.mult, ALU.add).then_inc(S["ms1"], 1)

            def first_norm(c):
                dve.wait_ge(S["rms1"], c + 1)
                for i in range(CT):
                    dve.scalar_tensor_tensor(h1[:, i], hsum[:, i], rstd2[:, i:i + 1], scales[:, 0, :],
                                             ALU.mult, ALU.mult).then_inc(S["h1_ready"], 1)

            def second_residual(c):
                for b in range(2):
                    dve.wait_ge(S["ff2_ps"], c * 2 + b + 1)
                    dve.tensor_tensor(flat(h1[:, 2 * b:2 * b + 2]), bank(4 + b), flat(h1[:, 2 * b:2 * b + 2]),
                                      ALU.add).then_inc(S["r_ready"], 1)

            def second_mean(c):
                dve.wait_ge(S["ss2"], c * CT + CT)
                dve.tensor_scalar(ve3[:, :], sq3[:, :], 1.0 / DM, 1e-12, ALU.mult, ALU.add).then_inc(S["ms2"], 1)

            def second_norm(c):
                dve.wait_ge(S["rms2"], c + 1)
                for i in range(CT):
                    dve.scalar_tensor_tensor(h1[:, i], h1[:, i], rstd3[:, i:i + 1], scales[:, 1, :],
                                             ALU.mult, ALU.mult).then_inc(S["rn_ready"], 1)

            def mamba_out(c):
                dve.wait_ge(S["rn_ready"], c * CT + CT)
                dve.tensor_tensor(xtile(c * CT, CT), xtile(c * CT, CT), h1, ALU.add).then_inc(S["x1_ready"], 1)

            def scan_chunk(c, first=False, second=False, last=False):
                for w in range(NU):
                    scan(c, w, first)
                    if w >= 1:
                        times_c(c, w - 1)
                    if w == 0 and not first and not second:
                        second_residual(c - 2)
                    if w == 1:
                        if not first:
                            gated(c - 1)
                        if not last:
                            norm_stats(c + 1)
                    if w == 2 and not last:
                        norm_moments(c + 1)
                    if w == 3:
                        if not last:
                            norm_variance(c + 1)
                        if not first and not second:
                            second_mean(c - 2)
                    if w in (4, 5) and not first:
                        first_residual(c - 1, w - 4)
                    if w == 6 and not first and not second:
                        second_norm(c - 2)
                    if w == 7 and not first:
                        if not second:
                            mamba_out(c - 2)
                        first_mean(c - 1)
                    if w == 8 and not last:
                        normed_input(c + 1)
                    if w == 9 and not last:
                        conv_history()
                    if w == 10 and not first:
                        first_norm(c - 1)
                    if not last:
                        if w in (13, 14, 16, 17):
                            convolution(c + 1, w - 13 - w // 16)
                        if w == 18:
                            conv_keep()
                        if w in (24, 26):
                            step_input(c + 1, w - 24)
                            step_input(c + 1, w - 23)
                        if w == 28:
                            step_max(c + 1)
                        if w == 29:
                            step_rounded(c + 1, first)
                            step_rest(c + 1)
                        if w == 30:
                            step_log(c + 1)
                            step_sum(c + 1)
                        if w == 31:
                            step_size(c + 1)
                            step_channels(c + 1)
                carry_over(c, NU - 1)
                times_c(c, NU - 1)

            norm_stats(0)
            norm_moments(0)
            norm_variance(0)
            normed_input(0, first=True)
            conv_history()
            for d in range(DB):
                convolution(0, d)
            conv_keep()
            for d in range(DB):
                step_input(0, d)
            step_max(0)
            step_rounded(0, first=True)
            step_rest(0)
            step_log(0)
            step_sum(0)
            step_size(0, first=True)
            step_channels(0, first=True)
            dve.wait_ge(S["w_mamba"], 16 * 6)
            scan_chunk(0, first=True)
            scan_chunk(1, second=True)
            with dve.Fori(2, NC - 1) as c:
                scan_chunk(c)
            scan_chunk(NC - 1, last=True)
            second_residual(NC - 2)
            gated(NC - 1)
            second_mean(NC - 2)
            for b in range(2):
                first_residual(NC - 1, b)
            second_norm(NC - 2)
            mamba_out(NC - 2)
            first_mean(NC - 1)
            dve.wait_ge(S["x1_ready"], NC - 1)
            first_norm(NC - 1)
            dve.wait_ge(S["h1_ready"], NC * CT)
            second_residual(NC - 1)
            second_mean(NC - 1)
            second_norm(NC - 1)
            mamba_out(NC - 1)
            dve.wait_ge(S["x1_ready"], NC)
            dve.sem_inc(S["mamba_done"], 1)

            for t in range(TT):
                dve.bn_stats(stat[:, t, :], xt[:, t, :]).then_inc(S["st2"], 1)
            for t in range(TT):
                dve.wait_ge(S["st2"], t + 1)
                dve.bn_aggr(mv[:, t, :], stat[:, t, :]).then_inc(S["st2"], 1)
            dve.wait_ge(S["st2"], 2 * TT)
            dve.tensor_scalar(ve[:, :], mv[:, :, 1], 1e-5, None, ALU.add).then_inc(S["ve3"], 1)
            dve.tensor_reduce(sel[:, :], ident.rearrange("p (d m) -> p m d", m=HALF), AX, ALU.add).then_inc(S["sel_ready"], 1)
            for k in range(DK):
                for j, (o, w) in enumerate(KCOLS):
                    dve.wait_ge(S["k_ps"], k * len(KCOLS) + j + 1)
                    dve.tensor_scalar(kf[:, k, o:o + w], ps[:, 4 * k + j, 0:w], ch("bk")[:, k:k + 1], None,
                                      ALU.add).then_inc(S["kf_ready"], 1)

            def normed(c):
                for i in range(CT):
                    t = c * CT + i
                    if c >= 2:
                        dve.wait_ge(S["xat_ps"], (c - 1) * DK)
                    dve.tensor_scalar(xa[:, c % 2, i], xt[:, t, :], mv[:, t, 0:1], rstd[:, t:t + 1],
                                      ALU.subtract, ALU.mult).then_inc(S["xa_ready"], 1)

            dve.wait_ge(S["rs3"], 1)
            normed(0)
            dve.wait_ge(S["kf_ready"], DK * len(KCOLS))
            dve.wait_ge(S["ksq_ready"], 1)
            for n in range(2):
                dve.wait_ge(S["kp_ready"], n + 1)
                if n:
                    dve.wait_ge(S["kr_ready"], n)
                dve.tensor_tensor(flat(kf), flat(kf), flat(kp[n]), ALU.subtract).then_inc(S["kr_ready"], 1)
                normed(n + 1)
            for c in range(NC):
                for k in range(DK):
                    dve.wait_ge(S["q_ps"], c * DK + k + 1)
                    if c >= 2:
                        dve.wait_ge(S["qp_ready"], 3 * (c - 1))
                    dve.tensor_scalar(qf[:, c % 2, k], bank(2 + 2 * (c % 2) + k), ch("bq")[:, k:k + 1], None,
                                      ALU.add).then_inc(S["qf_ready"], 1)
                dve.wait_ge(S["qf_ready"], c * DK + DK)
                for n in range(2):
                    dve.wait_ge(S["qp_ready"], c * 3 + n + 1)
                    if n:
                        dve.wait_ge(S["qr_ready"], c * 2 + n)
                    else:
                        dve.wait_ge(S["qsq_ready"], c + 1)
                    dve.tensor_tensor(flat(qf[:, c % 2]), flat(qf[:, c % 2]), qp[n][:, c % 2],
                                      ALU.subtract).then_inc(S["qr_ready"], 1)
                if c == 0:
                    normed(3)
                if c == 1:
                    dve.wait_ge(S["kn_ps"], 1)
                    dve.tensor_reduce(norm2[:, 0, :], ps[:, 6, 0:(KB - 1) * NH].rearrange("p (b h) -> p h b", h=NH),
                                      AX, ALU.max).then_inc(S["bound_step"], 1)
                    dve.wait_ge(S["bound_step"], 1)
                    dve.tensor_tensor(norm2[0:LAST, 0, :], norm2[0:LAST, 0, :], ps[0:LAST, 6, (KB - 1) * NH:KB * NH],
                                      ALU.max).then_inc(S["bound_step"], 1)
            dve.wait_ge(S["qn_ps"], NC)
            dve.tensor_reduce(norm2[:, 1, :], ps[:, 7, 0:TT * NH].rearrange("p (b h) -> p h b", h=NH),
                              AX, ALU.max).then_inc(S["bound_step"], 1)
            dve.wait_ge(S["bound_ps"], 1)
            dve.tensor_reduce(ncol[0:NH, 0:2], ps[0:NH, 0, 0:2 * P].rearrange("p (a b) -> p a b", b=P), AX,
                              ALU.max).then_inc(S["bound_step"], 1)
            dve.wait_ge(S["bound_step"], 4)
            dve.tensor_tensor(ncol[0:NH, 2:3], ncol[0:NH, 0:1], ncol[0:NH, 1:2], ALU.mult).then_inc(S["bound_step"], 1)
            dve.wait_ge(S["bound_ps"], 2)
            dve.tensor_reduce(ncol[0:1, 3:4], ps[0:1, 1, 0:NH], AX, ALU.max).then_inc(S["bound_step"], 1)
            dve.wait_ge(S["bound_ps"], 3)
            dve.tensor_copy(bound[:, 0:1], ps[:, 2, 0:1]).then_inc(S["bound_step"], 1)
            dve.tensor_scalar(bound[:, 2:3], ps[:, 2, 0:1], SMALL ** 2, None, ALU.is_le).then_inc(S["bound_step"], 1)
            dve.wait_ge(S["bound_step"], 8)
            dve.tensor_scalar(loose[:, :], bound[0:1, 2:3], -1.0, 1.0, ALU.mult, ALU.add).then_inc(S["bound_ready"], 1)
            dve.wait_ge(S["root_ready"], 1)
            dve.scalar_tensor_tensor(bound[:, 3:4], bound[:, 1:2], -HD ** -0.5, bound[:, 2:3], ALU.mult,
                                     ALU.mult).then_inc(S["bound_ready"], 1)
            dve.wait_ge(S["bound_ready"], 1)
            with dve.If(dve.value_load(loose[0:1, 0:1], min_val=0, max_val=1) > 0):
                for sent in qx_in:
                    dve.wait_ge(sent, NC // 2 * QX_SENT)
                with dve.Fori(0, TT) as t:
                    for h in range(NH):
                        dve.wait_ge(S["ms_ps"], t * NH + h + 1)
                        dve.tensor_reduce(nmax[:, h:h + 1], banks(4 * (h % 2), 4)[:, 0:KV], AX, ALU.max,
                                          negate=True).then_inc(S["nm_ready"], 1)
                    dve.wait_ge(S["nt_ps"], t + 1)
                    dve.tensor_copy(nrow[0:NH, :], ps[0:NH, 0, 0:P]).then_inc(S["nrow_ready"], 1)
                    dve.wait_ge(S["shift_in"], t * 16 + 16)

            def out_tail(c):
                for i in range(CT):
                    dve.wait_ge(S["oq_ps"], c * CT + i + 1)
                    o = bank(7).rearrange("p (h w) -> p h w", w=2 * HD)
                    dve.reciprocal(orec[:, i, :].unsqueeze(2), o[:, :, HD:HD + 1]).then_inc(S["orec_ready"], 1)
                    dve.wait_ge(S["orec_ready"], c * CT + i + 1)
                    dve.tensor_tensor(at[:, i].rearrange("p (h w) -> p h w", w=HD), o[:, :, 0:HD],
                                      orec[:, i, :].unsqueeze(2).to_broadcast([P, NH, HD]), ALU.mult).then_inc(S["at_ready"], 1)
                for k in range(DK):
                    dve.wait_ge(S["att_ps"], c * DK + k + 1)
                    dve.tensor_copy(att[:, k], bank(7)).then_inc(S["att_ready"], 1)
                for b in range(2):
                    dve.wait_ge(S["o_ps"], c * 2 + b + 1)
                    dve.tensor_tensor(xtile(c * CT + 2 * b, 2), xtile(c * CT + 2 * b, 2),
                                      bank(7).rearrange("p (a d) -> p a d", d=DM), ALU.add).then_inc(S["x2_ready"], 1)

            def heads_out(c):
                for g in range(NG):
                    dve.wait_ge(S["pv_done"], c * NV + KB * (g + 1))
                    dve.tensor_copy(ot[:, g], bank(6 + g % 2)).then_inc(S["o_evac"], 1)

            dve.wait_ge(S["ss4"], NE)
            dve.tensor_scalar(ve2[:, 0:NE], sqs[:, :], 1e-24, 1.0 / DM, ALU.max, ALU.mult).then_inc(S["ms4"], 1)
            dve.wait_ge(S["rms4"], 1)
            for x in range(NE):
                dve.scalar_tensor_tensor(se[:, x], se[:, x], rstd2[:, x:x + 1], scales[:, 3, :],
                                         ALU.mult, ALU.mult).then_inc(S["sn_ready"], 1)
            heads_out(0)
            with dve.Fori(1, NC) as c:
                out_tail(c - 1)
                dve.wait_ge(S["x2_ready"], c * 2)
                dve.memset(mark[:, :], 0.0).then_inc(S["mark1"], 1)
                for i in range(CT):
                    t = (c - 1) * CT + i
                    dve.bn_stats(stat[:, bass.ds(t, 1), :].rearrange("p a b -> p (a b)"), xtile(t)).then_inc(S["st5"], 1)
                heads_out(c)

            def token_moments(t0, t1):
                dve.wait_ge(S["st5"], t0 + t1)
                for t in range(t0, t1):
                    dve.bn_aggr(mv[:, t, :], stat[:, t, :]).then_inc(S["st5"], 1)
                dve.wait_ge(S["st5"], 2 * t1)
                dve.tensor_scalar(ve[:, t0:t1], mv[:, t0:t1, 1], 1e-5, None, ALU.add).then_inc(S["ve5"], 1)

            def token_mean_square(n, t0, t1):
                dve.wait_ge(S["rs5"], n + 1)
                dve.tensor_tensor(ve2[:, t0:t1], mv[:, t0:t1, 1], rstd[:, t0:t1], ALU.mult).then_inc(S["tscale_step"], 1)
                dve.wait_ge(S["tscale_step"], 3 * n + 1)
                dve.tensor_tensor(ve2[:, t0:t1], ve2[:, t0:t1], rstd[:, t0:t1], ALU.mult).then_inc(S["tscale_step"], 1)
                dve.wait_ge(S["tscale_step"], 3 * n + 2)
                dve.tensor_scalar(ve2[:, t0:t1], ve2[:, t0:t1], 1e-24 / DM, None, ALU.max).then_inc(S["ms5"], 1)

            def token_scale(n, t0, t1):
                dve.wait_ge(S["rms5"], n + 1)
                dve.tensor_tensor(tscale[:, t0:t1], rstd[:, t0:t1], rstd2[:, t0:t1], ALU.mult).then_inc(S["tscale_step"], 1)
                dve.wait_ge(S["tscale_step"], 3 * n + 3)

            def normed_tokens(t0, t1):
                for t in range(t0, t1):
                    dve.tensor_scalar(xn[:, t, 0:DM], xt[:, t, :], mv[:, t, 0:1], tscale[:, t:t + 1],
                                      ALU.subtract, ALU.mult).then_inc(S["y_normed"], 1)
                for t in range(t0, t1):
                    dve.wait_ge(S["y_normed"], t + 1)
                    dve.tensor_tensor(xn[:, t, 0:DM], xn[:, t, 0:DM], scales[:, 2, :], ALU.mult).then_inc(S["xn_ready"], 1)

            early, late = EARLY_LATE
            token_moments(*early)
            out_tail(NC - 1)
            token_mean_square(0, *early)
            dve.wait_ge(S["x2_ready"], 2 * NC)
            for t in range(*late):
                dve.bn_stats(stat[:, t, :], xt[:, t, :]).then_inc(S["st5"], 1)
            token_moments(*late)
            dve.memset(xn[:, :, DM:DM + 1], 1.0).then_inc(S["xn_one"], 1)
            dve.memset(mrun, -3.0e38).then_inc(S["xn_one"], 1)
            token_scale(0, *early)
            normed_tokens(0, 4)
            token_mean_square(1, *late)
            normed_tokens(4, early[1])
            token_scale(1, *late)
            normed_tokens(*late)
            dve.wait_ge(S["xn_one"], 2)
            for t in range(TT):
                dve.wait_ge(S["l_copy"], t + 1)
                dve.tensor_reduce(nmx[:, t:t + 1], lg[:, t], AX, ALU.max, negate=True).then_inc(S["l_max"], 1)
                if t >= 1:
                    dve.wait_ge(S["l_run"], t)
                dve.tensor_tensor(mrun, mrun, lg[:, t], ALU.max).then_inc(S["l_run"], 1)
            dve.wait_ge(S["mt_ps"], 1)
            dve.tensor_reduce(mcol[:, :], banks(0, 2).rearrange("p (e n) -> p e n", n=P), AX, ALU.max).then_inc(S["mcol_ready"], 1)
            dve.wait_ge(S["mcol_ready"], 1)
            for x in range(NE):
                dve.tensor_scalar(mdiag[:, x], ident[:, :], mcol[:, x:x + 1], None, ALU.mult).then_inc(S["mdiag_ready"], 1)
            dve.wait_ge(S["mb_ps"], 2)
            for t in range(TT):
                dve.wait_ge(S["l_exp"], t + 1)
                dve.tensor_tensor(lg[:, t], lg[:, t], banks(2, 2), ALU.subtract).then_inc(S["l_sub"], 1)
            for x in range(NE):
                acc = bank(4 + x if x < 4 else x - 4)
                dve.wait_ge(S["slot_ps"], x + 1)
                dve.reciprocal(srec[:, x:x + 1], acc[:, DM:DM + 1]).then_inc(S["srec_ready"], 1)
                dve.wait_ge(S["srec_ready"], x + 1)
                if x >= 4:
                    dve.wait_ge(S["slt_ps"], x - 3)
                dve.tensor_scalar(slot[:, x % 4], acc[:, 0:DM], srec[:, x:x + 1], None,
                                  ALU.mult).then_inc(S["slot_ready"], 1)
            for x in range(NE):
                dve.wait_ge(S["eo_ps"], x + 1)
                dve.tensor_copy(eo[:, x], ps[:, 4 + x % 2, 0:DM]).then_inc(S["eo_ready"], 1)
            dve.reciprocal(crec[:, :], csum[:, :]).then_inc(S["crec_ready"], 1)
            dve.wait_ge(S["crec_ready"], 1)
            for t in range(TT):
                dve.wait_ge(S["c_ps"], t + 1)
                dve.scalar_tensor_tensor(xt[:, t, :], ps[:, t % 8, 0:DM], crec[:, t:t + 1], xt[:, t, :],
                                         ALU.mult, ALU.add).then_inc(S["res_ready"], 1)

        @block.tensor
        def _(pe):
            mm = pe.matmul
            pe.wait_ge(S["consts"], 6)

            def turn(dst, src):
                return pe.transpose(dst, src, ident[:, :])

            def turn_input(c, first=False):
                if not first:
                    pe.wait_ge(S["z_ready"], (c - 1) * DB + DB)
                for k in range(DK):
                    for i in range(CT):
                        if k == 0:
                            pe.wait_ge(S["a0_ready"], c * CT + i + 1)
                        last = turn(bank(6 + k)[:, tok(i)], a0n[:, i, tok(k)])
                    last.then_inc(S["a0t_ps"], 1)

            def project(dst, o):
                for k in range(DK):
                    last = mm(dst, win[:, k, tok(o)], a0t[:, k], start=(k == 0), stop=(k == DK - 1))
                return last

            def channels(c, d):
                if d == 0:
                    pe.wait_ge(S["a0t_ready"], c * DK + DK)
                if d >= 2:
                    pe.wait_ge(S["u_raw"], c * DB + d - 1)
                project(bank(UB[d]), d).then_inc(S["u_ps"], 1)

            def gates(c, d):
                if d == 0:
                    pe.wait_ge(S["sp_in"], c * DB + DB)
                if d >= 2:
                    pe.wait_ge(S["z_ready"], c * DB + d - 1)
                project(bank(UB[d]), DB + d).then_inc(S["z_ps"], 1)

            def rank_b_c(c):
                for d in range(DB):
                    pe.wait_ge(S["u_ready"], c * DB + d + 1)
                    last = mm(ps[0:RANK + 2 * NS, 6, :], xproj[:, d], u[:, d], start=(d == 0), stop=(d == DB - 1))
                last.then_inc(S["xdbl_ps"], 1)

            def step_input(c, d):
                if d == 0:
                    pe.wait_ge(S["xdbl_ready"], c + 1)
                if d >= 2:
                    pe.wait_ge(S["sp_in"], c * DB + d - 1)
                mm(bank(DTB[d]), dtw[0:RANK, tok(d)], xdbl[0:RANK, :], start=True, stop=True).then_inc(S["dt_ps"], 1)

            def skip(c, first=False):
                if not first:
                    pe.wait_ge(S["yz_ready"], c)
                for d in range(DB):
                    mm(bank(d), diag_skip[:, d], u[:, d], start=True, stop=False)

            def add_states(c, j):
                p = j % DP
                if j in SUMMED:
                    pe.wait_ge(S["pair_ready"], c * len(SUMMED) + SUMMED.index(j) + 1)
                for s in range(1 if j in SUMMED else 2):
                    if j not in SUMMED:
                        pe.wait_ge(S["hc_ready"], c * NU + 2 * j + s + 1)
                    for x in range(2):
                        last = mm(bank(2 * p + x), ident[:, :], state(2 * j + s)[:, x], start=False,
                                  stop=(j >= NP - DP and (j in SUMMED or s == 1)))
                last.then_inc(S["y_acc"], 1)

            def out_project(c, i):
                for d in range(DB):
                    last = mm(bank(4 + i // 2)[:, part(i % 2)], yz[:, d, tok(i)], wout[:, d],
                              start=(d == 0), stop=(d == DB - 1))
                if i % 2:
                    last.then_inc(S["op_ps"], 1)

            def turn_h1(c):
                for k in range(DK):
                    for i in range(CT):
                        if k == 0:
                            pe.wait_ge(S["h1_ready"], c * CT + i + 1)
                        last = turn(bank(4 + k)[:, tok(i)], h1[:, i, tok(k)])
                    last.then_inc(S["h1t_ps"], 1)

            def hidden(c, f):
                if f == 0:
                    pe.wait_ge(S["h1t_ready"], c * DK + DK)
                if f >= 2:
                    pe.wait_ge(S["g_ready"], c * FB + f - 1)
                for k in range(DK):
                    last = mm(bank(4 + f % 2), w1[:, k, tok(f)], h1t[:, k], start=(k == 0), stop=(k == DK - 1))
                last.then_inc(S["ff1_ps"], 1)

            def ffn_out(c, i, h):
                acc = bank(4 + i // 2)[:, part(i % 2)]
                for f in range(h * FB // 2, (h + 1) * FB // 2):
                    if i == 0 and f == 0:
                        pe.wait_ge(S["g_ready"], c * FB + FB)
                    mm(acc, gate[:, f, tok(i)], w2[:, f], start=(f == 0), stop=False)
                if h:
                    last = mm(acc, ones[0:1, :], rows[0:1, 0, :], start=False, stop=True)
                    if i % 2:
                        last.then_inc(S["ff2_ps"], 1)

            def scan_chunk(c, first=False, last=False):
                for d in range(2):
                    gates(c, d)
                skip(c, first)
                for w in range(NU):
                    if 1 <= w <= 4 and not first:
                        out_project(c - 1, w - 1)
                    if 5 <= w <= 6:
                        gates(c, w - 3)
                    if w == 9 and not last:
                        turn_input(c + 1)
                    if w == 11 and not first:
                        turn_h1(c - 1)
                    if w in (10, 11, 13, 14) and not last:
                        channels(c + 1, w - 10 - w // 13)
                    if w in (12, 13, 15, 16, 18, 19, 21, 22) and not first:
                        hidden(c - 1, (w - 12) // 3 * 2 + w % 3)
                    if w == 21 and not last:
                        rank_b_c(c + 1)
                    if w in (23, 25) and not last:
                        step_input(c + 1, w - 23)
                        step_input(c + 1, w - 22)
                    if w >= 24 and not first:
                        ffn_out(c - 1, (w - 24) // 2, w % 2)
                    if w >= 3 and w % 2:
                        add_states(c, (w - 3) // 2)
                add_states(c, NP - 1)

            turn_input(0, first=True)
            pe.wait_ge(S["w_first"], 16 * 3)
            for d in range(DB):
                channels(0, d)
            rank_b_c(0)
            for d in range(DB):
                step_input(0, d)
            pe.wait_ge(S["w_mamba"], 16 * 6)
            pe.wait_ge(S["prep_dve"], 1 + DB)
            scan_chunk(0, first=True)
            with pe.Fori(1, NC - 1) as c:
                scan_chunk(c)
            scan_chunk(NC - 1, last=True)
            pe.wait_ge(S["yz_ready"], NC)
            for i in range(CT):
                out_project(NC - 1, i)

            def values(first, last):
                for v in range(first, last):
                    if v == len(VB) - 1:
                        pe.wait_ge(S["vx_ready"], 1)
                    for b in range(2 * v, min(2 * v + 2, KB)):
                        n = min(P, KV - b * P)
                        acc = ps[0:n, VB[v], part(b % 2)]
                        for x in range(2):
                            mm(acc, ctxt[0:CP, x, b * P:b * P + n], wv[0:CP, x], start=(x == 0), stop=False)
                        last_mm = mm(acc, ones[0:1, 0:n], rows[0:1, 1, :], start=False, stop=True)
                    last_mm.then_inc(S["v_ps"], 1)

            pe.wait_ge(S["w_attn"], 16 * 5)
            values(0, VE)
            turn_h1(NC - 1)
            for f in range(FB):
                hidden(NC - 1, f)
            for s in range(2 * CT):
                ffn_out(NC - 1, s // 2, s % 2)
            pe.wait_ge(S["ff2_ps"], 2 * NC)
            pe.sem_inc(S["mamba_done"], 1)

            values(VE, len(VB))
            pe.wait_ge(S["vx_ready"], len(VB))
            for k in range(DK):
                if k:
                    pe.wait_ge(S["r_ready"], 2 * NC)
                for j, (o, w) in enumerate(KCOLS):
                    for x in range(2):
                        last = mm(ps[:, 4 * k + j, 0:w], wk[0:CP, x, tok(k)], ctxt[0:CP, x, o:o + w],
                                  start=(x == 0), stop=(x == 1))
                    last.then_inc(S["k_ps"], 1)

            def q_chunk(c):
                for k in range(DK):
                    if c >= 1:
                        pe.wait_ge(S["xat_ready"], c * DK)
                    for i in range(CT):
                        if k == 0:
                            pe.wait_ge(S["xa_ready"], c * CT + i + 1)
                        last = turn(bank(k)[:, tok(i)], xa[:, c % 2, i, tok(k)])
                    last.then_inc(S["xat_ps"], 1)
                if c >= 2:
                    pe.wait_ge(S["qf_ready"], (c - 1) * DK)
                for k in range(DK):
                    for x in range(DK):
                        if k == 0:
                            pe.wait_ge(S["xat_ready"], c * DK + x + 1)
                        last = mm(bank(2 + 2 * (c % 2) + k), wq[:, x, tok(k)], xat[:, c % 2, x], start=(x == 0), stop=(x == DK - 1))
                    last.then_inc(S["q_ps"], 1)

            def q_lengths(c):
                pe.wait_ge(S["qsq_ready"], c + 1)
                for i in range(CT):
                    for k in range(DK):
                        at_col = (c * CT + i) * NH + k * HALF
                        last = mm(ps[:, 7, at_col:at_col + HALF], xat[:, c % 2, k, tok(i)], sel[:, :], start=True, stop=True)
                last.then_inc(S["qn_ps"], 1)

            pe.wait_ge(S["kf_ready"], DK * len(KCOLS))
            pe.wait_ge(S["sel_ready"], 1)
            q_chunk(0)
            for b in range(KB):
                for k in range(DK):
                    n = min(P, KV - b * P)
                    last = mm(ps[0:n, 6, b * NH + k * HALF:b * NH + k * HALF + HALF], ksq[:, k, b * P:b * P + n], sel[:, :],
                              start=True, stop=True)
            last.then_inc(S["kn_ps"], 1)
            q_chunk(1)
            q_lengths(0)
            q_chunk(2)
            q_lengths(1)
            q_chunk(3)
            q_lengths(2)
            q_lengths(3)
            pe.wait_ge(S["xat_ready"], DK * NC)
            for x in range(2):
                pe.wait_ge(S["bound_step"], 2 + x)
                last = turn(ps[0:NH, 0, tok(x)], norm2[:, x, :])
            last.then_inc(S["bound_ps"], 1)
            pe.wait_ge(S["bound_step"], 5)
            pe.transpose(ps[0:1, 1, 0:NH], ncol[0:NH, 2:3], ident[0:NH, 0:NH]).then_inc(S["bound_ps"], 1)
            pe.wait_ge(S["qf_ready"], DK * NC)
            pe.wait_ge(S["bound_step"], 6)
            mm(ps[:, 2, 0:1], ones[0:1, :], ncol[0:1, 3:4], start=True, stop=True).then_inc(S["bound_ps"], 1)

            for sent in qx_in:
                pe.wait_ge(sent, NC // 2 * QX_SENT)
            pe.wait_ge(S["vx_init"], 4)
            pe.wait_ge(S["bound_ready"], 1)
            with pe.If(pe.value_load(loose[0:1, 0:1], min_val=0, max_val=1) > 0):
                pe.wait_ge(S["bound_ready"], 2)
                with pe.Fori(0, TT) as t:
                    for h in range(NH):
                        if h >= 2:
                            pe.wait_ge(S["nm_ready"], t * NH + h - 1)
                        for j, (o, n) in enumerate(KCOLS):
                            last = mm(ps[:, 4 * (h % 2) + j, 0:n], qx[0:XR, h, bass.ds(t * P, P)], kx[0:XR, h, o:o + n],
                                      start=True, stop=True)
                        last.then_inc(S["ms_ps"], 1)
                    pe.wait_ge(S["nm_ready"], t * NH + NH)
                    turn(ps[0:NH, 0, 0:P], nmax[:, :]).then_inc(S["nt_ps"], 1)
                    pe.wait_ge(S["shift_in"], t * 16 + 16)

            def scores(c, v, first):
                g, b = v // KB, v % KB
                n = min(P, KV - b * P)
                for h in range(2):
                    r = 2 * v + h
                    if r >= 3 or not first:
                        pe.wait_ge(S["p_ready"], c * 2 * NV + r - (1 if r < 2 else 2))
                    for x in range(2):
                        head = G * g + 2 * h + x
                        last = mm(ps[0:n, 2 * (r % 3) + x, :], kx[0:XR + 1, head, b * P:b * P + n],
                                  qx[0:XR + 1, head, c * C:c * C + C] if first else qx[0:XR + 1, head, bass.ds(c * C, C)],
                                  start=True, stop=True)
                    last.then_inc(S["s_ps"], 1)

            def attend(c, v, first):
                g, b = v % NV // KB, v % KB
                n = min(P, KV - b * P)
                if b == 0 and (g >= 2 or not first):
                    pe.wait_ge(S["o_evac"], c * NG + g - 1)
                    if g == 1:
                        pe.wait_ge(S["x2_ready"], c * 2)
                pe.wait_ge(S["p_ready"], c * 2 * NV + 2 * v + 2)
                for x in range(G):
                    last = mm(ps[2 * HD * x:2 * HD * x + 2 * HD, 6 + g % 2, :], vx[0:n, b, G * g + x, :],
                              prob[0:n, v % 2, x], start=(b == 0), stop=(b == KB - 1))
                last.then_inc(S["pv_done"], 1)

            def out_piece(c, s):
                if s < CT:
                    if s == 0:
                        pe.wait_ge(S["o_evac"], c * NG + NG)
                    else:
                        pe.wait_ge(S["at_ready"], c * CT + s)
                    for g in range(NG):
                        last = turn(bank(7)[:, tok(g)], ot[:, g, tok(s)])
                    last.then_inc(S["oq_ps"], 1)
                elif s < CT + DK:
                    k = s - CT
                    if k == 0:
                        pe.wait_ge(S["at_ready"], c * CT + CT)
                    else:
                        pe.wait_ge(S["att_ready"], c * DK + k)
                    for i in range(CT):
                        last = turn(bank(7)[:, tok(i)], at[:, i, tok(k)])
                    last.then_inc(S["att_ps"], 1)
                elif s < PIECES:
                    i = s - CT - DK
                    if i == 0:
                        pe.wait_ge(S["att_ready"], c * DK + DK)
                    if i == 2:
                        pe.wait_ge(S["x2_ready"], c * 2 + 1)
                    acc = bank(7)[:, part(i % 2)]
                    for k in range(DK):
                        mm(acc, att[:, k, tok(i)], wo[:, k], start=(k == 0), stop=False)
                    last = mm(acc, ones[0:1, :], rows[0:1, 2, :], start=False, stop=True)
                    if i % 2:
                        last.then_inc(S["o_ps"], 1)

            for v in range(NV):
                scores(0, v, True)
                if v >= 1:
                    attend(0, v - 1, True)
            with pe.Fori(1, NC) as c:
                for v in range(NV):
                    scores(c, v, False)
                    attend(c, v - 1, False)
                    if v >= 2:
                        out_piece(c - 1, v - 2)
            attend(NC, -1, False)
            pe.wait_ge(S["sn_ready"], NE)
            for n in range(4):
                for x in range(4):
                    last = turn(bank(n)[:, tok(x)], se[:, 4 * (n % 2) + x, tok(n // 2)])
                last.then_inc(S["snt_ps"], 1)
            for s in range(PIECES):
                out_piece(NC - 1, s)

            def turn_tokens(t):
                pe.wait_ge(S["xn_ready"], t + 1)
                if t >= 2:
                    pe.wait_ge(S["xnt_ready"], t - 1)
                for k in range(DK):
                    last = turn(ps[:, 6 + t % 2, tok(k)], xn[:, t, tok(k)])
                last.then_inc(S["xnt_ps"], 1)

            turn_tokens(0)
            pe.wait_ge(S["snt_ready"], 4)
            for t in range(TT + 1):
                if t + 1 < TT:
                    turn_tokens(t + 1)
                if t < TT:
                    pe.wait_ge(S["xnt_ready"], t + 1)
                    if t >= 2:
                        pe.wait_ge(S["l_copy"], t - 1)
                    for n in range(2):
                        for k in range(DK):
                            last = mm(bank(2 * (t % 2) + n), xnt[:, t % 2, k], snt[:, k, n * 512:n * 512 + 512],
                                      start=(k == 0), stop=(k == DK - 1))
                    last.then_inc(S["l_ps"], 1)
                if t >= 1:
                    pe.wait_ge(S["l_exp"], t)
                    if t >= 2:
                        pe.wait_ge(S["et_ready"], t - 1)
                    for x in range(NE):
                        last = turn(bank(4 + x // 4)[:, tok(x % 4)], ex[:, (t - 1) % 2, tok(x)])
                    last.then_inc(S["et_ps"], 1)
            pe.wait_ge(S["l_run"], TT)
            pe.wait_ge(S["l_copy"], TT)
            for x in range(NE):
                last = turn(bank(x // 4)[:, tok(x % 4)], mrun[:, tok(x)])
            last.then_inc(S["mt_ps"], 1)
            for n in range(2):
                pe.wait_ge(S["mdiag_ready"], 4 * n + 4)
                mm(bank(2 + n), ones[:, :], mdiag[:, 4 * n:4 * n + 4], start=True, stop=True).then_inc(S["mb_ps"], 1)

            def turn_slots(x):
                pe.wait_ge(S["slot_ready"], x + 1)
                if x >= 4:
                    pe.wait_ge(S["slt_ready"], x - 3)
                for k in range(DK):
                    last = turn(ps[:, 4 + x % 4, tok(k)], slot[:, x % 4, tok(k)])
                last.then_inc(S["slt_ps"], 1)

            pe.wait_ge(S["xnt_ready"], TT)
            pe.wait_ge(S["et_ready"], TT)
            for x0 in range(0, NE, 4):
                for t in range(TT):
                    if x0 == 0:
                        pe.wait_ge(S["d_ready"], t + 1)
                    for x in range(x0, x0 + 4):
                        last = mm(ps[:, 4 + x if x < 4 else x - 4, 0:DM + 1], lg[:, t, tok(x)], xn[:, t, :],
                                  start=(t == 0), stop=(t == TT - 1))
                        if t == TT - 1:
                            last.then_inc(S["slot_ps"], 1)
                    if x0 and t == 1:
                        for x in range(4):
                            turn_slots(x)
            for x in range(4, NE):
                turn_slots(x)
            pe.wait_ge(S["w_b2"], 16)
            for x in range(NE + 1):
                if x < NE:
                    pe.wait_ge(S["slt_ready"], x + 1)
                    pe.wait_ge(w_exp[x % NW], 32 * (x // NW + 1))
                    if x >= 2:
                        pe.wait_ge(S["hid_ready"], FB * (x - 1))
                    for f in range(FB):
                        for k in range(DK):
                            last = mm(ps[:, 2 * (x % 2) + f // 4, tok(f % 4)], mw[x % NW][0][:, k, tok(f)], slt[:, x, k],
                                      start=(k == 0), stop=(k == DK - 1))
                        if f % 4 == 3:
                            last.then_inc(S["h_ps"], 1)
                if x >= 1:
                    y = x - 1
                    if y >= 2:
                        pe.wait_ge(S["eo_ready"], y - 1)
                    acc = ps[:, 4 + y % 2, 0:DM]
                    for f in range(FB):
                        pe.wait_ge(S["hid_ready"], FB * y + f + 1)
                        mm(acc, hid[:, y % 2, f], mw[y % NW][1][:, f], start=(f == 0), stop=False)
                    mm(acc, ones[0:1, :], b2[0:1, y, :], start=False, stop=True).then_inc(S["eo_ps"], 1)
            for t in range(TT):
                if t >= 8:
                    pe.wait_ge(S["res_ready"], t - 7)
                if t == 0:
                    pe.wait_ge(S["hid_ready"], FB * NE)
                if t == 4:
                    pe.wait_ge(S["eo_ready"], NE)
                for x in range(NE):
                    if t == 0:
                        pe.wait_ge(S["eo_ready"], x + 1)
                    last = mm(ps[:, t % 8, 0:DM], cwt[:, x, tok(t)], eo[:, x], start=(x == 0), stop=(x == NE - 1))
                last.then_inc(S["c_ps"], 1)


def kernel(x, ctx_768, L0_attn_in_proj_w, L0_attn_conv_w, L0_attn_conv_b, L0_attn_x_proj_w, L0_attn_dt_proj_w,
           L0_attn_dt_proj_b, L0_attn_A_log, L0_attn_D, L0_attn_out_proj_w, L0_attn_norm_w, L0_attn_ffn_w1,
           L0_attn_ffn_b1, L0_attn_ffn_w2, L0_attn_ffn_b2, L0_attn_ffn_norm_w, L0_xattn_Wq, L0_xattn_bq,
           L0_xattn_Wk, L0_xattn_bk, L0_xattn_Wv, L0_xattn_bv, L0_xattn_Wo, L0_xattn_bo, L0_ffn_norm_gamma,
           L0_ffn_slot_norm_gamma, L0_ffn_slot_embeds, L0_ffn_w1, L0_ffn_b1, L0_ffn_w2, L0_ffn_b2):
    import numpy as np
    import concourse.bacc as bacc
    from concourse.bass_utils import run_bass_kernel_spmd as run

    def blocks(w, p=P):
        w = np.asarray(w)
        return w.reshape(w.shape[0] // p, p, -1).transpose(1, 0, 2)

    def cols(v):
        return blocks(np.asarray(v).reshape(-1, 1))[:, :, 0]

    def spread(w):
        w = np.asarray(w)
        lead = w.shape[:-1]
        return w.reshape(*lead, DK, HALF, HD).swapaxes(-1, -2).reshape(*lead, DM)

    ins = {
        "x": np.asarray(x)[0],
        "ctx": blocks(np.asarray(ctx_768)[0].T, CP),
        "win": blocks(np.asarray(L0_attn_in_proj_w).T),
        "xproj": blocks(np.asarray(L0_attn_x_proj_w).T),
        "dtw": np.asarray(L0_attn_dt_proj_w).T,
        "wout": blocks(np.asarray(L0_attn_out_proj_w).T),
        "w1": blocks(np.asarray(L0_attn_ffn_w1).T),
        "w2": blocks(np.asarray(L0_attn_ffn_w2).T),
        "wq": blocks(spread(L0_xattn_Wq)),
        "wk": blocks(spread(L0_xattn_Wk), CP),
        "wv": blocks(L0_xattn_Wv, CP),
        "wo": blocks(L0_xattn_Wo),
        "chan": np.concatenate([
            blocks(L0_attn_conv_w).reshape(P, -1), cols(L0_attn_conv_b), cols(L0_attn_dt_proj_b),
            blocks(L0_attn_A_log).reshape(P, -1), cols(L0_attn_D), cols(L0_attn_ffn_b1),
            cols(spread(L0_xattn_bq)), cols(spread(L0_xattn_bk)), cols(np.asarray(L0_ffn_b1).reshape(-1))], axis=1),
        "scales": np.concatenate([np.asarray(v) for v in (L0_attn_norm_w, L0_attn_ffn_norm_w, L0_ffn_norm_gamma,
                                                          L0_ffn_slot_norm_gamma)])[None],
        "rows": np.concatenate([np.asarray(v) for v in (L0_attn_ffn_b2, L0_xattn_bv, L0_xattn_bo)])[None],
        "slots": np.asarray(L0_ffn_slot_embeds).transpose(1, 0, 2),
        "mw1": np.asarray(L0_ffn_w1).reshape(NE, DK, P, FH).transpose(0, 2, 1, 3),
        "mw2": np.asarray(L0_ffn_w2).reshape(NE, FB, P, DM).transpose(0, 2, 1, 3),
        "mb2": np.asarray(L0_ffn_b2).reshape(1, -1),
    }
    nc = bacc.Bacc("TRN2", target_bir_lowering=False, num_devices=1, dynamic_dma_scratch_size=64)
    arrays = {"in_" + k: np.ascontiguousarray(v) for k, v in ins.items()}
    args = [nc.dram_tensor(k, v.shape, mybir.dt.from_np(v.dtype), kind="ExternalInput").ap()
            for k, v in arrays.items()]
    out = nc.dram_tensor("out", (T, DM), F32, kind="ExternalOutput").ap()
    scratch = nc.dram_tensor("bc_scratch", (NC, 2 * NS, C), F32, kind="Internal").ap()
    decoder_layer(nc, *args, out, scratch)
    r = run(nc, [arrays], core_ids=[0])
    return r.results[0]["out"].reshape(1, T, DM)
```
